# Optimizing a Trainium2 kernel written in Bass

```python
import numpy as np
import jax
import jax.numpy as jnp

def _softmax(x, axis=-1):
    return jax.nn.softmax(x, axis=axis)

def _gelu(x):
    return jax.nn.gelu(x, approximate=True)

def _silu(x):
    return jax.nn.silu(x)

def _sigmoid(x):
    return jax.nn.sigmoid(x)

def _layernorm(x, axis=-1, eps=1e-05):
    m = jnp.mean(x, axis=axis, keepdims=True)
    v = jnp.var(x, axis=axis, keepdims=True)
    return (x - m) / jnp.sqrt(v + eps)

def _scatter_add(tgt, idx, src, axis=0):
    return tgt.at[idx].add(src)

def _segment_sum(src, seg, n):
    return jax.ops.segment_sum(src, seg, n)
kernel_name = 'mk_conv_attn_hybrid_d2_conv_nchw384_r2_b14d8f'

def setup_inputs(seed: int=0):
    np.random.seed(seed)
    _w = jnp.asarray

    def _rec_inputs():
        import jax
        import jax.numpy as jnp
        _gk = jax.random.key(seed)
        x = -0.001003 + 1 * jax.random.normal(jax.random.fold_in(_gk, 1), (4, 192, 32, 32), jnp.float32)
        return x
    x = _rec_inputs()

    def _L0_conv_setup():
        import jax, jax.numpy as jnp
        import numpy as np
        D_MODEL = 96
        D_STATE = 16
        SSM_RATIO = 2.0
        D_INNER = int(SSM_RATIO * D_MODEL)
        DT_RANK = int(np.ceil(D_MODEL / 16))
        K_GROUP = 4
        BATCH, HH, WW = (4, 32, 32)
        DT_MIN, DT_MAX = (0.001, 0.1)
        LN_EPS = 1e-05

        def _cross_scan(x):
            B, D, H, W = x.shape
            x0 = x.reshape(B, D, H * W)
            x1 = jnp.transpose(x, (0, 1, 3, 2)).reshape(B, D, H * W)
            return jnp.stack([x0, x1, x0[..., ::-1], x1[..., ::-1]], axis=1)

        def _cross_merge(ys, H, W):
            B, K, D, L = ys.shape
            y0 = ys[:, 0]
            y2 = ys[:, 2][..., ::-1]
            yt = ys[:, 1] + ys[:, 3][..., ::-1]
            yt = jnp.transpose(yt.reshape(B, D, W, H), (0, 1, 3, 2)).reshape(B, D, L)
            return y0 + y2 + yt

        def _selective_scan(u, dt, A, Bs, Cs):
            dt_l = jnp.moveaxis(dt, -1, 0)
            u_l = jnp.moveaxis(u, -1, 0)
            B_l = jnp.moveaxis(Bs, -1, 0)
            C_l = jnpp_move = jnp.moveaxis(Cs, -1, 0)

            def step(h, inp):
                dtt, ut, bt, ct = inp
                dA = jnp.exp(dtt[..., None] * A)
                h = h * dA + (dtt * ut)[..., None] * bt[:, :, None, :]
                y = jnp.einsum('bkdn,bkn->bkd', h, ct)
                return (h, y)
            h0 = jnp.zeros(u.shape[:3] + (A.shape[-1],), dtype=u.dtype)
            _, ys = jax.lax.scan(step, h0, (dt_l, u_l, B_l, C_l))
            return jnp.moveaxis(ys, 0, -1)
        key = jax.random.key(seed)
        ks = jax.random.split(key, 6)
        x = jax.random.normal(ks[0], (BATCH, D_INNER, HH, WW), dtype=jnp.float32)
        x_proj_weight = jax.random.normal(ks[1], (K_GROUP, DT_RANK + 2 * D_STATE, D_INNER), dtype=jnp.float32) * D_INNER ** (-0.5)
        dt_projs_weight = jax.random.normal(ks[2], (K_GROUP, D_INNER, DT_RANK), dtype=jnp.float32) * DT_RANK ** (-0.5)
        dt = jnp.exp(jax.random.uniform(ks[3], (K_GROUP, D_INNER)) * (np.log(DT_MAX) - np.log(DT_MIN)) + np.log(DT_MIN))
        dt = jnp.clip(dt, 0.0001, None)
        dt_projs_bias = dt + jnp.log(-jnp.expm1(-dt))
        A = jnp.tile(jnp.arange(1, D_STATE + 1, dtype=jnp.float32)[None, :], (K_GROUP * D_INNER, 1))
        A_logs = jnp.log(A)
        Ds = jnp.ones((K_GROUP * D_INNER,), dtype=jnp.float32)
        ln_weight = jnp.ones((D_INNER,), dtype=jnp.float32)
        ln_bias = jnp.zeros((D_INNER,), dtype=jnp.float32)
        return {'x': x, 'x_proj_weight': x_proj_weight, 'dt_projs_weight': dt_projs_weight, 'dt_projs_bias': dt_projs_bias, 'A_logs': A_logs, 'Ds': Ds, 'ln_weight': ln_weight, 'ln_bias': ln_bias}
    _L0_conv_all = _L0_conv_setup()
    _L0_conv_in = {k: v for k, v in _L0_conv_all.items() if k in ('x_proj_weight', 'dt_projs_weight', 'dt_projs_bias', 'A_logs', 'Ds', 'ln_weight', 'ln_bias')}
    del _L0_conv_all

    def _L1_attn_setup():
        import jax, jax.numpy as jnp
        import numpy as np
        T = 10
        NUM_HEADS = 12

        def _rel_pos_index(t):
            coords = jnp.arange(t)
            return coords[:, None] - coords[None, :] + (t - 1)
        key = jax.random.key(seed)
        ks = jax.random.split(key, 6)
        dim, attn_dim = (192, 192)
        B_ = 8192
        return {'x': jax.random.normal(ks[0], (B_, T, dim), dtype=jnp.float32), 'qkv_w': jax.random.normal(ks[1], (3 * attn_dim, dim), dtype=jnp.float32) * 0.02, 'qkv_b': jax.random.normal(ks[2], (3 * attn_dim,), dtype=jnp.float32) * 0.02, 'proj_w': jax.random.normal(ks[3], (dim, attn_dim), dtype=jnp.float32) * 0.02, 'proj_b': jax.random.normal(ks[4], (dim,), dtype=jnp.float32) * 0.02, 'bias_table': jax.random.normal(ks[5], (2 * T - 1, NUM_HEADS), dtype=jnp.float32) * 0.02}
    _L1_attn_all = _L1_attn_setup()
    _L1_attn_in = {k: v for k, v in _L1_attn_all.items() if k in ('qkv_w', 'qkv_b', 'proj_w', 'proj_b', 'bias_table')}
    del _L1_attn_all

    def _L1_ffn_setup():
        import jax, jax.numpy as jnp
        import numpy as np
        NUM_EXPERTS = 4
        TOP_K = 2
        DIM = 192
        HID = 4 * DIM
        key = jax.random.key(seed)
        ks = jax.random.split(key, 5)
        B, S = (16, 1024)
        scale_in = 1.0 / np.sqrt(DIM)
        scale_hid = 1.0 / np.sqrt(HID)
        return {'x': jax.random.normal(ks[0], (B, S, DIM), dtype=jnp.float32), 'gate_w': jax.random.normal(ks[1], (DIM, NUM_EXPERTS), dtype=jnp.float32) * scale_in, 'gate_b': jnp.zeros((NUM_EXPERTS,), dtype=jnp.float32), 'w1': jax.random.normal(ks[2], (NUM_EXPERTS, DIM, HID), dtype=jnp.float32) * scale_in, 'b1': jnp.zeros((NUM_EXPERTS, HID), dtype=jnp.float32), 'w2': jax.random.normal(ks[3], (NUM_EXPERTS, HID, DIM), dtype=jnp.float32) * scale_hid, 'b2': jnp.zeros((NUM_EXPERTS, DIM), dtype=jnp.float32)}
    _L1_ffn_all = _L1_ffn_setup()
    _L1_ffn_in = {k: v for k, v in _L1_ffn_all.items() if k in ('gate_w', 'gate_b', 'w1', 'b1', 'w2', 'b2')}
    del _L1_ffn_all
    return {'x': x, 'L0_conv_x_proj_weight': _L0_conv_in['x_proj_weight'], 'L0_conv_dt_projs_weight': _L0_conv_in['dt_projs_weight'], 'L0_conv_dt_projs_bias': _L0_conv_in['dt_projs_bias'], 'L0_conv_A_logs': _L0_conv_in['A_logs'], 'L0_conv_Ds': _L0_conv_in['Ds'], 'L0_conv_ln_weight': _L0_conv_in['ln_weight'], 'L0_conv_ln_bias': _L0_conv_in['ln_bias'], 'L1_attn_qkv_w': _L1_attn_in['qkv_w'], 'L1_attn_qkv_b': _L1_attn_in['qkv_b'], 'L1_attn_proj_w': _L1_attn_in['proj_w'], 'L1_attn_proj_b': _L1_attn_in['proj_b'], 'L1_attn_bias_table': _L1_attn_in['bias_table'], 'L1_ffn_gate_w': _L1_ffn_in['gate_w'], 'L1_ffn_gate_b': _L1_ffn_in['gate_b'], 'L1_ffn_w1': _L1_ffn_in['w1'], 'L1_ffn_b1': _L1_ffn_in['b1'], 'L1_ffn_w2': _L1_ffn_in['w2'], 'L1_ffn_b2': _L1_ffn_in['b2']}

def reference(x, L0_conv_x_proj_weight, L0_conv_dt_projs_weight, L0_conv_dt_projs_bias, L0_conv_A_logs, L0_conv_Ds, L0_conv_ln_weight, L0_conv_ln_bias, L1_attn_qkv_w, L1_attn_qkv_b, L1_attn_proj_w, L1_attn_proj_b, L1_attn_bias_table, L1_ffn_gate_w, L1_ffn_gate_b, L1_ffn_w1, L1_ffn_b1, L1_ffn_w2, L1_ffn_b2):
    import jax
    import jax.numpy as jnp

    def _L0_conv_ref(x, x_proj_weight, dt_projs_weight, dt_projs_bias, A_logs, Ds, ln_weight, ln_bias):
        import jax, jax.numpy as jnp
        import numpy as np
        D_MODEL = 96
        D_STATE = 16
        SSM_RATIO = 2.0
        D_INNER = int(SSM_RATIO * D_MODEL)
        DT_RANK = int(np.ceil(D_MODEL / 16))
        K_GROUP = 4
        BATCH, HH, WW = (4, 32, 32)
        DT_MIN, DT_MAX = (0.001, 0.1)
        LN_EPS = 1e-05

        def _cross_scan(x):
            B, D, H, W = x.shape
            x0 = x.reshape(B, D, H * W)
            x1 = jnp.transpose(x, (0, 1, 3, 2)).reshape(B, D, H * W)
            return jnp.stack([x0, x1, x0[..., ::-1], x1[..., ::-1]], axis=1)

        def _cross_merge(ys, H, W):
            B, K, D, L = ys.shape
            y0 = ys[:, 0]
            y2 = ys[:, 2][..., ::-1]
            yt = ys[:, 1] + ys[:, 3][..., ::-1]
            yt = jnp.transpose(yt.reshape(B, D, W, H), (0, 1, 3, 2)).reshape(B, D, L)
            return y0 + y2 + yt

        def _selective_scan(u, dt, A, Bs, Cs):
            dt_l = jnp.moveaxis(dt, -1, 0)
            u_l = jnp.moveaxis(u, -1, 0)
            B_l = jnp.moveaxis(Bs, -1, 0)
            C_l = jnpp_move = jnp.moveaxis(Cs, -1, 0)

            def step(h, inp):
                dtt, ut, bt, ct = inp
                dA = jnp.exp(dtt[..., None] * A)
                h = h * dA + (dtt * ut)[..., None] * bt[:, :, None, :]
                y = jnp.einsum('bkdn,bkn->bkd', h, ct)
                return (h, y)
            h0 = jnp.zeros(u.shape[:3] + (A.shape[-1],), dtype=u.dtype)
            _, ys = jax.lax.scan(step, h0, (dt_l, u_l, B_l, C_l))
            return jnp.moveaxis(ys, 0, -1)
        B, D, H, W = x.shape
        K = x_proj_weight.shape[0]
        N = D_STATE
        R = dt_projs_weight.shape[-1]
        L = H * W
        xs = _cross_scan(x)
        x_dbl = jnp.einsum('bkdl,kcd->bkcl', xs, x_proj_weight)
        dts, Bs, Cs = (x_dbl[:, :, :R], x_dbl[:, :, R:R + N], x_dbl[:, :, R + N:])
        dts = jnp.einsum('bkrl,kdr->bkdl', dts, dt_projs_weight)
        A = -jnp.exp(A_logs.astype(jnp.float32)).reshape(K, D, N)
        dt = jax.nn.softplus(dts.astype(jnp.float32) + dt_projs_bias.astype(jnp.float32)[None, :, :, None])
        u = xs.astype(jnp.float32)
        Bs = Bs.astype(jnp.float32)
        Cs = Cs.astype(jnp.float32)
        ys = _selective_scan(u, dt, A, Bs, Cs)
        ys = ys + Ds.astype(jnp.float32).reshape(K, D)[None, :, :, None] * u
        y = _cross_merge(ys, H, W).reshape(B, D, H, W)
        yc = jnp.transpose(y, (0, 2, 3, 1))
        mu = jnp.mean(yc, axis=-1, keepdims=True)
        var = jnp.mean((yc - mu) ** 2, axis=-1, keepdims=True)
        yc = (yc - mu) * jax.lax.rsqrt(var + LN_EPS) * ln_weight + ln_bias
        y = jnp.transpose(yc, (0, 3, 1, 2)).astype(x.dtype)
        return jax.nn.gelu(y, approximate=False)

    def _L1_attn_ref(x, qkv_w, qkv_b, proj_w, proj_b, bias_table):
        import jax, jax.numpy as jnp
        import numpy as np
        T = 10
        NUM_HEADS = 12

        def _rel_pos_index(t):
            coords = jnp.arange(t)
            return coords[:, None] - coords[None, :] + (t - 1)
        B_, N, C = x.shape
        H = NUM_HEADS
        Dh = qkv_w.shape[0] // (3 * H)
        scale = Dh ** (-0.5)
        qkv = x @ qkv_w.T + qkv_b
        qkv = qkv.reshape(B_, N, 3, H, Dh).transpose(2, 0, 3, 1, 4)
        q, k, v = (qkv[0], qkv[1], qkv[2])
        idx = _rel_pos_index(N)
        bias = bias_table[idx].transpose(2, 0, 1)
        attn = jnp.einsum('bhnd,bhmd->bhnm', q * scale, k) + bias[None]
        attn = jax.nn.softmax(attn, axis=-1)
        out = jnp.einsum('bhnm,bhmd->bhnd', attn, v)
        out = out.transpose(0, 2, 1, 3).reshape(B_, N, H * Dh)
        return out @ proj_w.T + proj_b

    def _L1_ffn_ref(x, gate_w, gate_b, w1, b1, w2, b2):
        import jax, jax.numpy as jnp
        import numpy as np
        NUM_EXPERTS = 4
        TOP_K = 2
        DIM = 192
        HID = 4 * DIM
        scores = jnp.einsum('bsd,de->bse', x, gate_w) + gate_b
        probs = jax.nn.softmax(scores, axis=-1)
        topk_vals, topk_idx = jax.lax.top_k(probs, TOP_K)
        mask = jnp.sum(jax.nn.one_hot(topk_idx, NUM_EXPERTS, dtype=probs.dtype), axis=-2)
        masked = probs * mask
        masked = masked / (jnp.sum(masked, axis=-1, keepdims=True) + 1e-09)
        h = jax.nn.gelu(jnp.einsum('bsd,edh->ebsh', x, w1) + b1[:, None, None, :], approximate=False)
        y = jnp.einsum('ebsh,ehd->ebsd', h, w2) + b2[:, None, None, :]
        out = jnp.einsum('bse,ebsd->bsd', masked, y)
        return out

    def _gn(v, G=32, eps=1e-05):
        B_, C_, H_, W_ = v.shape
        g = v.reshape(B_, G, C_ // G, H_, W_)
        m = jnp.mean(g, axis=(2, 3, 4), keepdims=True)
        s = jnp.var(g, axis=(2, 3, 4), keepdims=True)
        return ((g - m) / jnp.sqrt(s + eps)).reshape(v.shape)

    def _ln_c(v, eps=1e-06):
        m = jnp.mean(v, axis=1, keepdims=True)
        s = jnp.var(v, axis=1, keepdims=True)
        return (v - m) / jnp.sqrt(s + eps)

    def _ln_t(v, eps=1e-05):
        m = jnp.mean(v, axis=-1, keepdims=True)
        s = jnp.var(v, axis=-1, keepdims=True)
        return (v - m) / jnp.sqrt(s + eps)

    def _to_tokens(v):
        B_, C_, H_, W_ = v.shape
        return v.reshape(B_, C_, H_ * W_).transpose(0, 2, 1)

    def _from_tokens(t, like):
        B_, C_, H_, W_ = like.shape
        return t.transpose(0, 2, 1).reshape(B_, C_, H_, W_)
    x = x + _L0_conv_ref(_gn(x), L0_conv_x_proj_weight, L0_conv_dt_projs_weight, L0_conv_dt_projs_bias, L0_conv_A_logs, L0_conv_Ds, L0_conv_ln_weight, L0_conv_ln_bias)
    t = _to_tokens(x)
    t = t + _L1_attn_ref(_ln_t(t), L1_attn_qkv_w, L1_attn_qkv_b, L1_attn_proj_w, L1_attn_proj_b, L1_attn_bias_table)
    t = t + _L1_ffn_ref(_ln_t(t), L1_ffn_gate_w, L1_ffn_gate_b, L1_ffn_w1, L1_ffn_b1, L1_ffn_w2, L1_ffn_b2)
    x = _from_tokens(t, x)
    return x

_drawn_inputs = setup_inputs


def setup_inputs(seed=0):
    import zlib

    import numpy as np

    out = dict(_drawn_inputs(seed))
    spreads = {'L0_conv_Ds': (1.0, 0.2),
     'L0_conv_ln_weight': (1.0, 0.2),
     'L0_conv_ln_bias': (0.0, 0.1),
     'L1_ffn_gate_b': (0.0, 0.1),
     'L1_ffn_b1': (0.0, 0.33),
     'L1_ffn_b2': (0.0, 0.1)}
    factors = {'L1_attn_qkv_w': 6.087,
     'L1_attn_qkv_b': 5.795,
     'L1_attn_proj_w': 8.0,
     'L1_attn_proj_b': 3.362,
     'L1_attn_bias_table': 200.0}
    for name, (base, spread) in spreads.items():
        noise = np.random.default_rng([zlib.crc32(name.encode()), seed]).standard_normal(out[name].shape)
        drawn = base * np.exp(spread * noise) if base else spread * noise
        out[name] = jnp.asarray(drawn.astype(out[name].dtype))
    for name, factor in factors.items():
        out[name] = (out[name] * factor).astype(out[name].dtype)
    return out
```

```python
from contextlib import ExitStack

import concourse.bass as bass
from concourse import mybir

F32 = mybir.dt.float32
BF16 = mybir.dt.bfloat16
ALU = mybir.AluOpType
ACT = mybir.ActivationFunctionType
AX = mybir.AxisListType

NB = 4
D = 192
HC = 96
HH = WW = 32
L = HH * WW
CH = 512
K = 4
N = 16
R = 6
GN_CH = 6
DD = 8
BLK = 32
NBLK = HC // BLK
SUB = BLK // DD
TILES = HC // DD
UNITS = 2 * K
HEADS = 12
DH = 16
QPART = 3
EXPERTS = 4
HID = 768
HT = HID // 128

COL_DTB, COL_DS, COL_LNW, COL_LNB, COL_Q, COL_K, COL_PB = 0, 8, 16, 18, 20, 22, 24
NCOL = 26


class Own:

    def __init__(self, eng, sem):
        self.eng, self.sem, self.n = eng, sem, 0

    def __call__(self, ins):
        ins.then_inc(self.sem, 1)
        self.n += 1
        return ins

    def wait(self):
        self.eng.wait_ge(self.sem, self.n)


def prepare(nc, w, s):
    with ExitStack() as ctx:
        def sb(name, shape, dt=F32):
            return ctx.enter_context(nc.sbuf_tensor(name, shape, dt))

        def sem(name):
            return ctx.enter_context(nc.semaphore(name))

        rows = sb("rows", [NCOL, HC])
        a_rows = sb("a_rows", [HC, 128])
        wx = sb("wx", [R + 2 * N, K, D])
        wdt_rows = sb("wdt_rows", [HC, 2 * K, R])
        wdt = sb("wdt", [R, K, D])
        group = sb("group", [HC, HC])
        stats = sb("stats", [HC, 2 * NB, 2, 6])
        mv = sb("mv", [HC, 2 * NB, 2])
        mean = sb("mean", [HC, 2 * NB])
        spread = sb("spread", [HC, 2 * NB])
        rstd = sb("rstd", [HC, 2 * NB])
        a_exp = sb("a_exp", [128, HC])
        ps = ctx.enter_context(nc.psum_tensor("ps_prep", [128, 8, CH], F32))
        x_in = [sem(f"x_in{b}") for b in range(NB)]
        rows_in, wx_in, wdt_in, a_in = sem("rows_in"), sem("wx_in"), sem("wdt_in"), sem("a_in")
        masks, pe_small, pe_wx, pe_wdt, pe_mean, pe_var = (
            sem("masks"), sem("pe_small"), sem("pe_wx"), sem("pe_wdt"), sem("pe_mean"), sem("pe_var"))
        a_turned = sem("a_turned")
        wdt_turned = sem("wdt_turned")
        dve, aexp, std, gp, mean_in, var_in = sem("dve_prep"), sem("aexp"), sem("std"), sem("gp_prep"), sem("mean_in"), sem("var_in")

        with nc.Block() as block:
            @block.sync
            def _(sp):
                for b in range(NB):
                    sp.dma_start(s.X[:, b, :, :], w.x[b].rearrange("(f p) h w -> p f (h w)", p=HC)).then_inc(x_in[b], 16)

            @block.scalar
            def _(act):
                vec = [(COL_DTB, w.dtb.rearrange("k (f p) -> (k f) p", p=HC), 8),
                       (COL_DS, w.ds.rearrange("(k p) -> k p", p=HC), 8),
                       (COL_LNW, w.lnw.rearrange("(f p) -> f p", p=HC), 2),
                       (COL_LNB, w.lnb.rearrange("(f p) -> f p", p=HC), 2),
                       (COL_Q, w.qkvb[0:2 * D].rearrange("(f p) -> f p", p=HC), 4),
                       (COL_PB, w.projb.rearrange("(f p) -> f p", p=HC), 2)]
                for at, src, n in vec:
                    act.dma_start(rows[at:at + n, :], src).then_inc(rows_in, 16)
                act.dma_start(wx[:], w.wx.rearrange("k c d -> c k d")).then_inc(wx_in, 16)
                act.dma_start(a_rows[:], w.alog.rearrange("(g d) n -> g (d n)", d=DD)).then_inc(a_in, 16)
                act.dma_start(wdt_rows[:], w.wdt.rearrange("k (f p) r -> p (k f) r", p=HC)).then_inc(wdt_in, 16)
                act.wait_ge(a_turned, 1)
                nc.scalar.activation(a_exp[:], a_exp[:], ACT.Exp).then_inc(aexp, 1)
                act.wait_ge(pe_var, 1)
                act.wait_ge(gp, 1)
                nc.scalar.activation(spread[:], ps[0:HC, 1, 336:344], ACT.Sqrt, bias=s.eps5[0:HC, :]).then_inc(std, 1)

            @block.gpsimd
            def _(pool):
                pool.memset(s.eps5[:], 1e-5).then_inc(gp, 1)
                own = 1
                made = 0

                def step(ins):
                    nonlocal own
                    own += 1
                    ins.then_inc(gp, 1)
                    pool.wait_ge(gp, own)

                step(pool.memset(s.ident[:], 0.0))
                step(pool.affine_select(out=s.ident[:], in_=s.ident[:], compare_op=ALU.not_equal, fill=1.0,
                                        base=0, pattern=[[-1, 128]], channel_multiplier=1))
                pool.memset(s.one[:], 1.0).then_inc(masks, 1)
                pool.memset(s.average[:], 1.0 / D)
                step(pool.memset(s.ident_bf[:], 0.0))
                step(pool.affine_select(out=s.ident_bf[:], in_=s.ident_bf[:], compare_op=ALU.not_equal, fill=1.0,
                                        base=0, pattern=[[-1, 128]], channel_multiplier=1))
                step(pool.memset(s.sum_sel[:], 0.0))
                sel = s.sum_sel[:].rearrange("p (h c) -> p h c", c=32)
                step(pool.affine_select(out=sel, in_=sel, compare_op=ALU.not_equal, fill=1.0, base=-DH,
                                        pattern=[[-32, 4], [0, 32]], channel_multiplier=1))
                step(pool.memset(group[:], 1.0 / GN_CH))
                g3 = group[:].rearrange("p (g e) -> p g e", e=GN_CH)
                step(pool.affine_select(out=g3, in_=g3, compare_op=ALU.is_ge, fill=0.0, base=0,
                                        pattern=[[-GN_CH, HC // GN_CH], [0, GN_CH]], channel_multiplier=1))
                pool.affine_select(out=g3, in_=g3, compare_op=ALU.is_ge, fill=0.0, base=GN_CH - 1,
                                   pattern=[[GN_CH, HC // GN_CH], [0, GN_CH]], channel_multiplier=-1).then_inc(masks, 1)
                step(pool.memset(s.spread_sel[:], 0.0))
                v = s.spread_sel[:].rearrange("p s (d n) -> p s d n", d=DD)
                for part in range(QPART):
                    step(pool.affine_select(out=v, in_=v, compare_op=ALU.not_equal, fill=1.0, base=-BLK * part,
                                            pattern=[[-DD, SUB], [-1, DD], [0, N]], channel_multiplier=1))
                step(pool.memset(s.state_sel[:], 1.0))
                step(pool.affine_select(out=s.state_sel[:], in_=s.state_sel[:], compare_op=ALU.is_ge, fill=0.0, base=0,
                                        pattern=[[N * DD, SUB], [-N, BLK]], channel_multiplier=1))
                pool.affine_select(out=s.state_sel[:], in_=s.state_sel[:], compare_op=ALU.is_ge, fill=0.0, base=N - 1,
                                   pattern=[[-N * DD, SUB], [N, BLK]], channel_multiplier=-1).then_inc(masks, 1)

            @block.tensor
            def _(pe):
                pe.wait_ge(gp, 3)
                pe.wait_ge(rows_in, 6 * 16)
                pe.transpose(ps[0:HC, 0, 0:NCOL], rows[:], s.ident[0:NCOL, 0:NCOL]).then_inc(pe_small, 1)
                pe.wait_ge(a_in, 16)
                pe.transpose(ps[:, 0, 32:32 + HC], a_rows[:], s.ident[0:HC, 0:HC]).then_inc(pe_small, 1)
                pe.wait_ge(wx_in, 16)
                for k in range(K):
                    for f in range(2):
                        q = 2 * k + f
                        m = pe.transpose(ps[0:HC, 1, 38 * q:38 * q + 38], wx[:, k, HC * f:HC * f + HC],
                                         s.ident[0:38, 0:38])
                m.then_inc(pe_wx, 1)
                pe.wait_ge(wdt_in, 16)
                for q in range(2 * K):
                    bank, at = 6 + q // K, 0
                    m = pe.transpose(ps[0:R, bank, at + HC * (q % K):at + HC * (q % K) + HC], wdt_rows[:, q, :],
                                     s.ident[0:HC, 0:HC])
                m.then_inc(pe_wdt, 1)
                pe.wait_ge(wdt_turned, 1)
                for k in range(K):
                    for f in range(2):
                        m = pe.matmul(ps[0:HC, 2 + k, D * f:D * f + D], wx[0:R, k, HC * f:HC * f + HC],
                                      wdt[:, k, :], start=True, stop=True)
                m.then_inc(pe_wdt, 1)
                pe.wait_ge(masks, 2)
                pe.wait_ge(mean_in, 1)
                pe.matmul(ps[0:HC, 1, 320:328], group[:], mean[:], start=True, stop=True).then_inc(pe_mean, 1)
                pe.wait_ge(var_in, 1)
                pe.matmul(ps[0:HC, 1, 336:344], group[:], spread[:], start=True, stop=True).then_inc(pe_var, 1)

            @block.vector
            def _(v):
                own = Own(v, dve)
                for b in range(NB):
                    v.wait_ge(x_in[b], 16)
                    for f in range(2):
                        for c in range(2):
                            own(v.bn_stats(stats[:, 2 * b + f, c, :], s.X[:, b, f, CH * c:CH * c + CH]))
                own.wait()
                for q in range(2 * NB):
                    own(v.bn_aggr(mv[:, q, :], stats[:, q, :, :].rearrange("p c s -> p (c s)")))
                own.wait()
                v.tensor_copy(mean[:], mv[:, :, 0]).then_inc(mean_in, 1)
                v.wait_ge(pe_small, 2)
                v.tensor_copy(a_exp[:], ps[:, 0, 32:32 + HC]).then_inc(a_turned, 1)
                own(v.tensor_copy(s.cols[:], ps[0:HC, 0, 0:NCOL]))
                v.wait_ge(pe_wdt, 1)
                v.tensor_copy(wdt[:, 0:2, :], ps[0:R, 6, 0:4 * HC].rearrange("p (k d) -> p k d", k=2))
                v.tensor_copy(wdt[:, 2:4, :], ps[0:R, 7, 0:4 * HC].rearrange("p (k d) -> p k d", k=2)
                              ).then_inc(wdt_turned, 1)
                v.wait_ge(pe_mean, 1)
                own(v.tensor_tensor(spread[:], mv[:, :, 0], ps[0:HC, 1, 320:328], ALU.subtract))
                own(v.tensor_copy(mean[:], ps[0:HC, 1, 320:328]))
                own.wait()
                own(v.tensor_tensor(spread[:], spread[:], spread[:], ALU.mult))
                own.wait()
                v.tensor_tensor(spread[:], spread[:], mv[:, :, 1], ALU.add).then_inc(var_in, 1)
                v.wait_ge(std, 1)
                own(v.reciprocal(rstd[:], spread[:]))
                own.wait()
                for q in range(2 * NB):
                    own(v.tensor_scalar(s.X[:, q // 2, q % 2, :], s.X[:, q // 2, q % 2, :], mean[:, q:q + 1],
                                        rstd[:, q:q + 1], ALU.subtract, ALU.mult))
                own(v.memset(s.X[:, NB, :, :], 0.0))
                v.wait_ge(pe_wx, 1)
                for k in range(K):
                    for f in range(2):
                        q = 2 * k + f
                        for i, dst in ((0, s.w_b), (1, s.w_c)):
                            src = ps[0:HC, 1, 38 * q + R + N * i:38 * q + R + N * i + N]
                            own(v.tensor_copy(dst[:, k, f, :].rearrange("p (d n) -> p d n", d=DD),
                                              src.unsqueeze(1).broadcast_to([HC, DD, N])))
                v.wait_ge(pe_wdt, 2)
                for k in range(K):
                    own(v.tensor_copy(s.w_dt[:, k, :, :], ps[0:HC, 2 + k, 0:2 * D].rearrange("p (f d) -> p f d", f=2)))
                v.wait_ge(aexp, 1)
                own(v.tensor_scalar(s.a_neg[:], a_exp[:], -1.0, None, ALU.mult))
                own.wait()
                own(v.tensor_reduce(s.d_sum[:], s.cols[:, COL_DS:COL_DS + 8].rearrange("p (k f) -> p f k", f=2),
                                    AX.X, ALU.add))
                own.wait()


def scan(nc, w, s):
    with ExitStack() as ctx:
        def sb(name, shape, dt=F32):
            return ctx.enter_context(nc.sbuf_tensor(name, shape, dt))

        def sem(name):
            return ctx.enter_context(nc.semaphore(name))

        xt = sb("xt", [HC, 2, L])
        bc = sb("bc", [128, 2, 2, L])
        z_sb = sb("z_sb", [HC, L])
        sp_e = sb("sp_e", [HC, L])
        dt = sb("dt", [HC, 2, L])
        rest = sb("rest", [HC, 2, L])
        parts = sb("parts", [HC, 2, QPART, L], BF16)
        stack = sb("stack", [HC, 2, 2, NBLK, L], BF16)
        dbu = sb("dbu", [128, 3, CH])
        HR = 6
        hs = sb("hs", [128, HR, L])
        AR = 3
        psA = ctx.enter_context(nc.psum_tensor("psA", [128, AR, CH], F32))
        psU = ctx.enter_context(nc.psum_tensor("psU", [128, 2, CH], F32))
        psY = ctx.enter_context(nc.psum_tensor("psY", [128, 2, CH], F32))
        psP = ctx.enter_context(nc.psum_tensor("psP", [128, CH], F32))

        dt_spread = sem("dt_spread")
        dtu_spread = sem("dtu_spread")
        decay_ready = sem("decay_ready")
        dbu_ready = sem("dbu_ready")
        scan_done = sem("scan_done")
        hc_ready = sem("hc_ready")
        summed = sem("summed")
        y_taken = sem("y_taken")
        z_proj = sem("z_proj")
        bc_proj = sem("bc_proj")
        z_taken = sem("z_taken")
        clipped = sem("clipped")
        log_ready = sem("log_ready")
        exp_own = sem("exp_own")
        dt_own = sem("dt_own")
        dt_ready = sem("dt_ready")
        bc_ready = sem("bc_ready")
        hi_ready = sem("hi_ready")
        rest_ready = sem("rest_ready")
        mid_ready = sem("mid_ready")
        lo_ready = sem("lo_ready")
        xt_half = sem("xt_half")
        stacked = [sem(f"stacked{p}") for p in range(2)]

        def order(ui):
            p, r, f = ui // 4, ui // 2 % 2, ui % 2
            return p, r, f, p + 2 * r

        SP_LIMIT = 40.0

        def landed(b, ui):
            return (b * (UNITS // 2) + ui // 2 + 1) * (16 * QPART * NBLK)

        Z_PE = {12: (0, 0), 13: (0, 1), 15: (1, 0), 16: (1, 1)}
        BC_PE = {3 * (i // 2) + i % 2: (i // 2, i % 2) for i in range(8)}

        def source(nb, nu):
            p, r, f, k = order(nu)
            return (lambda h, lo: xt[:, h, lo:lo + CH]) if p else (lambda h, lo: s.X[:, nb, h, lo:lo + CH])

        def units_ahead(b, ui, d):
            return b + (ui + d) // UNITS, (ui + d) % UNITS, b * UNITS + (ui + d)

        with nc.Block() as block:
            @block.tensor
            def _(pe):
                pe.sem_inc(dbu_ready, 2)
                pe.sem_inc(scan_done, 2)
                pe.sem_inc(summed, 1)

                def project(out, wt, rhs, h, ready):
                    m = pe.matmul(out, wt, rhs, start=(h == 0), stop=(h == 1))
                    if h == 1:
                        m.then_inc(ready, 1)

                def z_side(q, nb, nu, n1, kk):
                    if q not in Z_PE:
                        return
                    c, h = Z_PE[q]
                    p, r, f, k = order(nu)
                    if h == 0:
                        if c:
                            pe.wait_ge(z_taken, n1 * 2 + 1)
                        elif kk is not None:
                            pe.wait_ge(bc_ready, kk * 4 + 4)
                        elif not isinstance(n1, int):
                            pe.wait_ge(z_taken, n1 * 2)
                        if p:
                            pe.wait_ge(xt_half, nb * 2 + 2)
                    project(psP[0:HC, :], s.w_dt[:, k, h, HC * f:HC * f + HC], source(nb, nu)(h, CH * c), h, z_proj)

                def bc_side(q, nb, nu, n1, kk):
                    if q not in BC_PE:
                        return
                    i, h = BC_PE[q]
                    p, r, f, k = order(nu)
                    if h == 0:
                        if i:
                            pe.wait_ge(bc_ready, kk * 4 + i)
                        else:
                            pe.wait_ge(z_taken, n1 * 2 + 2)
                        if p:
                            pe.wait_ge(xt_half, nb * 2 + 2)
                    project(psP[:, :], (s.w_b, s.w_c)[i // 2][:, k, h, :], source(nb, nu)(h, CH * (i % 2)), h, bc_proj)

                def sum_states(n, trip):
                    if trip == 0:
                        pe.wait_ge(y_taken, n)
                    pe.wait_ge(hc_ready, n * TILES + 3 * trip + 3)
                    for c in range(2):
                        for j in range(NBLK):
                            slot = (3 * trip + j) % HR
                            m = pe.matmul(psY[BLK * j:BLK * j + BLK, c, :], s.state_sel[:, trip, :],
                                          hs[:, slot, CH * c:CH * c + CH], start=(trip == 0), stop=(trip == SUB - 1))
                    m.then_inc(summed, 1)

                for q in Z_PE:
                    z_side(q, 0, 0, 0, None)
                for q in BC_PE:
                    bc_side(q, 0, 0, 0, 0)
                for q in Z_PE:
                    z_side(q, 0, 1, 1, 0)
                with pe.Fori(0, NB, 1) as b:
                    for ui in range(UNITS):
                        n = b * UNITS + ui
                        p, r, f, k = order(ui)
                        pe.wait_ge(stacked[ui % 2], landed(b, ui))
                        for t in range(TILES):
                            gg, j = t // NBLK, t % NBLK
                            for c in range(2):
                                q = 2 * t + c
                                pos = c if r == 0 else 1 - c
                                g = n * (2 * TILES) + q
                                pe.wait_ge(dbu_ready, g + 1)
                                pe.matmul(psU[:, q % 2, :], s.spread_sel[:, gg, :],
                                          stack[:, ui % 2, 1, j, CH * pos:CH * pos + CH],
                                          start=True, stop=True).then_inc(dtu_spread, 1)
                                pe.wait_ge(scan_done, g)
                                pe.matmul(psA[:, q % AR, :], s.spread_sel[:, gg, :],
                                          stack[:, ui % 2, 0, j, CH * pos:CH * pos + CH],
                                          start=True, stop=True).then_inc(dt_spread, 1)
                                if ui % 2:
                                    bc_side(q, *units_ahead(b, ui, 1), b * K + (ui + 1) // 2)
                                z_side(q, *units_ahead(b, ui, 2), b * K + (ui + 1) // 2 if ui % 2 else None)
                            if t % 3 == 2:
                                if t > 3:
                                    sum_states(n, t // 3 - 1)
                                elif ui:
                                    sum_states(n - 1, SUB - 1)
                        if ui == UNITS - 1:
                            sum_states(n, SUB - 1)

            @block.scalar
            def _(act):
                def z_side(q, nb, nu, n1):
                    p, r, f, k = order(nu)
                    if q in (14, 17):
                        c = (q - 14) // 3
                        act.wait_ge(z_proj, n1 * 2 + c + 1)
                        act.wait_ge(dt_own, n1 * 2)
                        nc.scalar.activation(z_sb[:, CH * c:CH * c + CH], psP[0:HC, :], ACT.Identity,
                                             bias=s.cols[:, COL_DTB + 2 * k + f:COL_DTB + 2 * k + f + 1]
                                             ).then_inc(z_taken, 1)
                    if q in (17, 20):
                        c = (q - 17) // 3
                        act.wait_ge(clipped, n1 * 2 + c + 1)
                        e = sp_e[:, CH * c:CH * c + CH]
                        nc.scalar.activation(e, e, ACT.Exp).then_inc(exp_own, 1)
                        act.wait_ge(exp_own, n1 * 2 + c + 1)
                        nc.scalar.activation(e, e, ACT.Ln, bias=s.one[0:HC, :]).then_inc(log_ready, 1)

                def bc_side(q, nu, kk):
                    if q in (2, 5, 8, 11):
                        i = q // 3
                        act.wait_ge(bc_proj, kk * 4 + i + 1)
                        if i == 0 and not isinstance(kk, int):
                            act.wait_ge(hc_ready, (kk - 1) * (2 * TILES))
                        nc.scalar.copy(bc[:, nu // 2 % 2, i // 2, CH * (i % 2):CH * (i % 2) + CH],
                                       psP[:, :]).then_inc(bc_ready, 1)

                def split_side(q, n1, b, ui):
                    if q == 0:
                        act.wait_ge(dt_ready, n1 * 2 + 2)
                        if ui is not None:
                            act.wait_ge(stacked[ui % 2], landed(b, ui))
                        for tq in range(2):
                            nc.scalar.copy(parts[:, tq, 0, :], dt[:, tq, :]).then_inc(hi_ready, 1)
                    if q in (4, 6):
                        tq = (q - 4) // 2
                        act.wait_ge(rest_ready, n1 * 2 + tq + 1)
                        nc.scalar.copy(parts[:, tq, 1, :], rest[:, tq, :]).then_inc(mid_ready, 1)

                nc.scalar.preload_act_table_set("natural_log_exp_and_others")
                for q in (14, 17, 20):
                    z_side(q, 0, 0, 0)
                for q in (2, 5, 8, 11):
                    bc_side(q, 0, 0)
                for q in (0, 4, 6):
                    split_side(q, 0, 0, None)
                for q in (14, 17, 20):
                    z_side(q, 0, 1, 1)
                with act.Fori(0, NB, 1) as b:
                    for ui in range(UNITS):
                        n = b * UNITS + ui
                        p, r, f, k = order(ui)
                        for t in range(TILES):
                            gg, j = t // NBLK, t % NBLK
                            col = k * (D // DD) + TILES * f + SUB * j + gg
                            for c in range(2):
                                q = 2 * t + c
                                g = n * (2 * TILES) + q
                                act.wait_ge(dt_spread, g + 1)
                                nc.scalar.activation(psA[:, q % AR, :], psA[:, q % AR, :], ACT.Exp,
                                                     scale=s.a_neg[:, col:col + 1]).then_inc(decay_ready, 1)
                                if ui % 2:
                                    bc_side(q, (ui + 1) % UNITS, b * K + (ui + 1) // 2)
                                split_side(q, n + 1, b, ui)
                                z_side(q, *units_ahead(b, ui, 2))
                                if ui == 1 and q in (21, 22):
                                    h = q - 21
                                    act.wait_ge(dt_ready, b * (2 * UNITS))
                                    nc.scalar.copy(xt[:, h, :].rearrange("p (w h) -> p w h", w=WW),
                                                   s.X[:, b, h, :].rearrange("p (h w) -> p w h", h=HH)
                                                   ).then_inc(xt_half, 1)

            @block.gpsimd
            def _(pool):
                def split_side(t, n1):
                    for tq in range(2):
                        if t == tq:
                            pool.wait_ge(hi_ready, n1 * 2 + tq + 1)
                            pool.wait_ge(mid_ready, n1 * 2)
                            pool.tensor_tensor(rest[:, tq, :], dt[:, tq, :], parts[:, tq, 0, :],
                                               ALU.subtract).then_inc(rest_ready, 1)
                        if t == 3 + tq:
                            pool.wait_ge(mid_ready, n1 * 2 + tq + 1)
                            pool.tensor_tensor(parts[:, tq, 2, :], rest[:, tq, :], parts[:, tq, 1, :],
                                               ALU.subtract).then_inc(lo_ready, 1)

                for t in (0, 1, 3, 4):
                    split_side(t, 0)
                with pool.Fori(0, NB, 1) as b:
                    for ui in range(UNITS):
                        n = b * UNITS + ui
                        kslot = ui // 2 % 2
                        pool.wait_ge(bc_ready, (b * K + ui // 2 + 1) * 4)
                        for t in range(TILES):
                            m = n * TILES + t
                            pool.wait_ge(scan_done, 2 * m + 2 + 2)
                            h = hs[:, t % HR, :]
                            pool.tensor_tensor(h, h, bc[:, kslot, 1, :], ALU.mult).then_inc(hc_ready, 1)
                            split_side(t, n + 1)

            @block.vector
            def _(v):
                own = [0]

                def z_side(q, nb, nu, n1):
                    p, r, f, k = order(nu)
                    if q in (15, 18):
                        c = (q - 15) // 3
                        cs = slice(CH * c, CH * c + CH)
                        v.wait_ge(z_taken, n1 * 2 + c + 1)
                        v.wait_ge(dt_ready, n1 * 2)
                        v.tensor_scalar(sp_e[:, cs], z_sb[:, cs], SP_LIMIT, None, ALU.min).then_inc(clipped, 1)
                    if q in (19, 22):
                        c = (q - 19) // 3
                        cs = slice(CH * c, CH * c + CH)
                        v.wait_ge(log_ready, n1 * 2 + c + 1)
                        v.wait_ge(rest_ready, n1 * 2)
                        v.tensor_tensor(dt[:, 0, cs], z_sb[:, cs], sp_e[:, cs], ALU.max).then_inc(dt_own, 1)
                        v.wait_ge(dt_own, n1 * 2 + c + 1)
                        v.tensor_tensor(dt[:, 1, cs], dt[:, 0, cs], source(nb, nu)(f, CH * c),
                                        ALU.mult).then_inc(dt_ready, 1)

                def product(n, ui, q, b):
                    p, r, f, k = order(ui)
                    g = n * (2 * TILES) + q
                    pos = q % 2 if r == 0 else 1 - q % 2
                    if q == 0 and ui % 2 == 0:
                        v.wait_ge(bc_ready, (b * K + ui // 2 + 1) * 4)
                    v.wait_ge(dtu_spread, g + 1)
                    v.wait_ge(scan_done, g)
                    v.tensor_tensor(dbu[:, q % 3, :], psU[:, q % 2, :],
                                    bc[:, ui // 2 % 2, 0, CH * pos:CH * pos + CH], ALU.mult).then_inc(dbu_ready, 1)

                def take(n, b, ui):
                    p, r, f, k = order(ui)
                    v.wait_ge(summed, n * SUB + SUB + 1)
                    acc = psY[0:HC, :, :].rearrange("p c l -> p (c l)")
                    y = s.Y[:, b, f, :]
                    if p == 0 and r == 0:
                        v.scalar_tensor_tensor(out=y, in0=s.X[:, b, f, :], scalar=s.d_sum[:, f:f + 1], in1=acc,
                                               op0=ALU.mult, op1=ALU.add).then_inc(y_taken, 1)
                    elif p == 0:
                        v.tensor_tensor(y, y, acc, ALU.add).then_inc(y_taken, 1)
                    else:
                        yt = y.rearrange("p (h w) -> p w h", h=HH)
                        v.tensor_tensor(yt, yt, acc.rearrange("p (w h) -> p w h", w=WW), ALU.add).then_inc(y_taken, 1)

                for n1 in range(2):
                    for q in (15, 18, 19, 22):
                        z_side(q, 0, n1, n1)
                with v.Fori(0, NB, 1) as b:
                    for ui in range(UNITS):
                        n = b * UNITS + ui
                        p, r, f, k = order(ui)
                        product(n, ui, 0, b)
                        for q in range(2 * TILES):
                            t = q // 2
                            g = n * (2 * TILES) + q
                            if q + 1 < 2 * TILES:
                                product(n, ui, q + 1, b)
                            pos = q % 2 if r == 0 else 1 - q % 2
                            if q % 6 == 0:
                                v.wait_ge(summed, n * SUB + q // 6)
                            v.wait_ge(decay_ready, g + 1)
                            v.wait_ge(dbu_ready, g + 1 + 2)
                            if q % 2:
                                v.wait_ge(scan_done, g + 2)
                            h = hs[:, t % HR, CH * pos:CH * pos + CH]
                            da, du = psA[:, q % AR, :], dbu[:, q % 3, :]
                            if r:
                                h, da, du = h[:, ::-1], da[:, ::-1], du[:, ::-1]
                            if q % 2 == 0:
                                init = 0.0
                            else:
                                at = CH - 1 if r == 0 else CH
                                init = hs[:, t % HR, at:at + 1]
                            v.tensor_tensor_scan(h, da, du, init, ALU.mult, ALU.add).then_inc(scan_done, 1)
                            if q == 9 and ui:
                                take(n - 1, b, ui - 1)
                            z_side(q, *units_ahead(b, ui, 2))
                        if ui == UNITS - 1:
                            take(n, b, ui)

            @block.sync
            def _(sp):
                def stack_up(n1, slot):
                    for part, ready in enumerate((hi_ready, mid_ready, lo_ready)):
                        sp.wait_ge(ready, n1 * 2 + 2)
                        for j in range(NBLK):
                            sp.dma_start(stack[BLK * part:BLK * part + BLK, slot, :, j, :],
                                         parts[BLK * j:BLK * j + BLK, :, part, :]).then_inc(stacked[slot], 16)

                stack_up(0, 0)
                with sp.Fori(0, NB, 1) as b:
                    for ui in range(UNITS):
                        n = b * UNITS + ui
                        sp.wait_ge(dt_spread, n * (2 * TILES))
                        stack_up(n + 1, (ui + 1) % 2)
                sp.wait_ge(stacked[0], landed(NB, 0))


def layer_norm(nc, s, src, dst, tag, after=None):
    with ExitStack() as ctx:
        def sb(name, shape, dt=F32):
            return ctx.enter_context(nc.sbuf_tensor(tag + name, shape, dt))

        def sem(name):
            return ctx.enter_context(nc.semaphore(tag + name))

        sq = sb("sq", [HC, 2, 2, CH])
        dev = sb("dev", [HC, 2, CH])
        ps_mean = ctx.enter_context(nc.psum_tensor(tag + "ps_mean", [HC, 2, CH], F32))
        ps_var = ctx.enter_context(nc.psum_tensor(tag + "ps_var", [HC, 2, CH], F32))
        mean_ready, var_ready = sem("mean_ready"), sem("var_ready")
        centred, inverse, normed = sem("centred"), sem("inverse"), sem("normed")
        squared, dev_ready = sem("squared"), sem("dev_ready")
        STEPS = 2 * NB

        def part(t, i, f):
            return t[:, i // 2, f, CH * (i % 2):CH * (i % 2) + CH]

        more = after(ctx, sb, sem, normed) if after else {}
        with nc.Block() as block:
            @block.tensor
            def _(pe):
                for i in range(STEPS + 1):
                    if i < STEPS:
                        if i >= 2:
                            pe.wait_ge(centred, i - 1)
                        for f in range(2):
                            m = pe.matmul(ps_mean[:, i % 2, :], s.average[:], part(src, i, f), start=(f == 0), stop=(f == 1))
                        m.then_inc(mean_ready, 1)
                    if i:
                        pe.wait_ge(squared, i)
                        if i >= 3:
                            pe.wait_ge(dev_ready, i - 2)
                        for f in range(2):
                            m = pe.matmul(ps_var[:, (i - 1) % 2, :], s.average[:], sq[:, (i - 1) % 2, f, :],
                                          start=(f == 0), stop=(f == 1))
                        m.then_inc(var_ready, 1)

            @block.vector
            def _(v):
                if "load" in more:
                    more["load"](v)
                for i in range(STEPS + 1):
                    if i < STEPS:
                        v.wait_ge(mean_ready, i + 1)
                        for f in range(2):
                            m = v.tensor_tensor(part(dst, i, f), part(src, i, f), ps_mean[:, i % 2, :], ALU.subtract)
                        m.then_inc(centred, 1)
                    if i:
                        v.wait_ge(dev_ready, i)
                        v.wait_ge(centred, i)
                        d = dev[:, (i - 1) % 2, :]
                        v.reciprocal(d, d).then_inc(inverse, 1)
                        v.wait_ge(inverse, i)
                        for f in range(2):
                            m = v.tensor_tensor(part(dst, i - 1, f), part(dst, i - 1, f), d, ALU.mult)
                        m.then_inc(normed, 1)
                if "vector" in more:
                    more["vector"](v)

            @block.scalar
            def _(act):
                for i in range(STEPS + 1):
                    if i < STEPS:
                        act.wait_ge(centred, i + 1)
                        if i >= 2:
                            act.wait_ge(var_ready, i - 1)
                        for f in range(2):
                            m = nc.scalar.activation(sq[:, i % 2, f, :], part(dst, i, f), ACT.Square)
                        m.then_inc(squared, 1)
                    if i:
                        act.wait_ge(var_ready, i)
                        if i >= 3:
                            act.wait_ge(normed, i - 2)
                        nc.scalar.activation(dev[:, (i - 1) % 2, :], ps_var[:, (i - 1) % 2, :], ACT.Sqrt,
                                             bias=s.eps5[0:HC, :]).then_inc(dev_ready, 1)
                if "scalar" in more:
                    more["scalar"](act)

            if "sync" in more:
                @block.sync
                def _(sp):
                    more["sync"](sp)


def conv_out(nc, w, s):
    def after(ctx, sb, sem, normed):
        x_in = [sem(f"x_again{b}") for b in range(NB)]
        gelu_done = sem("gelu_done")

        def scalar(act):
            act.wait_ge(normed, 2 * NB)
            for b in range(NB):
                for f in range(2):
                    nc.scalar.activation(s.Z[:, b, f, :], s.Z[:, b, f, :], ACT.Gelu,
                                         bias=s.cols[:, COL_LNB + f:COL_LNB + f + 1],
                                         scale=s.cols[:, COL_LNW + f:COL_LNW + f + 1]).then_inc(gelu_done, 1)

        def vector(v):
            for b in range(NB):
                v.wait_ge(x_in[b], 16)
                for f in range(2):
                    v.wait_ge(gelu_done, 2 * b + f + 1)
                    v.tensor_tensor(s.Y[:, b, f, :], s.raw[:, b, f, :], s.Z[:, b, f, :], ALU.add)

        def sync(sp):
            for b in range(NB):
                sp.dma_start(s.raw[:, b, :, :], w.x[b].rearrange("(f p) h w -> p f (h w)", p=HC)).then_inc(x_in[b], 16)

        return {"scalar": scalar, "vector": vector, "sync": sync}

    layer_norm(nc, s, s.Y, s.Z, "lc_", after)


def qkv(nc, w, s):
    with ExitStack() as ctx:
        def sb(name, shape, dt=F32):
            return ctx.enter_context(nc.sbuf_tensor(name, shape, dt))

        def sem(name):
            return ctx.enter_context(nc.semaphore(name))

        w_rows = sb("w_rows", [HC, 6, D])
        w_qkv = sb("w_qkv", [HC, 2, 3 * D])
        vb = sb("vb", [1, D])
        ones_row = sb("ones_row", [1, 128])
        qb = sb("qb", [HC, 4])
        p_rows = sb("p_rows", [HC, 2, D])
        p_pad = sb("p_pad", [HC, 2, 3, 4, 32])
        val = sb("val", [HC, 2, L])
        rest = sb("qrest", [HC, 2, L])
        parts = sb("qparts", [HC, 2, QPART, L], BF16)
        hankel = sb("hankel", [19, 19, HEADS])
        last_row = sb("last_row", [19, HEADS])
        ps_w = ctx.enter_context(nc.psum_tensor("ps_w", [128, 4, CH], F32))
        ps_q = ctx.enter_context(nc.psum_tensor("ps_q", [HC, 2, CH], F32))
        ps_v = ctx.enter_context(nc.psum_tensor("ps_v", [128, 2, CH], F32))
        w_in, vb_in, p_in, tab_ext, tab_in, last_in = (
            sem("w_in"), sem("vb_in"), sem("p_in"), sem("tab_ext"), sem("tab_in"), sem("last_in"))
        pool_ready, w_turned, w_taken, q_proj, q_taken, v_proj, v_taken = (
            sem("pool_ready"), sem("w_turned"), sem("w_taken"), sem("q_proj"), sem("q_taken"), sem("v_proj"), sem("v_taken"))
        own_v, hi_ready, rest_ready, mid_ready, lo_ready, padded, corner, corner_turned = (
            sem("own_v"), sem("qhi"), sem("qrestr"), sem("qmid"), sem("qlo"), sem("padded"), sem("corner"), sem("corner_turned"))
        stored = [sem(f"stored{i}") for i in range(2)]
        NQ = 4 * NB

        with nc.Block() as block:
            @block.sync
            def _(sp):
                sp.dma_start(w_rows[:], w.qkvw.rearrange("(m p) d -> p m d", p=HC)).then_inc(w_in, 16)
                sp.dma_start(vb[:], w.qkvb[2 * D:3 * D].rearrange("(o d) -> o d", o=1)).then_inc(vb_in, 16)
                sp.dma_start(p_rows[:], w.projw.rearrange("(m p) d -> p m d", p=HC)).then_inc(p_in, 16)
                sp.dma_start(s.ext[0:19, :], w.table).then_inc(tab_ext, 16)
                sp.dma_start(s.ext[19:37, :], w.table[0:18, :]).then_inc(tab_ext, 16)
                sp.dma_start(last_row[:], w.table[18:19, :].broadcast_to([19, HEADS])).then_inc(last_in, 16)
                sp.wait_ge(tab_ext, 32)
                win = bass.AP(s.ext[:, :].tensor, 0, [[HEADS, 19], [1, 19 * HEADS]])
                sp.dma_start(hankel[:].rearrange("p e h -> p (e h)"), win).then_inc(tab_in, 16)
                for i in range(NQ):
                    b, qk, f = i // 4, i // 2 % 2, i % 2
                    sp.wait_ge(lo_ready, i + 1)
                    sp.wait_ge(mid_ready, i + 1)
                    sp.dma_start(s.qk_dram[b, qk, :, HC * f:HC * f + HC, :].rearrange("a p l -> p a l"),
                                 parts[:, i % 2, :, :]).then_inc(stored[i % 2], 16)
                for i in range(2):
                    sp.wait_ge(stored[i], 16 * (NQ // 2))

            @block.gpsimd
            def _(pool):
                pool.memset(ones_row[:], 1.0).then_inc(pool_ready, 1)
                pool.memset(p_pad[:], 0.0).then_inc(pool_ready, 1)
                pool.memset(s.V[:], 0.0).then_inc(pool_ready, 1)
                pool.wait_ge(pool_ready, 3)
                pool.memset(s.V[:, :, :, :, DH:DH + 1].rearrange("p b t h o -> p (b t) (h o)"), 1.0).then_inc(pool_ready, 1)
                pool.memset(s.shift[:], 0.0).then_inc(pool_ready, 1)
                pool.wait_ge(pool_ready, 5)
                pool.affine_select(out=s.shift[:], in_=s.shift[:], compare_op=ALU.not_equal, fill=1.0, base=128 - 19,
                                   pattern=[[-1, 128]], channel_multiplier=1).then_inc(pool_ready, 1)
                pool.wait_ge(corner, 2)
                pool.affine_select(out=s.corner_q[:], in_=s.corner_q[:], compare_op=ALU.is_ge, fill=0.0, base=0,
                                   pattern=[[0, HEADS], [1, 19]], channel_multiplier=-1).then_inc(corner, 1)

            @block.tensor
            def _(pe):
                pe.wait_ge(w_in, 16)
                for m in range(6):
                    for f in range(2):
                        t = pe.transpose(ps_w[0:HC, 2 * f + m // 3, HC * (m % 3):HC * (m % 3) + HC],
                                         w_rows[:, m, HC * f:HC * f + HC], s.ident[0:HC, 0:HC])
                t.then_inc(w_turned, 1)
                pe.wait_ge(w_taken, 1)
                pe.wait_ge(pool_ready, 6)
                pe.wait_ge(vb_in, 16)
                nv = 0
                for b in range(NB):
                    for j in range(8):
                        i = 8 * b + j
                        qk, f, c = j // 4, j // 2 % 2, j % 2
                        if i >= 2:
                            pe.wait_ge(q_taken, i - 1)
                        for h in range(2):
                            t = pe.matmul(ps_q[:, i % 2, :], w_qkv[:, h, D * qk + HC * f:D * qk + HC * f + HC],
                                          s.Z[:, b, h, CH * c:CH * c + CH], start=(h == 0), stop=(h == 1))
                        t.then_inc(q_proj, 1)
                        if nv >= 2:
                            pe.wait_ge(v_taken, nv - 1)
                        for h in range(2):
                            pe.matmul(ps_v[:, nv % 2, 0:D], s.Z[:, b, h, 128 * j:128 * j + 128],
                                      w_qkv[:, h, 2 * D:3 * D], start=(h == 0), stop=False)
                        pe.matmul(ps_v[:, nv % 2, 0:D], ones_row[:], vb[:], start=False, stop=True).then_inc(v_proj, 1)
                        nv += 1
                pe.wait_ge(padded, 1)
                for g in range(3):
                    for f in range(2):
                        t = pe.transpose(ps_w[:, g, HC * f:HC * f + HC],
                                         p_pad[:, f, g, :, :].rearrange("p j c -> p (j c)"), s.ident[0:HC, 0:HC])
                pe.wait_ge(corner, 3)
                for h in range(HEADS):
                    t = pe.transpose(ps_w[0:19, 3, 19 * h:19 * h + 19], s.corner_q[:, h, :], s.ident[0:19, 0:19])
                t.then_inc(corner_turned, 1)

            @block.scalar
            def _(act):
                for i in range(NQ):
                    b, qk, f = i // 4, i // 2 % 2, i % 2
                    act.wait_ge(own_v, 1)
                    if i >= 2:
                        act.wait_ge(lo_ready, i - 1)
                        act.wait_ge(stored[i % 2], 16 * (i // 2))
                    for c in range(2):
                        act.wait_ge(q_proj, 2 * i + c + 1)
                        nc.scalar.activation(val[:, i % 2, CH * c:CH * c + CH], ps_q[:, (2 * i + c) % 2, :], ACT.Identity,
                                             bias=qb[:, 2 * qk + f:2 * qk + f + 1], scale=(DH ** -0.5 if qk == 0 else 1.0)
                                             ).then_inc(q_taken, 1)
                    act.wait_ge(q_taken, 2 * i + 2)
                    nc.scalar.copy(parts[:, i % 2, 0, :], val[:, i % 2, :]).then_inc(hi_ready, 1)
                    if i:
                        act.wait_ge(rest_ready, i)
                        nc.scalar.copy(parts[:, (i - 1) % 2, 1, :], rest[:, (i - 1) % 2, :]).then_inc(mid_ready, 1)
                act.wait_ge(rest_ready, NQ)
                nc.scalar.copy(parts[:, (NQ - 1) % 2, 1, :], rest[:, (NQ - 1) % 2, :]).then_inc(mid_ready, 1)

            @block.vector
            def _(v):
                v.tensor_scalar(qb[:, 0:2], s.cols[:, COL_Q:COL_Q + 2], DH ** -0.5, None, ALU.mult)
                v.tensor_copy(qb[:, 2:4], s.cols[:, COL_K:COL_K + 2]).then_inc(own_v, 1)
                v.wait_ge(w_turned, 1)
                for f in range(2):
                    for g in range(2):
                        t = v.tensor_copy(w_qkv[:, f, 3 * HC * g:3 * HC * g + 3 * HC], ps_w[0:HC, 2 * f + g, 0:3 * HC])
                t.then_inc(w_taken, 1)
                v.wait_ge(pool_ready, 4)
                nv = 0
                for i in range(NQ + 1):
                    if i < NQ:
                        v.wait_ge(hi_ready, i + 1)
                        if i >= 2:
                            v.wait_ge(mid_ready, i - 1)
                        v.tensor_tensor(rest[:, i % 2, :], val[:, i % 2, :], parts[:, i % 2, 0, :],
                                        ALU.subtract).then_inc(rest_ready, 1)
                        for _ in range(2):
                            v.wait_ge(v_proj, nv + 1)
                            v.tensor_copy(s.V[:, nv // 8, nv % 8, :, 0:DH],
                                          ps_v[:, nv % 2, 0:D].rearrange("p (h d) -> p h d", d=DH)).then_inc(v_taken, 1)
                            nv += 1
                    if i:
                        v.wait_ge(mid_ready, i)
                        v.tensor_tensor(parts[:, (i - 1) % 2, 2, :], rest[:, (i - 1) % 2, :], parts[:, (i - 1) % 2, 1, :],
                                        ALU.subtract).then_inc(lo_ready, 1)
                v.wait_ge(p_in, 16)
                v.wait_ge(pool_ready, 4)
                for f in range(2):
                    v.tensor_copy(p_pad[:, f, :, :, 0:DH].rearrange("p g j c -> p (g j) c"),
                                  p_rows[:, f, :].rearrange("p (g c) -> p g c", c=DH))
                    t = v.tensor_copy(p_pad[:, f, 0, 0, DH:DH + 1], s.cols[:, COL_PB + f:COL_PB + f + 1])
                t.then_inc(padded, 1)
                v.wait_ge(tab_in, 16)
                v.wait_ge(last_in, 16)
                v.tensor_copy(s.corner_q[:], hankel[:].rearrange("p e h -> p h e")[:, :, ::-1]).then_inc(corner, 1)
                v.wait_ge(corner, 1)
                v.tensor_tensor(s.corner_q[:], s.corner_q[:], last_row[:].unsqueeze(2).broadcast_to([19, HEADS, 19]),
                                ALU.subtract).then_inc(corner, 1)
                v.wait_ge(corner_turned, 1)
                v.tensor_copy(s.corner_k[:].rearrange("p h j -> p (h j)"), ps_w[0:19, 3, 0:19 * HEADS])
                v.tensor_copy(s.w_proj[:], ps_w[:, 0:3, 0:D])


def attention(nc, w, s):
    with ExitStack() as ctx:
        def sb(name, shape, dt=F32):
            return ctx.enter_context(nc.sbuf_tensor(name, shape, dt))

        def sem(name):
            return ctx.enter_context(nc.semaphore(name))

        Q_PARTS, K_PARTS = [0, 0, 1, 1, 0, 2], [0, 1, 0, 1, 2, 0]
        KQ = DH * len(Q_PARTS)
        KM = KQ + QPART
        NHG = 3
        GH = 4
        KT = L // 128
        HALF = 2 * NHG * KT
        MAXES = GH * KT * 2

        qs = sb("qs", [KM, NHG, GH, L], BF16)
        ks = sb("ks", [KM, NHG, GH, L], BF16)
        mx = sb("mx", [128, NHG, MAXES])
        nm = sb("nm", [128, 2, 32])
        nmp = sb("nmp", [128, QPART, 32], BF16)
        nmt = sb("nmt", [QPART * 32, 128], BF16)
        P = sb("P", [128, 2, GH, CH])
        v_now = sb("v_now", [128, KT, HEADS, 32])
        o_raw = sb("o_raw", [128, 2, CH])
        rec = sb("rec", [128, CH])
        o_n = sb("o_n", [128, NHG, L])
        ps1 = ctx.enter_context(nc.psum_tensor("ps1", [128, 2, CH], F32))
        ps2 = ctx.enter_context(nc.psum_tensor("ps2", [128, 2, 2, CH], F32))
        psO = ctx.enter_context(nc.psum_tensor("psO", [128, CH], F32))
        psM = ctx.enter_context(nc.psum_tensor("psM", [128, CH], F32))

        stack_in = [sem(f"stack_in{i}") for i in range(NHG)]
        rows_set = sem("rows_set")
        s1_ready = sem("s1_ready")
        max_done = sem("max_done")
        s2_ready = sem("s2_ready")
        exp_done = sem("exp_done")
        pv_done = sem("pv_done")
        o_taken = sem("o_taken")
        misc_ready = sem("misc_ready")
        misc_taken = sem("misc_taken")
        own = sem("own_at")
        nmp_ready = sem("nmp_ready")
        nm_store, nm_in = sem("nm_store"), sem("nm_in")
        on_ready = sem("on_ready")
        v_set = sem("v_set")
        OWN = 6

        MISC = 3 * NHG + 4

        def step_ahead(b, hg, d):
            return b + (hg + d) // NHG, (hg + d) % NHG, b * NHG + hg + d

        with nc.Block() as block:
            @block.gpsimd
            def _(pool):
                pool.memset(ks[KQ:KM, :, :, :].rearrange("p g h l -> p (g h l)"), 1.0).then_inc(rows_set, 1)

                def place(b, hg):
                    h = slice(GH * hg, GH * hg + GH)
                    pool.tensor_copy(v_now[:, :, h, :].rearrange("p t h d -> p t (h d)"),
                                     s.V[:, b, :, h, :].rearrange("p t h d -> p t (h d)")).then_inc(v_set, 1)

                pool.wait_ge(rows_set, 1)
                for hg in range(NHG):
                    place(0, hg)
                with pool.Fori(0, NB, 1) as b:
                    for hg in range(NHG):
                        pool.wait_ge(pv_done, (b * NHG + (hg + 1)) * (2 * KT) + 1)
                        place((b + 1) % NB, hg)

            @block.sync
            def _(sp):
                def load(b, hg):
                    for j in range(len(Q_PARTS)):
                        for stack, qk, part in ((qs, 0, Q_PARTS[j]), (ks, 1, K_PARTS[j])):
                            sp.dma_start(stack[DH * j:DH * j + DH, hg, :, :],
                                         s.qk_dram[b, qk, part, DH * GH * hg:DH * GH * (hg + 1), :]
                                         .rearrange("(h c) l -> c h l", c=DH)).then_inc(stack_in[hg], 16)

                def maxima(i, hg):
                    sp.dma_start(s.nm_dram[:, :], nmt[:]).then_inc(nm_store, 16)
                    sp.wait_ge(nm_store, (i + 1) * 16)
                    sp.dma_start(qs[KQ:KM, hg, :, :].rearrange("p h l -> p (h l)"),
                                 s.nm_dram[:, :].rearrange("(a r) c -> a (r c)", a=QPART)).then_inc(nm_in, 16)
                    sp.wait_ge(nm_in, (i + 1) * 16)

                for hg in range(NHG):
                    load(0, hg)
                sp.wait_ge(misc_taken, 1)
                maxima(0, 0)
                with sp.Fori(0, NB, 1) as b:
                    for hg in range(NHG):
                        sp.wait_ge(misc_taken, b * MISC + (3 * hg + 2))
                        maxima(b * NHG + (hg + 1), (hg + 1) % NHG)
                        sp.wait_ge(s2_ready, (b * HALF + (hg + 1) * 2 * KT) * 2)
                        load((b + 1) % NB, hg)
                for hg in range(NHG):
                    sp.wait_ge(stack_in[hg], (NB + 1) * 2 * len(Q_PARTS) * 16)

            @block.tensor
            def _(pe):
                pe.sem_inc(max_done, 1)
                pe.sem_inc(exp_done, 2)
                pe.sem_inc(pv_done, 1)
                pe.sem_inc(on_ready, 1)

                def first_scores(u, i, hg):
                    head, qt, c = u // (2 * KT), u // 2 % KT, u % 2
                    pe.wait_ge(max_done, i * MAXES + u)
                    corner = qt == 0 and c == 1
                    m = pe.matmul(ps1[:, u % 2, :], qs[0:KQ, hg, head, 128 * qt:128 * qt + 128],
                                  ks[0:KQ, hg, head, CH * c:CH * c + CH], start=True, stop=not corner)
                    if corner:
                        m = pe.matmul(ps1[:, u % 2, CH - 19:CH], s.ident[0:19, :], s.corner_q[:, GH * hg + head, :],
                                      start=False, stop=True)
                    m.then_inc(s1_ready, 1)

                def second_scores(sl, hg, qc, kt):
                    for pair in range(2):
                        pe.wait_ge(exp_done, sl * 2 + pair + 1)
                        for e in range(2):
                            head = 2 * pair + e
                            corner = qc == 0 and kt == KT - 1
                            m = pe.matmul(ps2[:, pair, e, :], ks[0:KM, hg, head, 128 * kt:128 * kt + 128],
                                          qs[0:KM, hg, head, CH * qc:CH * qc + CH], start=True, stop=not corner)
                            if corner:
                                m = pe.matmul(ps2[:, pair, e, 0:19], s.shift[:], s.corner_k[:, GH * hg + head, :],
                                              start=False, stop=True)
                        m.then_inc(s2_ready, 1)

                def values(sl, b, hg, qc, kt, half):
                    pe.wait_ge(exp_done, sl * 2 + 4)
                    if kt == 0:
                        pe.wait_ge(o_taken, half)
                    for head in range(GH):
                        m = pe.matmul(psO[32 * head:32 * head + 32, :], v_now[:, kt, GH * hg + head, :],
                                      P[:, kt % 2, head, :], start=(kt == 0), stop=(kt == KT - 1))
                    m.then_inc(pv_done, 1)

                def turn_maxima(use):
                    pe.wait_ge(misc_taken, use)
                    pe.transpose(psM[0:QPART * 32, 0:64].bitcast(BF16), nmp[:].rearrange("p a r -> p (a r)"),
                                 s.ident_bf[:]).then_inc(misc_ready, 1)

                def spread_sums(use, half, hb):
                    pe.wait_ge(o_taken, half + 1)
                    pe.wait_ge(misc_taken, use)
                    pe.matmul(psM[:, :], s.sum_sel[:], o_raw[:, hb, :], start=True, stop=True).then_inc(misc_ready, 1)

                for hg in range(NHG):
                    pe.wait_ge(stack_in[hg], 2 * len(Q_PARTS) * 16)
                for u in range(MAXES):
                    first_scores(u, 0, 0)
                pe.wait_ge(nmp_ready, 1)
                turn_maxima(0)
                for u in range(MAXES // 2):
                    first_scores(u, 1, 1)
                pe.wait_ge(rows_set, 1)
                with pe.Fori(0, NB, 1) as b:
                    late = None
                    for hg in range(NHG):
                        for qc in range(2):
                            half = b * (2 * NHG) + 2 * hg + qc
                            nb, nhg, ni = step_ahead(b, hg, 1 + qc)
                            if qc == 0:
                                pe.wait_ge(nm_in, (b * NHG + (hg + 1)) * 16)
                                pe.wait_ge(v_set, b * NHG + (hg + 1))
                            else:
                                pe.wait_ge(stack_in[nhg], (nb + 1) * (2 * len(Q_PARTS) * 16))
                            for kt in range(KT):
                                sl = half * KT + kt
                                second_scores(sl, hg, qc, kt)
                                for x in range(GH):
                                    u = MAXES // 2 * (1 - qc) + GH * kt + x
                                    first_scores(u, ni, nhg)
                                if late:
                                    values(*late)
                                late = (sl, b, hg, qc, kt, half)
                                if kt == 2 and (hg or qc):
                                    spread_sums(b * MISC + (1 + (3 * hg + 1 if qc else 3 * hg - 1)), half - 1, 1 - qc)
                                if kt == 1 and qc == 1:
                                    pe.wait_ge(nmp_ready, b * NHG + (hg + 2))
                                    turn_maxima(b * MISC + (1 + 3 * hg))
                    values(*late)
                    half = b * (2 * NHG) + 2 * NHG - 1
                    spread_sums(b * MISC + (3 * NHG), half, 1)
                    for x in range(4):
                        f, c = x // 2, x % 2
                        pe.wait_ge(misc_taken, b * MISC + (1 + 3 * NHG + x))
                        pe.wait_ge(on_ready, b * (2 * NHG) + (2 * NHG + 1))
                        for g in range(NHG):
                            m = pe.matmul(psM[0:HC, :], s.w_proj[:, g, HC * f:HC * f + HC], o_n[:, g, CH * c:CH * c + CH],
                                          start=(g == 0), stop=(g == NHG - 1))
                        m.then_inc(misc_ready, 1)

            @block.scalar
            def _(act):
                def read_sums(half, qc):
                    act.wait_ge(pv_done, half * KT + (KT + 1))
                    act.wait_ge(on_ready, half)
                    nc.scalar.copy(o_raw[:, qc, :], psO[:, :]).then_inc(o_taken, 1)

                with act.Fori(0, NB, 1) as b:
                    for hg in range(NHG):
                        for qc in range(2):
                            half = b * (2 * NHG) + (2 * hg + qc)
                            for kt in range(KT):
                                sl = half * KT + kt
                                act.wait_ge(pv_done, sl)
                                for pair in range(2):
                                    act.wait_ge(s2_ready, sl * 2 + (pair + 1))
                                    nc.scalar.activation(P[:, kt % 2, 2 * pair:2 * pair + 2, :], ps2[:, pair, :, :],
                                                         ACT.Exp).then_inc(exp_done, 1)
                                if kt == 0 and (hg or qc):
                                    read_sums(half - 1, 1 - qc)
                    read_sums(b * (2 * NHG) + (2 * NHG - 1), 1)

            @block.vector
            def _(v):
                def tile_max(i, u, slot):
                    v.wait_ge(s1_ready, i * MAXES + (u + 1))
                    v.reduce_max(mx[:, slot, u:u + 1], ps1[:, u % 2, :], AX.X).then_inc(max_done, 1)

                def split_max(i, slot):
                    link = [0]

                    def done(ins):
                        link[0] += 1
                        ins.then_inc(own, 1)
                        v.wait_ge(own, i * OWN + link[0])

                    v.wait_ge(max_done, i * MAXES + (MAXES + 1))
                    done(v.reduce_max(nm[:, 1, :], mx[:, slot, :].rearrange("p (t c) -> p t c", c=2), AX.X))
                    done(v.tensor_scalar(nm[:, 0, :], nm[:, 1, :], -1.0, None, ALU.mult))
                    done(v.tensor_copy(nmp[:, 0, :], nm[:, 0, :]))
                    done(v.tensor_tensor(nm[:, 1, :], nm[:, 0, :], nmp[:, 0, :], ALU.subtract))
                    done(v.tensor_copy(nmp[:, 1, :], nm[:, 1, :]))
                    done(v.tensor_tensor(nmp[:, 2, :], nm[:, 1, :], nmp[:, 1, :], ALU.subtract))
                    v.sem_inc(nmp_ready, 1)

                def take_maxima(use, i):
                    v.wait_ge(misc_ready, use + 1)
                    v.wait_ge(nm_store, i * 16)
                    v.tensor_copy(nmt[:], psM[0:QPART * 32, 0:64].bitcast(BF16)).then_inc(misc_taken, 1)

                def normalise(use, half, hg, qc):
                    v.wait_ge(misc_ready, use + 1)
                    v.reciprocal(rec[:], psM[:, :]).then_inc(misc_taken, 1)
                    v.wait_ge(misc_taken, use + 1)
                    v.tensor_tensor(o_n[:, hg, CH * qc:CH * qc + CH], o_raw[:, qc, :], rec[:], ALU.mult
                                    ).then_inc(on_ready, 1)

                for u in range(MAXES):
                    tile_max(0, u, 0)
                split_max(0, 0)
                take_maxima(0, 0)
                for u in range(MAXES // 2):
                    tile_max(1, u, 1)
                with v.Fori(0, NB, 1) as b:
                    for hg in range(NHG):
                        for qc in range(2):
                            half = b * (2 * NHG) + (2 * hg + qc)
                            nb, nhg, ni = step_ahead(b, hg, 1 + qc)
                            for kt in range(KT):
                                for x in range(GH):
                                    tile_max(ni, MAXES // 2 * (1 - qc) + GH * kt + x, nhg)
                                if kt == 1 and qc == 1:
                                    take_maxima(b * MISC + (1 + 3 * hg), b * NHG + (hg + 1))
                                if kt == 2 and (hg or qc):
                                    normalise(b * MISC + (1 + (3 * hg + 1 if qc else 3 * hg - 1)), half - 1,
                                              hg if qc else hg - 1, 1 - qc)
                            if qc == 0:
                                split_max(ni, nhg)
                    normalise(b * MISC + (3 * NHG), b * (2 * NHG) + (2 * NHG - 1), NHG - 1, 1)
                    for x in range(4):
                        f, c = x // 2, x % 2
                        v.wait_ge(misc_ready, b * MISC + (2 + 3 * NHG + x))
                        y = s.Y[:, b, f, CH * c:CH * c + CH]
                        v.tensor_tensor(y, y, psM[0:HC, :], ALU.add).then_inc(misc_taken, 1)


def experts(nc, w, s):
    with ExitStack() as ctx:
        def sb(name, shape, dt=F32):
            return ctx.enter_context(nc.sbuf_tensor(name, shape, dt))

        def sem(name):
            return ctx.enter_context(nc.semaphore(name))

        TT = NB * L // 128
        CT = CH // 128
        w1 = sb("w1", [HC, EXPERTS, 2, HID])
        w2 = sb("w2", [128, EXPERTS, HT, D])
        b1_rows = sb("b1_rows", [EXPERTS * HT, 128])
        b1 = sb("b1", [128, EXPERTS * HT])
        b2 = sb("b2", [128, EXPERTS, D])
        gate_w = sb("gate_w", [HC, 2, 32])
        gate_b = sb("gate_b", [128, 1])
        logit_t = sb("logit_t", [128, 2, CH])
        pr = sb("pr", [128, TT, EXPERTS])
        tot = sb("tot", [128, TT])
        beats = sb("beats", [128, TT])
        rank = sb("rank", [128, TT, EXPERTS])
        gate = sb("gate", [128, NB, 2, CT, EXPERTS])
        hid = sb("hid", [128, 2, HT, CH])
        acc = sb("acc", [128, 2, CT, D])
        res = sb("res", [HC, 2, 2, CH])
        psH = ctx.enter_context(nc.psum_tensor("psH", [128, 3, CH], F32))
        psE = ctx.enter_context(nc.psum_tensor("psE", [128, 2, CH], F32))
        psT = ctx.enter_context(nc.psum_tensor("psT", [128, 2, CH], F32))
        w1_in = [sem(f"w1_in{e}") for e in range(EXPERTS)]
        w2_in = [sem(f"w2_in{e}") for e in range(EXPERTS)]
        b1_in, b2_in, gw_in, gb_in = sem("b1_in"), sem("b2_in"), sem("gw_in"), sem("gb_in")
        cleared, b1_turned, logits, logits_taken, logits_turned, own, gates_ready = (
            sem("cleared"), sem("b1_turned"), sem("logits"), sem("logits_taken"), sem("logits_turned"), sem("own_ex"),
            sem("gates_ready"))
        exp_ready = sem("exp_ready")
        h_ready = sem("h_ready")
        h_done = sem("h_done")
        e_ready = sem("e_ready")
        e_taken = sem("e_taken")
        acc_set = sem("acc_set")
        turned = sem("turned")
        summed = sem("res_ready")
        stored = [sem(f"res_out{c}") for c in range(2)]

        with nc.Block() as block:
            @block.sync
            def _(sp):
                sp.wait_ge(cleared, 2)
                sp.dma_start(gate_w[:, :, 0:EXPERTS], w.gatew.rearrange("(f p) e -> p f e", p=HC)).then_inc(gw_in, 16)
                for j in range(4):
                    sp.dma_start(gate_b[32 * j:32 * j + EXPERTS, :], w.gateb.rearrange("(e o) -> e o", o=1)).then_inc(gb_in, 16)
                sp.dma_start(b1_rows[:], w.b1.rearrange("e (t p) -> (e t) p", p=128)).then_inc(b1_in, 16)
                for e in range(EXPERTS):
                    sp.dma_start(w1[:, e, :, :], w.w1[e].rearrange("(f p) h -> p f h", p=HC)).then_inc(w1_in[e], 16)
                    sp.dma_start(w2[:, e, :, :], w.w2[e].rearrange("(t p) d -> p t d", p=128)).then_inc(w2_in[e], 16)
                    if e == 0:
                        sp.dma_start(b2[:], w.b2.rearrange("(o e) d -> o e d", o=1).broadcast_to([128, EXPERTS, D])
                                     ).then_inc(b2_in, 16)
                with sp.Fori(0, NB, 1) as b:
                    for c in range(2):
                        sp.wait_ge(summed, b * 2 + (c + 2))
                        sp.dma_start(w.out[b].rearrange("(f p) h w -> p f (h w)", p=HC)[:, :, CH * c:CH * c + CH],
                                     res[:, c, :, :]).then_inc(stored[c], 16)
                for c in range(2):
                    sp.wait_ge(stored[c], 16 * NB)

            @block.gpsimd
            def _(pool):
                pool.memset(gate_w[:], 0.0).then_inc(cleared, 1)
                pool.memset(gate_b[:], 0.0).then_inc(cleared, 1)

            @block.tensor
            def _(pe):
                pe.sem_inc(h_done, 2)
                pe.sem_inc(e_ready, CT)
                pe.sem_inc(e_taken, 1)
                pe.sem_inc(summed, 1)
                pe.wait_ge(b1_in, 16)
                pe.transpose(psE[:, 0, 0:EXPERTS * HT], b1_rows[:], s.ident[0:EXPERTS * HT, 0:EXPERTS * HT]).then_inc(b1_turned, 1)
                pe.wait_ge(gw_in, 16)
                for g in range(2):
                    for f in range(2):
                        for j in range(4):
                            i = 4 * g + j
                            m = pe.matmul(psT[32 * j:32 * j + 32, g, :], gate_w[:, f, :],
                                          s.Z[:, i // 2, f, CH * (i % 2):CH * (i % 2) + CH], start=(f == 0), stop=(f == 1))
                m.then_inc(logits, 1)
                pe.wait_ge(logits_taken, 2)
                for g in range(2):
                    for t in range(CT):
                        m = pe.transpose(psH[:, g, 128 * t:128 * t + 128], logit_t[:, g, 128 * t:128 * t + 128], s.ident[:])
                m.then_inc(logits_turned, 1)
                for e in range(EXPERTS):
                    pe.wait_ge(w1_in[e], 16)
                    pe.wait_ge(w2_in[e], 16)
                pe.wait_ge(gates_ready, 1)

                def hidden(b, c, e, n):
                    for t in range(HT):
                        pe.wait_ge(h_done, n * HT + t)
                        for f in range(2):
                            m = pe.matmul(psH[:, t % 3, :], w1[:, e, f, 128 * t:128 * t + 128],
                                          s.Z[:, b, f, CH * c:CH * c + CH], start=(f == 0), stop=(f == 1))
                        m.then_inc(h_ready, 1)

                def outputs(e, n):
                    pe.wait_ge(h_done, n * HT + (HT + 2))
                    for tt in range(CT):
                        pe.wait_ge(e_taken, n * CT + tt)
                        for t in range(HT):
                            m = pe.matmul(psE[:, tt % 2, 0:D], hid[:, e % 2, t, 128 * tt:128 * tt + 128], w2[:, e, t, :],
                                          start=(t == 0), stop=(t == HT - 1))
                        m.then_inc(e_ready, 1)

                def turn_back(b, c, n):
                    pe.wait_ge(e_taken, n * CT + (CT + 1))
                    pe.wait_ge(summed, b * 2 + (c + 1))
                    for f in range(2):
                        for tt in range(CT):
                            m = pe.transpose(psT[0:HC, f, 128 * tt:128 * tt + 128], acc[:, c, tt, HC * f:HC * f + HC], s.ident[:])
                    m.then_inc(turned, 1)

                with pe.Fori(0, NB, 1) as b:
                    hidden(b, 0, 0, b * (2 * EXPERTS))
                    for c in range(2):
                        for e in range(EXPERTS):
                            n = b * (2 * EXPERTS) + (c * EXPERTS + e)
                            if e + 1 < EXPERTS:
                                hidden(b, c, e + 1, n + 1)
                            elif c == 0:
                                hidden(b, 1, 0, n + 1)
                            outputs(e, n)
                        turn_back(b, c, n)

            @block.scalar
            def _(act):
                act.wait_ge(own, 2)
                nc.scalar.activation(pr[:], pr[:], ACT.Exp).then_inc(exp_ready, 1)
                with act.Fori(0, NB, 1) as b:
                    for c in range(2):
                        for e in range(EXPERTS):
                            n = b * (2 * EXPERTS) + (c * EXPERTS + e)
                            act.wait_ge(b1_turned, 2)
                            for t in range(HT):
                                act.wait_ge(h_ready, n * HT + (t + 1))
                                if t == 0:
                                    act.wait_ge(e_ready, n * CT)
                                nc.scalar.activation(hid[:, e % 2, t, :], psH[:, t % 3, :], ACT.Gelu,
                                                     bias=b1[:, HT * e + t:HT * e + t + 1]).then_inc(h_done, 1)

            @block.vector
            def _(v):
                chain = Own(v, own)

                def step(ins):
                    chain(ins)
                    chain.wait()

                v.wait_ge(b1_turned, 1)
                v.tensor_copy(b1[:], psE[:, 0, 0:EXPERTS * HT]).then_inc(b1_turned, 1)
                v.wait_ge(logits, 1)
                v.wait_ge(gb_in, 64)
                for g in range(2):
                    v.tensor_scalar(logit_t[:, g, :], psT[:, g, :], gate_b[:, 0:1], None, ALU.add).then_inc(logits_taken, 1)
                v.wait_ge(logits_turned, 1)
                for g in range(2):
                    for t in range(CT):
                        m = v.tensor_copy(pr[:, 16 * g + t:16 * g + 16:CT, :],
                                          psH[:, g, 128 * t:128 * t + 128].rearrange("p (j e) -> p j e", e=32)[:, :, 0:EXPERTS])
                m.then_inc(gates_ready, 1)
                v.wait_ge(gates_ready, 1)
                step(v.reduce_max(tot[:], pr[:], AX.X))
                step(v.tensor_tensor(pr[:], pr[:], tot[:].unsqueeze(2).broadcast_to([128, TT, EXPERTS]), ALU.subtract))
                v.wait_ge(exp_ready, 1)
                step(v.reduce_sum(tot[:], pr[:], AX.X))
                step(v.reciprocal(tot[:], tot[:]))
                step(v.tensor_tensor(pr[:], pr[:], tot[:].unsqueeze(2).broadcast_to([128, TT, EXPERTS]), ALU.mult))
                step(v.memset(rank[:], 0.0))
                for lo in range(EXPERTS):
                    for hi in range(lo + 1, EXPERTS):
                        step(v.tensor_tensor(beats[:], pr[:, :, lo], pr[:, :, hi], ALU.is_ge))
                        step(v.tensor_tensor(rank[:, :, hi], rank[:, :, hi], beats[:], ALU.add))
                        step(v.tensor_scalar(beats[:], beats[:], -1.0, 1.0, ALU.mult, ALU.add))
                        step(v.tensor_tensor(rank[:, :, lo], rank[:, :, lo], beats[:], ALU.add))
                step(v.tensor_scalar(rank[:], rank[:], 1.5, None, ALU.is_le))
                step(v.tensor_tensor(pr[:], pr[:], rank[:], ALU.mult))
                step(v.reduce_sum(tot[:], pr[:], AX.X))
                step(v.tensor_scalar(tot[:], tot[:], 1e-9, None, ALU.add))
                step(v.reciprocal(tot[:], tot[:]))
                step(v.tensor_tensor(gate[:].rearrange("p b c t e -> p (b c t) e"), pr[:],
                                     tot[:].unsqueeze(2).broadcast_to([128, TT, EXPERTS]), ALU.mult))
                v.wait_ge(b2_in, 16)
                with v.Fori(0, NB, 1) as b:
                    for c in range(2):
                        for e in range(EXPERTS):
                            n = b * (2 * EXPERTS) + (c * EXPERTS + e)
                            for tt in range(CT):
                                g = gate[:, b, c, tt, e:e + 1]
                                a = acc[:, c, tt, :]
                                if e == 0:
                                    v.tensor_scalar(a, b2[:, 0, :], g, None, ALU.mult).then_inc(acc_set, 1)
                                    for x in range(1, EXPERTS):
                                        v.wait_ge(acc_set, (b * 2 + c) * (CT * EXPERTS) + (tt * EXPERTS + x))
                                        v.scalar_tensor_tensor(out=a, in0=b2[:, x, :], scalar=gate[:, b, c, tt, x:x + 1],
                                                               in1=a, op0=ALU.mult, op1=ALU.add).then_inc(acc_set, 1)
                                    v.wait_ge(acc_set, (b * 2 + c) * (CT * EXPERTS) + (tt * EXPERTS + EXPERTS))
                                else:
                                    v.wait_ge(e_taken, n * CT + (tt - CT + 2))
                                v.wait_ge(e_ready, n * CT + (CT + tt + 1))
                                v.scalar_tensor_tensor(out=a, in0=psE[:, tt % 2, 0:D], scalar=g, in1=a,
                                                       op0=ALU.mult, op1=ALU.add).then_inc(e_taken, 1)
                        v.wait_ge(turned, b * 2 + (c + 1))
                        v.wait_ge(stored[c], b * 16)
                        v.tensor_tensor(res[:, c, :, :], psT[0:HC, :, :], s.Y[:, b, :, CH * c:CH * c + CH], ALU.add
                                        ).then_inc(summed, 1)


class Views:
    pass


def program(nc, ins, out):
    w = Views()
    (w.x, w.wx, w.wdt, w.dtb, w.alog, w.ds, w.lnw, w.lnb, w.qkvw, w.qkvb, w.projw, w.projb, w.table,
     w.gatew, w.gateb, w.w1, w.b1, w.w2, w.b2) = ins
    w.out = out
    with ExitStack() as ctx:
        def sb(name, shape, dt=F32):
            return ctx.enter_context(nc.sbuf_tensor(name, shape, dt))

        s = Views()
        s.Y = sb("Y", [HC, NB, 2, L])
        s.cols = sb("cols", [HC, NCOL])
        s.ident = sb("ident", [128, 128])
        s.ident_bf = sb("ident_bf", [128, 128], BF16)
        s.average = sb("average", [HC, HC])
        s.sum_sel = sb("sum_sel", [128, 128])
        s.one = sb("one", [128, 1])
        s.eps5 = sb("eps5", [128, 1])
        s.qk_dram = nc.dram_tensor("qk_parts", (NB, 2, QPART, D, L), BF16, kind="Internal").ap()
        s.nm_dram = nc.dram_tensor("max_parts", (QPART * 32, 128), BF16, kind="Internal").ap()
        s.ext = nc.dram_tensor("table_twice", (37, HEADS), F32, kind="Internal").ap()
        with ExitStack() as c2:
            def sb2(name, shape, dt=F32):
                return c2.enter_context(nc.sbuf_tensor(name, shape, dt))
            s.X = sb2("X", [HC, NB + 1, 2, L])
            s.d_sum = sb2("d_sum", [HC, 2])
            s.w_b = sb2("w_b", [HC, K, 2, 128])
            s.w_c = sb2("w_c", [HC, K, 2, 128])
            s.w_dt = sb2("w_dt", [HC, K, 2, D])
            s.a_neg = sb2("a_neg", [128, HC])
            s.spread_sel = sb2("spread_sel", [HC, SUB, 128], BF16)
            s.state_sel = sb2("state_sel", [128, SUB, BLK])
            prepare(nc, w, s)
            scan(nc, w, s)
        with ExitStack() as c2:
            s.Z = c2.enter_context(nc.sbuf_tensor("Z", [HC, NB, 2, L], F32))
            with nc.sbuf_tensor("raw", [HC, NB, 2, L], F32) as raw:
                s.raw = raw
                conv_out(nc, w, s)
        with ExitStack() as c2:
            def sb2(name, shape, dt=F32):
                return c2.enter_context(nc.sbuf_tensor(name, shape, dt))
            s.w_proj = sb2("w_proj", [128, 3, D])
            s.corner_q = sb2("corner_q", [19, HEADS, 19])
            s.corner_k = sb2("corner_k", [19, HEADS, 19])
            s.shift = sb2("shift", [19, 128])
            s.V = sb2("V", [128, NB, 8, HEADS, 32])
            with nc.sbuf_tensor("Zq", [HC, NB, 2, L], F32) as z:
                s.Z = z
                layer_norm(nc, s, s.Y, s.Z, "la_")
                qkv(nc, w, s)
            attention(nc, w, s)
        with nc.sbuf_tensor("Zf", [HC, NB, 2, L], F32) as z:
            s.Z = z
            layer_norm(nc, s, s.Y, s.Z, "lf_")
            experts(nc, w, s)


_INS = ["x", "L0_conv_x_proj_weight", "L0_conv_dt_projs_weight", "L0_conv_dt_projs_bias", "L0_conv_A_logs",
        "L0_conv_Ds", "L0_conv_ln_weight", "L0_conv_ln_bias", "L1_attn_qkv_w", "L1_attn_qkv_b", "L1_attn_proj_w",
        "L1_attn_proj_b", "L1_attn_bias_table", "L1_ffn_gate_w", "L1_ffn_gate_b", "L1_ffn_w1", "L1_ffn_b1",
        "L1_ffn_w2", "L1_ffn_b2"]
_OUT = ((NB, D, HH, WW), "float32")


def kernel(**inputs):
    import numpy as _np
    import concourse.bacc as _bacc
    from concourse import mybir as _mybir
    from concourse.bass_utils import run_bass_kernel_spmd as _run

    nc = _bacc.Bacc("TRN2", target_bir_lowering=False, num_devices=1)
    arrays, args = {}, []
    for name in _INS:
        a = _np.ascontiguousarray(inputs[name])
        arrays[f"in_{name}_dram"] = a
        args.append(nc.dram_tensor(f"in_{name}_dram", a.shape, _mybir.dt.from_np(a.dtype), kind="ExternalInput").ap())
    shape, dtype = _OUT
    out = nc.dram_tensor("out_dram", shape, _mybir.dt.from_np(_np.dtype(dtype)), kind="ExternalOutput").ap()
    program(nc, args, out)
    r = _run(nc, [arrays], core_ids=[0])
    return r.results[0]["out_dram"]
```

```python
from contextlib import ExitStack

import concourse.bass as bass
from concourse import mybir

F32 = mybir.dt.float32
BF16 = mybir.dt.bfloat16
ALU = mybir.AluOpType
ACT = mybir.ActivationFunctionType
AX = mybir.AxisListType

NB = 4
D = 192
HC = 96
HH = WW = 32
L = HH * WW
CH = 512
K = 4
N = 16
R = 6
GN_CH = 6
DD = 8
BLK = 32
NBLK = HC // BLK
SUB = BLK // DD
TILES = HC // DD
UNITS = 2 * K
HEADS = 12
DH = 16
QPART = 3
EXPERTS = 4
HID = 768
HT = HID // 128
START = 1

COL_DTB, COL_DS, COL_LNW, COL_LNB, COL_Q, COL_K, COL_PB = 0, 8, 16, 18, 20, 22, 24
NCOL = 26


class Own:

    def __init__(self, eng, sem):
        self.eng, self.sem, self.n = eng, sem, 0

    def __call__(self, ins):
        ins.then_inc(self.sem, 1)
        self.n += 1
        return ins

    def wait(self):
        self.eng.wait_ge(self.sem, self.n)


def prepare(nc, w, s):
    with ExitStack() as ctx:
        def sb(name, shape, dt=F32):
            return ctx.enter_context(nc.sbuf_tensor(name, shape, dt))

        def sem(name):
            return ctx.enter_context(nc.semaphore(name))

        rows = sb("rows", [NCOL, HC])
        a_rows = sb("a_rows", [HC, 128])
        wx = sb("wx", [R + 2 * N, K, D])
        wdt_rows = sb("wdt_rows", [HC, 2 * K, R])
        wdt = sb("wdt", [R, K, D])
        group = sb("group", [HC, HC])
        stats = sb("stats", [HC, 2 * NB, 2, 6])
        mv = sb("mv", [HC, 2 * NB, 2])
        mean = sb("mean", [HC, 2 * NB])
        spread = sb("spread", [HC, 2 * NB])
        rstd = sb("rstd", [HC, 2 * NB])
        a_exp = sb("a_exp", [128, HC])
        ps = ctx.enter_context(nc.psum_tensor("ps_prep", [128, 8, CH], F32))
        x_in = [sem(f"x_in{b}") for b in range(NB)]
        rows_in, wx_in, wdt_in, a_in = sem("rows_in"), sem("wx_in"), sem("wdt_in"), sem("a_in")
        masks, pe_small, pe_wx, pe_wdt, pe_mean, pe_var = (
            sem("masks"), sem("pe_small"), sem("pe_wx"), sem("pe_wdt"), sem("pe_mean"), sem("pe_var"))
        a_turned = sem("a_turned")
        wdt_turned = sem("wdt_turned")
        dve, aexp, std, gp, mean_in, var_in = sem("dve_prep"), sem("aexp"), sem("std"), sem("gp_prep"), sem("mean_in"), sem("var_in")

        with nc.Block() as block:
            @block.sync
            def _(sp):
                for b in range(NB):
                    sp.dma_start(s.X[:, b, :, :], w.x[b].rearrange("(f p) h w -> p f (h w)", p=HC)).then_inc(x_in[b], 16)

            @block.scalar
            def _(act):
                vec = [(COL_DTB, w.dtb.rearrange("k (f p) -> (k f) p", p=HC), 8),
                       (COL_DS, w.ds.rearrange("(k p) -> k p", p=HC), 8),
                       (COL_LNW, w.lnw.rearrange("(f p) -> f p", p=HC), 2),
                       (COL_LNB, w.lnb.rearrange("(f p) -> f p", p=HC), 2),
                       (COL_Q, w.qkvb[0:2 * D].rearrange("(f p) -> f p", p=HC), 4),
                       (COL_PB, w.projb.rearrange("(f p) -> f p", p=HC), 2)]
                for at, src, n in vec:
                    act.dma_start(rows[at:at + n, :], src).then_inc(rows_in, 16)
                act.dma_start(wx[:], w.wx.rearrange("k c d -> c k d")).then_inc(wx_in, 16)
                act.dma_start(a_rows[:], w.alog.rearrange("(g d) n -> g (d n)", d=DD)).then_inc(a_in, 16)
                act.dma_start(wdt_rows[:], w.wdt.rearrange("k (f p) r -> p (k f) r", p=HC)).then_inc(wdt_in, 16)
                act.wait_ge(a_turned, 1)
                nc.scalar.activation(a_exp[:], a_exp[:], ACT.Exp).then_inc(aexp, 1)
                act.wait_ge(pe_var, 1)
                act.wait_ge(gp, 1)
                nc.scalar.activation(spread[:], ps[0:HC, 1, 336:344], ACT.Sqrt, bias=s.eps5[0:HC, :]).then_inc(std, 1)

            @block.gpsimd
            def _(pool):
                pool.memset(s.eps5[:], 1e-5).then_inc(gp, 1)
                own = 1
                made = 0

                def step(ins):
                    nonlocal own
                    own += 1
                    ins.then_inc(gp, 1)
                    pool.wait_ge(gp, own)

                pool.memset(s.Y[:, NB - 1, 1, :], 0.0)
                step(pool.memset(s.ident[:], 0.0))
                step(pool.affine_select(out=s.ident[:], in_=s.ident[:], compare_op=ALU.not_equal, fill=1.0,
                                        base=0, pattern=[[-1, 128]], channel_multiplier=1))
                pool.memset(s.one[:], 1.0).then_inc(masks, 1)
                pool.memset(s.average[:], 1.0 / D)
                step(pool.memset(s.ident_bf[:], 0.0))
                step(pool.affine_select(out=s.ident_bf[:], in_=s.ident_bf[:], compare_op=ALU.not_equal, fill=1.0,
                                        base=0, pattern=[[-1, 128]], channel_multiplier=1))
                step(pool.memset(s.sum_sel[:], 0.0))
                sel = s.sum_sel[:].rearrange("p (h c) -> p h c", c=32)
                step(pool.affine_select(out=sel, in_=sel, compare_op=ALU.not_equal, fill=1.0, base=-DH,
                                        pattern=[[-32, 4], [0, 32]], channel_multiplier=1))
                step(pool.memset(group[:], 1.0 / GN_CH))
                g3 = group[:].rearrange("p (g e) -> p g e", e=GN_CH)
                step(pool.affine_select(out=g3, in_=g3, compare_op=ALU.is_ge, fill=0.0, base=0,
                                        pattern=[[-GN_CH, HC // GN_CH], [0, GN_CH]], channel_multiplier=1))
                pool.affine_select(out=g3, in_=g3, compare_op=ALU.is_ge, fill=0.0, base=GN_CH - 1,
                                   pattern=[[GN_CH, HC // GN_CH], [0, GN_CH]], channel_multiplier=-1).then_inc(masks, 1)
                step(pool.memset(s.spread_sel[:], 0.0))
                v = s.spread_sel[:].rearrange("p s (d n) -> p s d n", d=DD)
                for part in range(QPART):
                    step(pool.affine_select(out=v, in_=v, compare_op=ALU.not_equal, fill=1.0, base=-BLK * part,
                                            pattern=[[-DD, SUB], [-1, DD], [0, N]], channel_multiplier=1))
                step(pool.memset(s.state_sel[:], 1.0))
                step(pool.affine_select(out=s.state_sel[:], in_=s.state_sel[:], compare_op=ALU.is_ge, fill=0.0, base=0,
                                        pattern=[[N * DD, SUB], [-N, BLK]], channel_multiplier=1))
                pool.affine_select(out=s.state_sel[:], in_=s.state_sel[:], compare_op=ALU.is_ge, fill=0.0, base=N - 1,
                                   pattern=[[-N * DD, SUB], [N, BLK]], channel_multiplier=-1).then_inc(masks, 1)

            @block.tensor
            def _(pe):
                pe.wait_ge(gp, 3)
                pe.wait_ge(rows_in, 6 * 16)
                pe.transpose(ps[0:HC, 0, 0:NCOL], rows[:], s.ident[0:NCOL, 0:NCOL]).then_inc(pe_small, 1)
                pe.wait_ge(a_in, 16)
                pe.transpose(ps[:, 0, 32:32 + HC], a_rows[:], s.ident[0:HC, 0:HC]).then_inc(pe_small, 1)
                pe.wait_ge(wx_in, 16)
                for k in range(K):
                    for f in range(2):
                        q = 2 * k + f
                        m = pe.transpose(ps[0:HC, 1, 38 * q:38 * q + 38], wx[:, k, HC * f:HC * f + HC],
                                         s.ident[0:38, 0:38])
                m.then_inc(pe_wx, 1)
                pe.wait_ge(wdt_in, 16)
                for q in range(2 * K):
                    bank, at = 6 + q // K, 0
                    m = pe.transpose(ps[0:R, bank, at + HC * (q % K):at + HC * (q % K) + HC], wdt_rows[:, q, :],
                                     s.ident[0:HC, 0:HC])
                m.then_inc(pe_wdt, 1)
                pe.wait_ge(wdt_turned, 1)
                for k in range(K):
                    for f in range(2):
                        m = pe.matmul(ps[0:HC, 2 + k, D * f:D * f + D], wx[0:R, k, HC * f:HC * f + HC],
                                      wdt[:, k, :], start=True, stop=True)
                m.then_inc(pe_wdt, 1)
                pe.wait_ge(masks, 2)
                pe.wait_ge(mean_in, 1)
                pe.matmul(ps[0:HC, 1, 320:328], group[:], mean[:], start=True, stop=True).then_inc(pe_mean, 1)
                pe.wait_ge(var_in, 1)
                pe.matmul(ps[0:HC, 1, 336:344], group[:], spread[:], start=True, stop=True).then_inc(pe_var, 1)

            @block.vector
            def _(v):
                own = Own(v, dve)
                for b in range(NB):
                    v.wait_ge(x_in[b], 16)
                    for f in range(2):
                        for c in range(2):
                            own(v.bn_stats(stats[:, 2 * b + f, c, :], s.X[:, b, f, CH * c:CH * c + CH]))
                own.wait()
                for q in range(2 * NB):
                    own(v.bn_aggr(mv[:, q, :], stats[:, q, :, :].rearrange("p c s -> p (c s)")))
                own.wait()
                v.tensor_copy(mean[:], mv[:, :, 0]).then_inc(mean_in, 1)
                v.wait_ge(pe_small, 2)
                v.tensor_copy(a_exp[:], ps[:, 0, 32:32 + HC]).then_inc(a_turned, 1)
                own(v.tensor_copy(s.cols[:], ps[0:HC, 0, 0:NCOL]))
                v.wait_ge(pe_wdt, 1)
                v.tensor_copy(wdt[:, 0:2, :], ps[0:R, 6, 0:4 * HC].rearrange("p (k d) -> p k d", k=2))
                v.tensor_copy(wdt[:, 2:4, :], ps[0:R, 7, 0:4 * HC].rearrange("p (k d) -> p k d", k=2)
                              ).then_inc(wdt_turned, 1)
                v.wait_ge(pe_mean, 1)
                own(v.tensor_tensor(spread[:], mv[:, :, 0], ps[0:HC, 1, 320:328], ALU.subtract))
                own(v.tensor_copy(mean[:], ps[0:HC, 1, 320:328]))
                own.wait()
                own(v.tensor_tensor(spread[:], spread[:], spread[:], ALU.mult))
                own.wait()
                v.tensor_tensor(spread[:], spread[:], mv[:, :, 1], ALU.add).then_inc(var_in, 1)
                v.wait_ge(std, 1)
                own(v.reciprocal(rstd[:], spread[:]))
                own.wait()
                for q in range(2 * NB):
                    own(v.tensor_scalar(s.X[:, q // 2, q % 2, :], s.X[:, q // 2, q % 2, :], mean[:, q:q + 1],
                                        rstd[:, q:q + 1], ALU.subtract, ALU.mult))
                own(v.memset(s.X[:, NB, :, :], 0.0))
                v.wait_ge(pe_wx, 1)
                for k in range(K):
                    for f in range(2):
                        q = 2 * k + f
                        for i, dst in ((0, s.w_b), (1, s.w_c)):
                            src = ps[0:HC, 1, 38 * q + R + N * i:38 * q + R + N * i + N]
                            own(v.tensor_copy(dst[:, k, f, :].rearrange("p (d n) -> p d n", d=DD),
                                              src.unsqueeze(1).broadcast_to([HC, DD, N])))
                v.wait_ge(pe_wdt, 2)
                for k in range(K):
                    own(v.tensor_copy(s.w_dt[:, k, :, :], ps[0:HC, 2 + k, 0:2 * D].rearrange("p (f d) -> p f d", f=2)))
                v.wait_ge(aexp, 1)
                own(v.tensor_scalar(s.a_neg[:], a_exp[:], -1.0, None, ALU.mult))
                own.wait()
                own(v.tensor_reduce(s.d_sum[:], s.cols[:, COL_DS:COL_DS + 8].rearrange("p (k f) -> p f k", f=2),
                                    AX.X, ALU.add))
                own.wait()


def scan(nc, w, s):
    with ExitStack() as ctx:
        def sb(name, shape, dt=F32):
            return ctx.enter_context(nc.sbuf_tensor(name, shape, dt))

        def sem(name):
            return ctx.enter_context(nc.semaphore(name))

        xt = sb("xt", [HC, 2, L])
        bc = sb("bc", [128, 2, 2, L])
        z_sb = sb("z_sb", [HC, L])
        sp_e = sb("sp_e", [HC, L])
        dt = sb("dt", [HC, 2, L])
        rest = sb("rest", [HC, 2, L])
        parts = sb("parts", [HC, 2, QPART, L], BF16)
        stack = sb("stack", [HC, 2, 2, NBLK, L], BF16)
        dbu = sb("dbu", [128, 3, CH])
        HR = 6
        hs = sb("hs", [128, HR, L])
        AR = 3
        psA = ctx.enter_context(nc.psum_tensor("psA", [128, AR, CH], F32))
        psU = ctx.enter_context(nc.psum_tensor("psU", [128, 2, CH], F32))
        psY = ctx.enter_context(nc.psum_tensor("psY", [128, 2, CH], F32))
        psP = ctx.enter_context(nc.psum_tensor("psP", [128, CH], F32))

        dt_spread = sem("dt_spread")
        dtu_spread = sem("dtu_spread")
        decay_ready = sem("decay_ready")
        dbu_ready = sem("dbu_ready")
        scan_done = sem("scan_done")
        hc_ready = sem("hc_ready")
        summed = sem("summed")
        y_taken = sem("y_taken")
        z_proj = sem("z_proj")
        bc_proj = sem("bc_proj")
        z_taken = sem("z_taken")
        clipped = sem("clipped")
        log_ready = sem("log_ready")
        exp_own = sem("exp_own")
        dt_own = sem("dt_own")
        dt_ready = sem("dt_ready")
        bc_ready = sem("bc_ready")
        hi_ready = sem("hi_ready")
        rest_ready = sem("rest_ready")
        mid_ready = sem("mid_ready")
        lo_ready = sem("lo_ready")
        xt_half = sem("xt_half")
        stacked = [sem(f"stacked{p}") for p in range(2)]

        def order(ui):
            p, r, f = ui // 4, ui // 2 % 2, ui % 2
            return p, r, f, p + 2 * r

        SP_LIMIT = 40.0

        def landed(b, ui):
            return (b * (UNITS // 2) + ui // 2 + 1) * (16 * QPART * NBLK)

        Z_PE = {12: (0, 0), 13: (0, 1), 15: (1, 0), 16: (1, 1)}
        BC_PE = {3 * (i // 2) + i % 2: (i // 2, i % 2) for i in range(8)}

        def source(nb, nu):
            p, r, f, k = order(nu)
            return (lambda h, lo: xt[:, h, lo:lo + CH]) if p else (lambda h, lo: s.X[:, nb, h, lo:lo + CH])

        def units_ahead(b, ui, d):
            return b + (ui + d) // UNITS, (ui + d) % UNITS, b * UNITS + (ui + d)

        with nc.Block() as block:
            @block.tensor
            def _(pe):
                pe.sem_inc(dbu_ready, 2)
                pe.sem_inc(scan_done, 2 + START)
                pe.sem_inc(summed, 1 + START + (SUB - 2))
                for first in (y_taken, hc_ready, dt_spread, dt_ready):
                    pe.sem_inc(first, START)

                def project(out, wt, rhs, h, ready):
                    m = pe.matmul(out, wt, rhs, start=(h == 0), stop=(h == 1))
                    if h == 1:
                        m.then_inc(ready, 1)

                def z_side(q, nb, nu, n1, kk):
                    if q not in Z_PE:
                        return
                    c, h = Z_PE[q]
                    p, r, f, k = order(nu)
                    if h == 0:
                        if c:
                            pe.wait_ge(z_taken, n1 * 2 + 1)
                        elif kk is not None:
                            pe.wait_ge(bc_ready, kk * 4 + 4)
                        elif not isinstance(n1, int):
                            pe.wait_ge(z_taken, n1 * 2)
                        if p:
                            pe.wait_ge(xt_half, nb * 2 + 2)
                    project(psP[0:HC, :], s.w_dt[:, k, h, HC * f:HC * f + HC], source(nb, nu)(h, CH * c), h, z_proj)

                def bc_side(q, nb, nu, n1, kk):
                    if q not in BC_PE:
                        return
                    i, h = BC_PE[q]
                    p, r, f, k = order(nu)
                    if h == 0:
                        if i:
                            pe.wait_ge(bc_ready, kk * 4 + i)
                        else:
                            pe.wait_ge(z_taken, n1 * 2 + 2)
                        if p:
                            pe.wait_ge(xt_half, nb * 2 + 2)
                    project(psP[:, :], (s.w_b, s.w_c)[i // 2][:, k, h, :], source(nb, nu)(h, CH * (i % 2)), h, bc_proj)

                def sum_states(n, trip, c, first=0):
                    if c == 0:
                        if trip == 0:
                            pe.wait_ge(y_taken, n + (1 + START))
                        pe.wait_ge(hc_ready, n * TILES + (TILES + 3 * trip + 3 + START))
                    for j in range(NBLK):
                        slot = (3 * trip + j) % HR
                        m = pe.matmul(psY[BLK * j:BLK * j + BLK, c, :], s.state_sel[:, trip, :],
                                      hs[:, slot, CH * c:CH * c + CH], start=(trip == first), stop=(trip == SUB - 1))
                    if c == 1:
                        m.then_inc(summed, 1)

                for q in Z_PE:
                    z_side(q, 0, 0, 0, None)
                for q in BC_PE:
                    bc_side(q, 0, 0, 0, 0)
                for q in Z_PE:
                    z_side(q, 0, 1, 1, 0)
                for c in range(2):
                    sum_states(-1, SUB - 2, c, first=SUB - 2)
                with pe.Fori(0, NB, 1) as b:
                    for ui in range(UNITS):
                        n = b * UNITS + ui
                        p, r, f, k = order(ui)
                        pe.wait_ge(stacked[ui % 2], landed(b, ui))
                        for t in range(TILES):
                            gg, j = t // NBLK, t % NBLK
                            for c in range(2):
                                q = 2 * t + c
                                pos = c if r == 0 else 1 - c
                                g = n * (2 * TILES) + q
                                pe.wait_ge(dbu_ready, g + 1)
                                pe.matmul(psU[:, q % 2, :], s.spread_sel[:, gg, :],
                                          stack[:, ui % 2, 1, j, CH * pos:CH * pos + CH],
                                          start=True, stop=True).then_inc(dtu_spread, 1)
                                pe.wait_ge(scan_done, g + START)
                                pe.matmul(psA[:, q % AR, :], s.spread_sel[:, gg, :],
                                          stack[:, ui % 2, 0, j, CH * pos:CH * pos + CH],
                                          start=True, stop=True).then_inc(dt_spread, 1)
                                if ui % 2:
                                    bc_side(q, *units_ahead(b, ui, 1), b * K + (ui + 1) // 2)
                                z_side(q, *units_ahead(b, ui, 2), b * K + (ui + 1) // 2 if ui % 2 else None)
                                if t % 3 == 2:
                                    if t > 3:
                                        sum_states(n, t // 3 - 1, c)
                                    else:
                                        sum_states(n - 1, SUB - 1, c)
                for c in range(2):
                    sum_states(NB * UNITS - 1, SUB - 1, c)

            @block.scalar
            def _(act):
                def z_side(q, nb, nu, n1):
                    p, r, f, k = order(nu)
                    if q in (14, 17):
                        c = (q - 14) // 3
                        act.wait_ge(z_proj, n1 * 2 + c + 1)
                        act.wait_ge(dt_own, n1 * 2)
                        nc.scalar.activation(z_sb[:, CH * c:CH * c + CH], psP[0:HC, :], ACT.Identity,
                                             bias=s.cols[:, COL_DTB + 2 * k + f:COL_DTB + 2 * k + f + 1]
                                             ).then_inc(z_taken, 1)
                    if q in (17, 20):
                        c = (q - 17) // 3
                        act.wait_ge(clipped, n1 * 2 + c + 1)
                        e = sp_e[:, CH * c:CH * c + CH]
                        nc.scalar.activation(e, e, ACT.Exp).then_inc(exp_own, 1)
                        act.wait_ge(exp_own, n1 * 2 + c + 1)
                        nc.scalar.activation(e, e, ACT.Ln, bias=s.one[0:HC, :]).then_inc(log_ready, 1)

                def bc_side(q, nu, kk):
                    if q in (2, 5, 8, 11):
                        i = q // 3
                        act.wait_ge(bc_proj, kk * 4 + i + 1)
                        if i == 0 and not isinstance(kk, int):
                            act.wait_ge(hc_ready, (kk - 1) * (2 * TILES) + (TILES + START))
                        nc.scalar.copy(bc[:, nu // 2 % 2, i // 2, CH * (i % 2):CH * (i % 2) + CH],
                                       psP[:, :]).then_inc(bc_ready, 1)

                def split_side(q, n1, b, ui):
                    if q == 0:
                        act.wait_ge(dt_ready, n1 * 2 + 2 + START)
                        if ui is not None:
                            act.wait_ge(stacked[ui % 2], landed(b, ui))
                        for tq in range(2):
                            nc.scalar.copy(parts[:, tq, 0, :], dt[:, tq, :]).then_inc(hi_ready, 1)
                    if q in (6, 10):
                        tq = (q - 6) // 4
                        act.wait_ge(rest_ready, n1 * 2 + tq + 1)
                        nc.scalar.copy(parts[:, tq, 1, :], rest[:, tq, :]).then_inc(mid_ready, 1)

                nc.scalar.preload_act_table_set("natural_log_exp_and_others")
                for q in (14, 17, 20):
                    z_side(q, 0, 0, 0)
                for q in (2, 5, 8, 11):
                    bc_side(q, 0, 0)
                for q in (0, 6, 10):
                    split_side(q, 0, 0, None)
                for q in (14, 17, 20):
                    z_side(q, 0, 1, 1)
                with act.Fori(0, NB, 1) as b:
                    for ui in range(UNITS):
                        n = b * UNITS + ui
                        p, r, f, k = order(ui)
                        for t in range(TILES):
                            gg, j = t // NBLK, t % NBLK
                            col = k * (D // DD) + TILES * f + SUB * j + gg
                            for c in range(2):
                                q = 2 * t + c
                                g = n * (2 * TILES) + q
                                act.wait_ge(dt_spread, g + 1 + START)
                                nc.scalar.activation(psA[:, q % AR, :], psA[:, q % AR, :], ACT.Exp,
                                                     scale=s.a_neg[:, col:col + 1]).then_inc(decay_ready, 1)
                                if ui % 2:
                                    bc_side(q, (ui + 1) % UNITS, b * K + (ui + 1) // 2)
                                split_side(q, n + 1, b, ui)
                                z_side(q, *units_ahead(b, ui, 2))
                                if ui == 1 and q in (21, 22):
                                    h = q - 21
                                    act.wait_ge(dt_ready, b * (2 * UNITS) + START)
                                    nc.scalar.copy(xt[:, h, :].rearrange("p (w h) -> p w h", w=WW),
                                                   s.X[:, b, h, :].rearrange("p (h w) -> p w h", h=HH)
                                                   ).then_inc(xt_half, 1)

            @block.gpsimd
            def _(pool):
                def split_side(t, n1):
                    for tq in range(2):
                        if t == 2 * tq:
                            pool.wait_ge(hi_ready, n1 * 2 + tq + 1)
                            pool.wait_ge(mid_ready, n1 * 2)
                            pool.tensor_tensor(rest[:, tq, :], dt[:, tq, :], parts[:, tq, 0, :],
                                               ALU.subtract).then_inc(rest_ready, 1)
                        if t == 5 + 3 * tq:
                            pool.wait_ge(mid_ready, n1 * 2 + tq + 1)
                            pool.tensor_tensor(parts[:, tq, 2, :], rest[:, tq, :], parts[:, tq, 1, :],
                                               ALU.subtract).then_inc(lo_ready, 1)

                pool.memset(hs[:], 0.0).then_inc(hc_ready, TILES)
                for t in (0, 2, 5, 8):
                    split_side(t, 0)
                with pool.Fori(0, NB, 1) as b:
                    for ui in range(UNITS):
                        n = b * UNITS + ui
                        kslot = ui // 2 % 2
                        pool.wait_ge(bc_ready, (b * K + ui // 2 + 1) * 4)
                        for t in range(TILES):
                            m = n * TILES + t
                            pool.wait_ge(scan_done, 2 * m + 2 + 2 + START)
                            h = hs[:, t % HR, :]
                            pool.tensor_tensor(h, h, bc[:, kslot, 1, :], ALU.mult).then_inc(hc_ready, 1)
                            split_side(t, n + 1)

            @block.vector
            def _(v):
                own = [0]

                def z_side(q, nb, nu, n1):
                    p, r, f, k = order(nu)
                    if q in (15, 18):
                        c = (q - 15) // 3
                        cs = slice(CH * c, CH * c + CH)
                        v.wait_ge(z_taken, n1 * 2 + c + 1)
                        v.wait_ge(dt_ready, n1 * 2 + START)
                        v.tensor_scalar(sp_e[:, cs], z_sb[:, cs], SP_LIMIT, None, ALU.min).then_inc(clipped, 1)
                    if q in (19, 22):
                        c = (q - 19) // 3
                        cs = slice(CH * c, CH * c + CH)
                        v.wait_ge(log_ready, n1 * 2 + c + 1)
                        v.wait_ge(rest_ready, n1 * 2)
                        v.tensor_tensor(dt[:, 0, cs], z_sb[:, cs], sp_e[:, cs], ALU.max).then_inc(dt_own, 1)
                        v.wait_ge(dt_own, n1 * 2 + c + 1)
                        v.tensor_tensor(dt[:, 1, cs], dt[:, 0, cs], source(nb, nu)(f, CH * c),
                                        ALU.mult).then_inc(dt_ready, 1)

                def product(n, ui, q, b):
                    p, r, f, k = order(ui)
                    g = n * (2 * TILES) + q
                    pos = q % 2 if r == 0 else 1 - q % 2
                    if q == 0 and ui % 2 == 0:
                        v.wait_ge(bc_ready, (b * K + ui // 2 + 1) * 4)
                    v.wait_ge(dtu_spread, g + 1)
                    v.wait_ge(scan_done, g + START)
                    v.tensor_tensor(dbu[:, q % 3, :], psU[:, q % 2, :],
                                    bc[:, ui // 2 % 2, 0, CH * pos:CH * pos + CH], ALU.mult).then_inc(dbu_ready, 1)

                def take(n, b, ui):
                    p, r, f, k = order(ui)
                    v.wait_ge(summed, n * SUB + (2 * SUB + 1 + START))
                    acc = psY[0:HC, :, :].rearrange("p c l -> p (c l)")
                    y = s.Y[:, b, f, :]
                    if p == 0 and r == 0:
                        v.scalar_tensor_tensor(out=y, in0=s.X[:, b, f, :], scalar=s.d_sum[:, f:f + 1], in1=acc,
                                               op0=ALU.mult, op1=ALU.add).then_inc(y_taken, 1)
                    elif p == 0:
                        v.tensor_tensor(y, y, acc, ALU.add).then_inc(y_taken, 1)
                    else:
                        yt = y.rearrange("p (h w) -> p w h", h=HH)
                        v.tensor_tensor(yt, yt, acc.rearrange("p (w h) -> p w h", w=WW), ALU.add).then_inc(y_taken, 1)

                for n1 in range(2):
                    for q in (15, 18, 19, 22):
                        z_side(q, 0, n1, n1)
                with v.Fori(0, NB, 1) as b:
                    for ui in range(UNITS):
                        n = b * UNITS + ui
                        p, r, f, k = order(ui)
                        product(n, ui, 0, b)
                        for q in range(2 * TILES):
                            t = q // 2
                            g = n * (2 * TILES) + q
                            if q + 1 < 2 * TILES:
                                product(n, ui, q + 1, b)
                            pos = q % 2 if r == 0 else 1 - q % 2
                            if q % 6 == 0:
                                v.wait_ge(summed, n * SUB + (SUB + q // 6 + START))
                            v.wait_ge(decay_ready, g + 1)
                            v.wait_ge(dbu_ready, g + 1 + 2)
                            if q % 2:
                                v.wait_ge(scan_done, g + 2 + START)
                            h = hs[:, t % HR, CH * pos:CH * pos + CH]
                            da, du = psA[:, q % AR, :], dbu[:, q % 3, :]
                            if r:
                                h, da, du = h[:, ::-1], da[:, ::-1], du[:, ::-1]
                            if q % 2 == 0:
                                init = 0.0
                            else:
                                at = CH - 1 if r == 0 else CH
                                init = hs[:, t % HR, at:at + 1]
                            v.tensor_tensor_scan(h, da, du, init, ALU.mult, ALU.add).then_inc(scan_done, 1)
                            if q == 7:
                                take(n - 1, b if ui else (b + (NB - 1)) % NB, (ui - 1) % UNITS)
                            z_side(q, *units_ahead(b, ui, 2))
                take(NB * UNITS - 1, NB - 1, UNITS - 1)

            @block.sync
            def _(sp):
                def stack_up(n1, slot):
                    for part, ready in enumerate((hi_ready, mid_ready, lo_ready)):
                        sp.wait_ge(ready, n1 * 2 + 2)
                        for j in range(NBLK):
                            sp.dma_start(stack[BLK * part:BLK * part + BLK, slot, :, j, :],
                                         parts[BLK * j:BLK * j + BLK, :, part, :]).then_inc(stacked[slot], 16)

                stack_up(0, 0)
                with sp.Fori(0, NB, 1) as b:
                    for ui in range(UNITS):
                        n = b * UNITS + ui
                        sp.wait_ge(dt_spread, n * (2 * TILES) + START)
                        stack_up(n + 1, (ui + 1) % 2)
                sp.wait_ge(stacked[0], landed(NB, 0))


def layer_norm(nc, s, src, dst, tag, after=None):
    with ExitStack() as ctx:
        def sb(name, shape, dt=F32):
            return ctx.enter_context(nc.sbuf_tensor(tag + name, shape, dt))

        def sem(name):
            return ctx.enter_context(nc.semaphore(tag + name))

        sq = sb("sq", [HC, 2, 2, CH])
        dev = sb("dev", [HC, 2, CH])
        ps_mean = ctx.enter_context(nc.psum_tensor(tag + "ps_mean", [HC, 2, CH], F32))
        ps_var = ctx.enter_context(nc.psum_tensor(tag + "ps_var", [HC, 2, CH], F32))
        mean_ready, var_ready = sem("mean_ready"), sem("var_ready")
        centred, normed = sem("centred"), sem("normed")
        squared, log_ready, dev_ready = sem("squared"), sem("log_ready"), sem("dev_ready")
        STEPS = 2 * NB

        def part(t, i, f):
            return t[:, i // 2, f, CH * (i % 2):CH * (i % 2) + CH]

        more = after(ctx, sb, sem, normed) if after else {}
        with nc.Block() as block:
            @block.tensor
            def _(pe):
                for i in range(STEPS + 1):
                    if i < STEPS:
                        if i >= 2:
                            pe.wait_ge(centred, i - 1)
                        for f in range(2):
                            m = pe.matmul(ps_mean[:, i % 2, :], s.average[:], part(src, i, f), start=(f == 0), stop=(f == 1))
                        m.then_inc(mean_ready, 1)
                    if i:
                        pe.wait_ge(squared, i)
                        if i >= 3:
                            pe.wait_ge(log_ready, i - 2)
                        for f in range(2):
                            m = pe.matmul(ps_var[:, (i - 1) % 2, :], s.average[:], sq[:, (i - 1) % 2, f, :],
                                          start=(f == 0), stop=(f == 1))
                        m.then_inc(var_ready, 1)

            @block.vector
            def _(v):
                if "load" in more:
                    more["load"](v)
                for i in range(STEPS + 1):
                    if i < STEPS:
                        v.wait_ge(mean_ready, i + 1)
                        for f in range(2):
                            m = v.tensor_tensor(part(dst, i, f), part(src, i, f), ps_mean[:, i % 2, :], ALU.subtract)
                        m.then_inc(centred, 1)
                    if i:
                        v.wait_ge(dev_ready, i)
                        v.wait_ge(centred, i)
                        d = dev[:, (i - 1) % 2, :]
                        for f in range(2):
                            m = v.tensor_tensor(part(dst, i - 1, f), part(dst, i - 1, f), d, ALU.mult)
                        m.then_inc(normed, 1)
                if "vector" in more:
                    more["vector"](v)

            @block.scalar
            def _(act):
                nc.scalar.preload_act_table_set("natural_log_exp_and_others")
                for i in range(STEPS + 1):
                    if i < STEPS:
                        act.wait_ge(centred, i + 1)
                        if i >= 2:
                            act.wait_ge(var_ready, i - 1)
                        for f in range(2):
                            m = nc.scalar.activation(sq[:, i % 2, f, :], part(dst, i, f), ACT.Square)
                        m.then_inc(squared, 1)
                    if i:
                        act.wait_ge(var_ready, i)
                        if i >= 3:
                            act.wait_ge(normed, i - 2)
                        d = dev[:, (i - 1) % 2, :]
                        nc.scalar.activation(d, ps_var[:, (i - 1) % 2, :], ACT.Ln, bias=s.eps5[0:HC, :]).then_inc(log_ready, 1)
                        act.wait_ge(log_ready, i)
                        nc.scalar.activation(d, d, ACT.Exp, scale=-0.5).then_inc(dev_ready, 1)
                if "scalar" in more:
                    more["scalar"](act)

            if "gpsimd" in more:
                @block.gpsimd
                def _(pool):
                    more["gpsimd"](pool)

            if "sync" in more:
                @block.sync
                def _(sp):
                    more["sync"](sp)


def conv_out(nc, w, s):
    def after(ctx, sb, sem, normed):
        x_in = [sem(f"x_again{b}") for b in range(NB)]
        gelu_done = sem("gelu_done")

        def scalar(act):
            act.wait_ge(normed, 2 * NB)
            for b in range(NB):
                for f in range(2):
                    nc.scalar.activation(s.Z[:, b, f, :], s.Z[:, b, f, :], ACT.Gelu,
                                         bias=s.cols[:, COL_LNB + f:COL_LNB + f + 1],
                                         scale=s.cols[:, COL_LNW + f:COL_LNW + f + 1]).then_inc(gelu_done, 1)

        def vector(v):
            for b in range(NB):
                v.wait_ge(x_in[b], 16)
                for f in range(2):
                    v.wait_ge(gelu_done, 2 * b + f + 1)
                    v.tensor_tensor(s.Y[:, b, f, :], s.raw[:, b, f, :], s.Z[:, b, f, :], ALU.add)

        def sync(sp):
            for b in range(NB):
                sp.dma_start(s.raw[:, b, :, :], w.x[b].rearrange("(f p) h w -> p f (h w)", p=HC)).then_inc(x_in[b], 16)

        return {"scalar": scalar, "vector": vector, "sync": sync}

    layer_norm(nc, s, s.Y, s.Z, "lc_", after)


def token_norm(nc, s):
    def after(ctx, sb, sem, normed):
        cleared = sem("cleared")

        def pool(pool):
            pool.memset(s.V[:], 0.0).then_inc(cleared, 1)
            pool.wait_ge(cleared, 1)
            pool.memset(s.V[:, :, :, :, DH:DH + 1].rearrange("p b t h o -> p (b t) (h o)"), 1.0)

        return {"gpsimd": pool}

    layer_norm(nc, s, s.Y, s.Z, "la_", after)


def qkv(nc, w, s):
    with ExitStack() as ctx:
        def sb(name, shape, dt=F32):
            return ctx.enter_context(nc.sbuf_tensor(name, shape, dt))

        def sem(name):
            return ctx.enter_context(nc.semaphore(name))

        w_rows = sb("w_rows", [HC, 6, D])
        w_qkv = sb("w_qkv", [HC, 2, 3 * D])
        vb = sb("vb", [128, D])
        qb = sb("qb", [HC, 4])
        p_rows = sb("p_rows", [HC, 2, D])
        p_pad = sb("p_pad", [HC, 2, 3, 4, 32])
        val = sb("val", [HC, 2, L])
        rest = sb("qrest", [HC, 2, L])
        parts = sb("qparts", [HC, 2, QPART, L], BF16)
        hankel = sb("hankel", [19, 19, HEADS])
        last_row = sb("last_row", [19, HEADS])
        RING = 4
        ps_w = ctx.enter_context(nc.psum_tensor("ps_w", [128, RING, CH], F32))
        ps_v = ctx.enter_context(nc.psum_tensor("ps_v", [128, RING, CH], F32))
        w_in, vb_in, p_in, tab_ext, tab_in, last_in = (
            sem("w_in"), sem("vb_in"), sem("p_in"), sem("tab_ext"), sem("tab_in"), sem("last_in"))
        pool_ready, w_turned, w_taken, q_proj, q_taken, v_proj, v_taken = (
            sem("pool_ready"), sem("w_turned"), sem("w_taken"), sem("q_proj"), sem("q_taken"), sem("v_proj"), sem("v_taken"))
        own_v, hi_ready, rest_ready, mid_ready, lo_ready, padded, corner, corner_turned = (
            sem("own_v"), sem("qhi"), sem("qrestr"), sem("qmid"), sem("qlo"), sem("padded"), sem("corner"), sem("corner_turned"))
        stored = [sem(f"stored{i}") for i in range(2)]
        NQ = 4 * NB

        with nc.Block() as block:
            @block.sync
            def _(sp):
                sp.dma_start(w_rows[:], w.qkvw.rearrange("(m p) d -> p m d", p=HC)).then_inc(w_in, 16)
                sp.dma_start(vb[:], w.qkvb[2 * D:3 * D].rearrange("(o d) -> o d", o=1).broadcast_to([128, D])).then_inc(vb_in, 16)
                sp.dma_start(p_rows[:], w.projw.rearrange("(m p) d -> p m d", p=HC)).then_inc(p_in, 16)
                sp.dma_start(s.ext[0:19, :], w.table).then_inc(tab_ext, 16)
                sp.dma_start(s.ext[19:37, :], w.table[0:18, :]).then_inc(tab_ext, 16)
                sp.dma_start(last_row[:], w.table[18:19, :].broadcast_to([19, HEADS])).then_inc(last_in, 16)
                sp.wait_ge(tab_ext, 32)
                win = bass.AP(s.ext[:, :].tensor, 0, [[HEADS, 19], [1, 19 * HEADS]])
                sp.dma_start(hankel[:].rearrange("p e h -> p (e h)"), win).then_inc(tab_in, 16)
                for i in range(NQ):
                    b, qk, f = i // 4, i // 2 % 2, i % 2
                    sp.wait_ge(lo_ready, i + 1)
                    sp.wait_ge(mid_ready, i + 1)
                    sp.dma_start(s.qk_dram[b, qk, :, HC * f:HC * f + HC, :].rearrange("a p l -> p a l"),
                                 parts[:, i % 2, :, :]).then_inc(stored[i % 2], 16)
                for i in range(2):
                    sp.wait_ge(stored[i], 16 * (NQ // 2))

            @block.gpsimd
            def _(pool):
                pool.memset(p_pad[:], 0.0).then_inc(pool_ready, 1)
                pool.memset(s.shift[:], 0.0).then_inc(pool_ready, 1)
                pool.wait_ge(pool_ready, 2)
                pool.affine_select(out=s.shift[:], in_=s.shift[:], compare_op=ALU.not_equal, fill=1.0, base=128 - 19,
                                   pattern=[[-1, 128]], channel_multiplier=1).then_inc(pool_ready, 1)
                pool.wait_ge(corner, 2)
                pool.affine_select(out=s.corner_q[:], in_=s.corner_q[:], compare_op=ALU.is_ge, fill=0.0, base=0,
                                   pattern=[[0, HEADS], [1, 19]], channel_multiplier=-1).then_inc(corner, 1)

            @block.tensor
            def _(pe):
                pe.wait_ge(w_in, 16)
                for m in range(6):
                    for f in range(2):
                        t = pe.transpose(ps_w[0:HC, 2 * f + m // 3, HC * (m % 3):HC * (m % 3) + HC],
                                         w_rows[:, m, HC * f:HC * f + HC], s.ident[0:HC, 0:HC])
                t.then_inc(w_turned, 1)
                pe.wait_ge(w_taken, 1)
                nv = 0
                for b in range(NB):
                    for j in range(8):
                        i = 8 * b + j
                        qk, f, c = j // 4, j // 2 % 2, j % 2
                        if i >= RING:
                            pe.wait_ge(q_taken, i - RING + 1)
                        for h in range(2):
                            t = pe.matmul(ps_w[0:HC, i % RING, :], w_qkv[:, h, D * qk + HC * f:D * qk + HC * f + HC],
                                          s.Z[:, b, h, CH * c:CH * c + CH], start=(h == 0), stop=(h == 1))
                        t.then_inc(q_proj, 1)
                        if nv >= RING:
                            pe.wait_ge(v_taken, nv - RING + 1)
                        for h in range(2):
                            t = pe.matmul(ps_v[:, nv % RING, 0:D], s.Z[:, b, h, 128 * j:128 * j + 128],
                                          w_qkv[:, h, 2 * D:3 * D], start=(h == 0), stop=(h == 1))
                        t.then_inc(v_proj, 1)
                        nv += 1
                pe.wait_ge(q_taken, 8 * NB)
                pe.wait_ge(padded, 1)
                for g in range(3):
                    for f in range(2):
                        t = pe.transpose(ps_w[:, g, HC * f:HC * f + HC],
                                         p_pad[:, f, g, :, :].rearrange("p j c -> p (j c)"), s.ident[0:HC, 0:HC])
                pe.wait_ge(corner, 3)
                for h in range(HEADS):
                    t = pe.transpose(ps_w[0:19, 3, 19 * h:19 * h + 19], s.corner_q[:, h, :], s.ident[0:19, 0:19])
                t.then_inc(corner_turned, 1)

            @block.scalar
            def _(act):
                for i in range(NQ):
                    b, qk, f = i // 4, i // 2 % 2, i % 2
                    act.wait_ge(own_v, 1)
                    if i >= 2:
                        act.wait_ge(lo_ready, i - 1)
                        act.wait_ge(stored[i % 2], 16 * (i // 2))
                    for c in range(2):
                        act.wait_ge(q_proj, 2 * i + c + 1)
                        nc.scalar.activation(val[:, i % 2, CH * c:CH * c + CH], ps_w[0:HC, (2 * i + c) % RING, :], ACT.Identity,
                                             bias=qb[:, 2 * qk + f:2 * qk + f + 1], scale=(DH ** -0.5 if qk == 0 else 1.0)
                                             ).then_inc(q_taken, 1)
                    act.wait_ge(q_taken, 2 * i + 2)
                    nc.scalar.copy(parts[:, i % 2, 0, :], val[:, i % 2, :]).then_inc(hi_ready, 1)
                    if i:
                        act.wait_ge(rest_ready, i)
                        nc.scalar.copy(parts[:, (i - 1) % 2, 1, :], rest[:, (i - 1) % 2, :]).then_inc(mid_ready, 1)
                act.wait_ge(rest_ready, NQ)
                nc.scalar.copy(parts[:, (NQ - 1) % 2, 1, :], rest[:, (NQ - 1) % 2, :]).then_inc(mid_ready, 1)

            @block.vector
            def _(v):
                v.tensor_scalar(qb[:, 0:2], s.cols[:, COL_Q:COL_Q + 2], DH ** -0.5, None, ALU.mult)
                v.tensor_copy(qb[:, 2:4], s.cols[:, COL_K:COL_K + 2]).then_inc(own_v, 1)
                v.wait_ge(w_turned, 1)
                for f in range(2):
                    for g in range(2):
                        t = v.tensor_copy(w_qkv[:, f, 3 * HC * g:3 * HC * g + 3 * HC], ps_w[0:HC, 2 * f + g, 0:3 * HC])
                t.then_inc(w_taken, 1)
                v.wait_ge(vb_in, 16)
                nv = 0
                for i in range(NQ + 1):
                    if i < NQ:
                        for _ in range(2):
                            v.wait_ge(v_proj, nv + 1)
                            v.tensor_tensor(s.V[:, nv // 8, nv % 8, :, 0:DH],
                                            ps_v[:, nv % RING, 0:D].rearrange("p (h d) -> p h d", d=DH),
                                            vb[:].rearrange("p (h d) -> p h d", d=DH), ALU.add).then_inc(v_taken, 1)
                            nv += 1
                        v.wait_ge(hi_ready, i + 1)
                        if i >= 2:
                            v.wait_ge(mid_ready, i - 1)
                        v.tensor_tensor(rest[:, i % 2, :], val[:, i % 2, :], parts[:, i % 2, 0, :],
                                        ALU.subtract).then_inc(rest_ready, 1)
                    if i:
                        v.wait_ge(mid_ready, i)
                        v.tensor_tensor(parts[:, (i - 1) % 2, 2, :], rest[:, (i - 1) % 2, :], parts[:, (i - 1) % 2, 1, :],
                                        ALU.subtract).then_inc(lo_ready, 1)
                v.wait_ge(p_in, 16)
                v.wait_ge(pool_ready, 1)
                for f in range(2):
                    v.tensor_copy(p_pad[:, f, :, :, 0:DH].rearrange("p g j c -> p (g j) c"),
                                  p_rows[:, f, :].rearrange("p (g c) -> p g c", c=DH))
                    t = v.tensor_copy(p_pad[:, f, 0, 0, DH:DH + 1], s.cols[:, COL_PB + f:COL_PB + f + 1])
                t.then_inc(padded, 1)
                v.wait_ge(tab_in, 16)
                v.wait_ge(last_in, 16)
                v.tensor_copy(s.corner_q[:], hankel[:].rearrange("p e h -> p h e")[:, :, ::-1]).then_inc(corner, 1)
                v.wait_ge(corner, 1)
                v.tensor_tensor(s.corner_q[:], s.corner_q[:], last_row[:].unsqueeze(2).broadcast_to([19, HEADS, 19]),
                                ALU.subtract).then_inc(corner, 1)
                v.wait_ge(corner_turned, 1)
                v.tensor_copy(s.corner_k[:].rearrange("p h j -> p (h j)"), ps_w[0:19, 3, 0:19 * HEADS])
                v.tensor_copy(s.w_proj[:], ps_w[:, 0:3, 0:D])


def attention(nc, w, s):
    with ExitStack() as ctx:
        def sb(name, shape, dt=F32):
            return ctx.enter_context(nc.sbuf_tensor(name, shape, dt))

        def sem(name):
            return ctx.enter_context(nc.semaphore(name))

        Q_PARTS, K_PARTS = [0, 0, 1, 1, 0, 2], [0, 1, 0, 1, 2, 0]
        KQ = DH * len(Q_PARTS)
        KM = KQ + QPART
        NHG = 3
        GH = 4
        KT = L // 128
        HALF = 2 * NHG * KT
        MAXES = GH * KT * 2

        qs = sb("qs", [KM, NHG, GH, L], BF16)
        ks = sb("ks", [KM, NHG, GH, L], BF16)
        mx = sb("mx", [128, NHG, MAXES])
        nm = sb("nm", [128, 2, 32])
        nmp = sb("nmp", [128, QPART, 32], BF16)
        nmt = sb("nmt", [QPART * 32, 128], BF16)
        P = sb("P", [128, 2, GH, CH])
        v_now = sb("v_now", [128, KT, HEADS, 32])
        o_raw = sb("o_raw", [128, 2, CH])
        rec = sb("rec", [128, CH])
        o_n = sb("o_n", [128, NHG, L])
        ps1 = ctx.enter_context(nc.psum_tensor("ps1", [128, 2, CH], F32))
        ps2 = ctx.enter_context(nc.psum_tensor("ps2", [128, 2, 2, CH], F32))
        psO = ctx.enter_context(nc.psum_tensor("psO", [128, CH], F32))
        psM = ctx.enter_context(nc.psum_tensor("psM", [128, CH], F32))

        stack_in = [sem(f"stack_in{i}") for i in range(NHG)]
        rows_set = sem("rows_set")
        s1_ready = sem("s1_ready")
        max_done = sem("max_done")
        s2_ready = sem("s2_ready")
        exp_done = sem("exp_done")
        pv_done = sem("pv_done")
        o_taken = sem("o_taken")
        misc_ready = sem("misc_ready")
        misc_taken = sem("misc_taken")
        own = sem("own_at")
        nmp_ready = sem("nmp_ready")
        nm_store, nm_in = sem("nm_store"), sem("nm_in")
        rec_ready = sem("rec_ready")
        on_ready = sem("on_ready")
        v_set = sem("v_set")
        OWN = 6

        MISC = 3 * NHG + 4
        PROJ = (3 * NHG - 1, 3 * NHG, 3 * NHG + 2, 3 * NHG + 3)
        LAST_SUMS = 3 * NHG + 1

        def step_ahead(b, hg, d):
            return b + (hg + d) // NHG, (hg + d) % NHG, b * NHG + hg + d

        LATER = [(0, hg, qc) for hg in range(NHG) for qc in range(2) if hg or qc] + [(1, 0, 0)]

        def in_psM(b, hg, qc):
            return b * MISC + (1 + 3 * hg + 1) if qc else b * MISC + (1 + 3 * hg - 1)

        with nc.Block() as block:
            @block.gpsimd
            def _(pool):
                pool.memset(ks[KQ:KM, :, :, :].rearrange("p g h l -> p (g h l)"), 1.0).then_inc(rows_set, 1)

                def place(b, hg):
                    h = slice(GH * hg, GH * hg + GH)
                    pool.tensor_copy(v_now[:, :, h, :].rearrange("p t h d -> p t (h d)"),
                                     s.V[:, b, :, h, :].rearrange("p t h d -> p t (h d)")).then_inc(v_set, 1)

                pool.wait_ge(rows_set, 1)
                for hg in range(NHG):
                    place(0, hg)
                with pool.Fori(0, NB, 1) as b:
                    for hg in range(NHG):
                        pool.wait_ge(pv_done, (b * NHG + (hg + 1)) * (2 * KT) + 1 + START)
                        place((b + 1) % NB, hg)

            @block.sync
            def _(sp):
                def load(b, hg):
                    for j in range(len(Q_PARTS)):
                        for stack, qk, part in ((qs, 0, Q_PARTS[j]), (ks, 1, K_PARTS[j])):
                            sp.dma_start(stack[DH * j:DH * j + DH, hg, :, :],
                                         s.qk_dram[b, qk, part, DH * GH * hg:DH * GH * (hg + 1), :]
                                         .rearrange("(h c) l -> c h l", c=DH)).then_inc(stack_in[hg], 16)

                def maxima(i, hg):
                    sp.dma_start(s.nm_dram[:, :], nmt[:]).then_inc(nm_store, 16)
                    sp.wait_ge(nm_store, (i + 1) * 16)
                    sp.dma_start(qs[KQ:KM, hg, :, :].rearrange("p h l -> p (h l)"),
                                 s.nm_dram[:, :].rearrange("(a r) c -> a (r c)", a=QPART)).then_inc(nm_in, 16)
                    sp.wait_ge(nm_in, (i + 1) * 16)

                for hg in range(NHG):
                    load(0, hg)
                sp.wait_ge(misc_taken, 1)
                maxima(0, 0)
                with sp.Fori(0, NB, 1) as b:
                    for hg in range(NHG):
                        sp.wait_ge(misc_taken, b * MISC + (3 * hg + 2))
                        maxima(b * NHG + (hg + 1), (hg + 1) % NHG)
                        sp.wait_ge(s2_ready, (b * HALF + (hg + 1) * 2 * KT) * 2)
                        load((b + 1) % NB, hg)
                for hg in range(NHG):
                    sp.wait_ge(stack_in[hg], (NB + 1) * 2 * len(Q_PARTS) * 16)

            @block.tensor
            def _(pe):
                pe.sem_inc(max_done, 1)
                pe.sem_inc(exp_done, 2)
                pe.sem_inc(pv_done, 1 + START)
                pe.sem_inc(on_ready, 1 + START)
                pe.sem_inc(o_taken, START)

                def first_scores(u, i, hg):
                    head, qt, c = u // (2 * KT), u // 2 % KT, u % 2
                    pe.wait_ge(max_done, i * MAXES + u)
                    corner = qt == 0 and c == 1
                    m = pe.matmul(ps1[:, u % 2, :], qs[0:KQ, hg, head, 128 * qt:128 * qt + 128],
                                  ks[0:KQ, hg, head, CH * c:CH * c + CH], start=True, stop=not corner)
                    if corner:
                        m = pe.matmul(ps1[:, u % 2, CH - 19:CH], s.ident[0:19, :], s.corner_q[:, GH * hg + head, :],
                                      start=False, stop=True)
                    m.then_inc(s1_ready, 1)

                def second_scores(sl, hg, qc, kt, pair):
                    pe.wait_ge(exp_done, sl * 2 + (pair + 1))
                    for e in range(2):
                        head = 2 * pair + e
                        corner = qc == 0 and kt == KT - 1
                        m = pe.matmul(ps2[:, pair, e, :], ks[0:KM, hg, head, 128 * kt:128 * kt + 128],
                                      qs[0:KM, hg, head, CH * qc:CH * qc + CH], start=True, stop=not corner)
                        if corner:
                            m = pe.matmul(ps2[:, pair, e, 0:19], s.shift[:], s.corner_k[:, GH * hg + head, :],
                                          start=False, stop=True)
                    m.then_inc(s2_ready, 1)

                def values(part, sl, hg, kt, half):
                    if part == 0:
                        pe.wait_ge(exp_done, sl * 2 + 4)
                        if kt == 0:
                            pe.wait_ge(o_taken, half + START)
                    cols = slice(CH // 2 * part, CH // 2 * (part + 1))
                    for head in range(GH):
                        m = pe.matmul(psO[32 * head:32 * head + 32, cols], v_now[:, kt, GH * hg + head, :],
                                      P[:, kt % 2, head, cols], start=(kt == 0 and part == 0),
                                      stop=(kt == KT - 1 and part == 1))
                    if part == 1:
                        m.then_inc(pv_done, 1)

                def turn_maxima(use):
                    pe.wait_ge(misc_taken, use)
                    pe.transpose(psM[0:QPART * 32, 0:64].bitcast(BF16), nmp[:].rearrange("p a r -> p (a r)"),
                                 s.ident_bf[:]).then_inc(misc_ready, 1)

                def spread_sums(use, half, hb):
                    pe.wait_ge(o_taken, half + 1 + START)
                    pe.wait_ge(misc_taken, use)
                    pe.matmul(psM[:, :], s.sum_sel[:], o_raw[:, hb, :], start=True, stop=True).then_inc(misc_ready, 1)

                def project(b, x):
                    c, f = x // 2, x % 2
                    pe.wait_ge(misc_taken, b * MISC + (1 + PROJ[x]))
                    pe.wait_ge(on_ready, b * (2 * NHG) + (2 * NHG + c) + START)
                    for g in range(NHG):
                        m = pe.matmul(psM[0:HC, :], s.w_proj[:, g, HC * f:HC * f + HC], o_n[:, g, CH * c:CH * c + CH],
                                      start=(g == 0), stop=(g == NHG - 1))
                    m.then_inc(misc_ready, 1)

                pe.wait_ge(stack_in[0], 2 * len(Q_PARTS) * 16)
                for u in range(MAXES):
                    first_scores(u, 0, 0)
                pe.wait_ge(nmp_ready, 1)
                turn_maxima(0)
                pe.wait_ge(stack_in[1], 2 * len(Q_PARTS) * 16)
                for u in range(MAXES // 2):
                    first_scores(u, 1, 1)
                pe.wait_ge(rows_set, 1)
                def half_of(b, hg, qc, before):
                    half = b * (2 * NHG) + (2 * hg + qc)
                    nb, nhg, ni = step_ahead(b, hg, 1 + qc)
                    if qc == 0:
                        pe.wait_ge(nm_in, (b * NHG + (hg + 1)) * 16)
                        pe.wait_ge(v_set, b * NHG + (hg + 1))
                    else:
                        pe.wait_ge(stack_in[nhg], (nb + 1) * (2 * len(Q_PARTS) * 16))
                    for kt in range(KT):
                        sl = half * KT + kt
                        if kt:
                            late = (sl - 1, hg, kt - 1, half)
                        else:
                            late = (sl - 1, before[1], KT - 1, half - 1) if before else None
                        u = MAXES // 2 * (1 - qc) + GH * kt
                        for pair in range(2):
                            first_scores(u + pair, ni, nhg)
                            second_scores(sl, hg, qc, kt, pair)
                        first_scores(u + 2, ni, nhg)
                        if late:
                            values(0, *late)
                        first_scores(u + 3, ni, nhg)
                        if late:
                            values(1, *late)
                        if kt == 2 and before:
                            if hg or qc:
                                spread_sums(in_psM(b, hg, qc), half - 1, 1 - qc)
                            else:
                                spread_sums(before[0] * MISC + (1 + LAST_SUMS), half - 1, 1)
                        if kt == 1 and qc == 1:
                            pe.wait_ge(nmp_ready, b * NHG + (hg + 2))
                            turn_maxima(b * MISC + (1 + 3 * hg))
                        if kt >= 6 and hg == NHG - 1 and qc == 1:
                            project(b, kt - 6)
                        if kt >= 6 and hg == 0 and qc == 0 and before:
                            project(before[0], kt - 4)

                def halves(b, later):
                    for d, hg, qc in later:
                        half_of(b + d if d else b, hg, qc, (b, NHG - 1) if d else (b, hg - (1 - qc)))

                half_of(0, 0, 0, None)
                with pe.Fori(0, NB - 1, 1) as b:
                    halves(b, LATER)
                halves(NB - 1, LATER[:-1])
                half = NB * 2 * NHG - 1
                for part in range(2):
                    values(part, half * KT + KT - 1, NHG - 1, KT - 1, half)
                spread_sums((NB - 1) * MISC + (1 + LAST_SUMS), half, 1)
                project(NB - 1, 2)
                project(NB - 1, 3)

            @block.scalar
            def _(act):
                def read_sums(half, qc):
                    act.wait_ge(pv_done, half * KT + (KT + 1) + START)
                    act.wait_ge(on_ready, half + START)
                    nc.scalar.copy(o_raw[:, qc, :], psO[:, :]).then_inc(o_taken, 1)

                def invert_sums(use, half):
                    act.wait_ge(misc_ready, use + 1)
                    act.wait_ge(on_ready, half + 1 + START)
                    nc.scalar.activation(rec[:], psM[:, :], ACT.Ln).then_inc(misc_taken, 1)
                    act.wait_ge(misc_taken, use + 1)
                    nc.scalar.activation(rec[:], rec[:], ACT.Exp, scale=-1.0).then_inc(rec_ready, 1)

                nc.scalar.preload_act_table_set("natural_log_exp_and_others")
                def half_of(b, hg, qc, before):
                    half = b * (2 * NHG) + (2 * hg + qc)
                    for kt in range(KT):
                        sl = half * KT + kt
                        act.wait_ge(pv_done, sl + START)
                        for pair in range(2):
                            act.wait_ge(s2_ready, sl * 2 + (pair + 1))
                            nc.scalar.activation(P[:, kt % 2, 2 * pair:2 * pair + 2, :], ps2[:, pair, :, :],
                                                 ACT.Exp).then_inc(exp_done, 1)
                        if kt == 0 and before:
                            read_sums(half - 1, 1 - qc)
                        if kt == 3 and before:
                            if hg or qc:
                                invert_sums(in_psM(b, hg, qc), half - 1)
                            else:
                                invert_sums(before[0] * MISC + (1 + LAST_SUMS), half - 1)

                def halves(b, later):
                    for d, hg, qc in later:
                        half_of(b + d if d else b, hg, qc, (b,))

                half_of(0, 0, 0, None)
                with act.Fori(0, NB - 1, 1) as b:
                    halves(b, LATER)
                halves(NB - 1, LATER[:-1])
                half = NB * 2 * NHG - 1
                read_sums(half, 1)
                invert_sums((NB - 1) * MISC + (1 + LAST_SUMS), half)

            @block.vector
            def _(v):
                def tile_max(i, u, slot):
                    v.wait_ge(s1_ready, i * MAXES + (u + 1))
                    v.reduce_max(mx[:, slot, u:u + 1], ps1[:, u % 2, :], AX.X).then_inc(max_done, 1)

                def split_max(i, slot):
                    link = [0]

                    def done(ins):
                        link[0] += 1
                        ins.then_inc(own, 1)
                        v.wait_ge(own, i * OWN + link[0])

                    v.wait_ge(max_done, i * MAXES + (MAXES + 1))
                    done(v.reduce_max(nm[:, 1, :], mx[:, slot, :].rearrange("p (t c) -> p t c", c=2), AX.X))
                    done(v.tensor_scalar(nm[:, 0, :], nm[:, 1, :], -1.0, None, ALU.mult))
                    done(v.tensor_copy(nmp[:, 0, :], nm[:, 0, :]))
                    done(v.tensor_tensor(nm[:, 1, :], nm[:, 0, :], nmp[:, 0, :], ALU.subtract))
                    done(v.tensor_copy(nmp[:, 1, :], nm[:, 1, :]))
                    done(v.tensor_tensor(nmp[:, 2, :], nm[:, 1, :], nmp[:, 1, :], ALU.subtract))
                    v.sem_inc(nmp_ready, 1)

                def take_maxima(use, i):
                    v.wait_ge(misc_ready, use + 1)
                    v.wait_ge(nm_store, i * 16)
                    v.tensor_copy(nmt[:], psM[0:QPART * 32, 0:64].bitcast(BF16)).then_inc(misc_taken, 1)

                def normalise(half, hg, qc):
                    v.wait_ge(rec_ready, half + 1)
                    v.tensor_tensor(o_n[:, hg, CH * qc:CH * qc + CH], o_raw[:, qc, :], rec[:], ALU.mult
                                    ).then_inc(on_ready, 1)

                def add_projection(b, x):
                    c, f = x // 2, x % 2
                    v.wait_ge(misc_ready, b * MISC + (2 + PROJ[x]))
                    y = s.Y[:, b, f, CH * c:CH * c + CH]
                    v.tensor_tensor(y, y, psM[0:HC, :], ALU.add).then_inc(misc_taken, 1)

                for u in range(MAXES):
                    tile_max(0, u, 0)
                split_max(0, 0)
                take_maxima(0, 0)
                for u in range(MAXES // 2):
                    tile_max(1, u, 1)
                def half_of(b, hg, qc, before):
                    half = b * (2 * NHG) + (2 * hg + qc)
                    nb, nhg, ni = step_ahead(b, hg, 1 + qc)
                    for kt in range(KT):
                        for x in range(GH):
                            tile_max(ni, MAXES // 2 * (1 - qc) + GH * kt + x, nhg)
                        if kt == 1 and qc == 1:
                            take_maxima(b * MISC + (1 + 3 * hg), b * NHG + (hg + 1))
                        if kt == 4 and before:
                            normalise(half - 1, before[1], 1 - qc)
                        if kt >= 6 and hg == NHG - 1 and qc == 1:
                            add_projection(b, kt - 6)
                        if kt >= 6 and hg == 0 and qc == 0 and before:
                            add_projection(before[0], kt - 4)
                    if qc == 0:
                        split_max(ni, nhg)

                def halves(b, later):
                    for d, hg, qc in later:
                        half_of(b + d if d else b, hg, qc, (b, NHG - 1) if d else (b, hg - (1 - qc)))

                half_of(0, 0, 0, None)
                with v.Fori(0, NB - 1, 1) as b:
                    halves(b, LATER)
                halves(NB - 1, LATER[:-1])
                normalise(NB * 2 * NHG - 1, NHG - 1, 1)
                add_projection(NB - 1, 2)
                add_projection(NB - 1, 3)


def experts(nc, w, s):
    with ExitStack() as ctx:
        def sb(name, shape, dt=F32):
            return ctx.enter_context(nc.sbuf_tensor(name, shape, dt))

        def sem(name):
            return ctx.enter_context(nc.semaphore(name))

        TT = NB * L // 128
        CT = CH // 128
        w1 = sb("w1", [HC, EXPERTS, 2, HID])
        w2 = sb("w2", [128, EXPERTS, HT, D])
        b1_rows = sb("b1_rows", [EXPERTS * HT, 128])
        b1 = sb("b1", [128, EXPERTS * HT])
        b2 = sb("b2", [128, EXPERTS, D])
        gate_w = sb("gate_w", [HC, 2, 32])
        gate_b = sb("gate_b", [128, 1])
        logit_t = sb("logit_t", [128, 2, CH])
        pr = sb("pr", [128, TT, EXPERTS])
        tot = sb("tot", [128, TT])
        beats = sb("beats", [128, TT])
        rank = sb("rank", [128, TT, EXPERTS])
        gate = sb("gate", [128, NB, 2, CT, EXPERTS])
        hid = sb("hid", [128, 2, HT, CH])
        acc = sb("acc", [128, 2, CT, D])
        res = sb("res", [HC, 2, 2, CH])
        psH = ctx.enter_context(nc.psum_tensor("psH", [128, 3, CH], F32))
        psE = ctx.enter_context(nc.psum_tensor("psE", [128, 2, CH], F32))
        psT = ctx.enter_context(nc.psum_tensor("psT", [128, 2, CH], F32))
        w1_in = [sem(f"w1_in{e}") for e in range(EXPERTS)]
        w2_in = [sem(f"w2_in{e}") for e in range(EXPERTS)]
        b1_in, b2_in, gw_in, gb_in = sem("b1_in"), sem("b2_in"), sem("gw_in"), sem("gb_in")
        cleared, b1_turned, logits, logits_taken, logits_turned, own, gates_ready = (
            sem("cleared"), sem("b1_turned"), sem("logits"), sem("logits_taken"), sem("logits_turned"), sem("own_ex"),
            sem("gates_ready"))
        exp_ready = sem("exp_ready")
        h_ready = sem("h_ready")
        h_done = sem("h_done")
        e_ready = sem("e_ready")
        e_taken = sem("e_taken")
        acc_set = sem("acc_set")
        turned = sem("turned")
        summed = sem("res_ready")
        stored = [sem(f"res_out{c}") for c in range(2)]

        with nc.Block() as block:
            @block.sync
            def _(sp):
                sp.wait_ge(cleared, 2)
                sp.dma_start(gate_w[:, :, 0:EXPERTS], w.gatew.rearrange("(f p) e -> p f e", p=HC)).then_inc(gw_in, 16)
                for j in range(4):
                    sp.dma_start(gate_b[32 * j:32 * j + EXPERTS, :], w.gateb.rearrange("(e o) -> e o", o=1)).then_inc(gb_in, 16)
                sp.dma_start(b1_rows[:], w.b1.rearrange("e (t p) -> (e t) p", p=128)).then_inc(b1_in, 16)
                for e in range(EXPERTS):
                    sp.dma_start(w1[:, e, :, :], w.w1[e].rearrange("(f p) h -> p f h", p=HC)).then_inc(w1_in[e], 16)
                    sp.dma_start(w2[:, e, :, :], w.w2[e].rearrange("(t p) d -> p t d", p=128)).then_inc(w2_in[e], 16)
                    if e == 0:
                        sp.dma_start(b2[:], w.b2.rearrange("(o e) d -> o e d", o=1).broadcast_to([128, EXPERTS, D])
                                     ).then_inc(b2_in, 16)
                with sp.Fori(0, NB, 1) as b:
                    for c in range(2):
                        sp.wait_ge(summed, b * 2 + (c + 2))
                        sp.dma_start(w.out[b].rearrange("(f p) h w -> p f (h w)", p=HC)[:, :, CH * c:CH * c + CH],
                                     res[:, c, :, :]).then_inc(stored[c], 16)
                for c in range(2):
                    sp.wait_ge(stored[c], 16 * NB + START)

            @block.gpsimd
            def _(pool):
                pool.memset(gate_w[:], 0.0).then_inc(cleared, 1)
                pool.memset(gate_b[:], 0.0).then_inc(cleared, 1)

            @block.tensor
            def _(pe):
                pe.sem_inc(h_done, 2 + START)
                pe.sem_inc(e_ready, CT + START)
                for c in range(2):
                    pe.sem_inc(stored[c], START)
                pe.sem_inc(e_taken, 1 + START)
                pe.sem_inc(summed, 1)
                pe.wait_ge(b1_in, 16)
                pe.transpose(psE[:, 0, 0:EXPERTS * HT], b1_rows[:], s.ident[0:EXPERTS * HT, 0:EXPERTS * HT]).then_inc(b1_turned, 1)
                pe.wait_ge(gw_in, 16)
                for g in range(2):
                    for f in range(2):
                        for j in range(4):
                            i = 4 * g + j
                            m = pe.matmul(psT[32 * j:32 * j + 32, g, :], gate_w[:, f, :],
                                          s.Z[:, i // 2, f, CH * (i % 2):CH * (i % 2) + CH], start=(f == 0), stop=(f == 1))
                m.then_inc(logits, 1)
                pe.wait_ge(logits_taken, 2)
                for g in range(2):
                    for t in range(CT):
                        m = pe.transpose(psH[:, g, 128 * t:128 * t + 128], logit_t[:, g, 128 * t:128 * t + 128], s.ident[:])
                m.then_inc(logits_turned, 1)
                for e in range(EXPERTS):
                    pe.wait_ge(w1_in[e], 16)
                    pe.wait_ge(w2_in[e], 16)
                pe.wait_ge(gates_ready, 1)

                def hidden(b, c, e, n):
                    for t in range(HT):
                        pe.wait_ge(h_done, n * HT + t + START)
                        for f in range(2):
                            m = pe.matmul(psH[:, t % 3, :], w1[:, e, f, 128 * t:128 * t + 128],
                                          s.Z[:, b, f, CH * c:CH * c + CH], start=(f == 0), stop=(f == 1))
                        m.then_inc(h_ready, 1)

                def outputs(e, n):
                    pe.wait_ge(h_done, n * HT + (HT + 2) + START)
                    for tt in range(CT):
                        pe.wait_ge(e_taken, n * CT + tt + START)
                        for t in range(HT):
                            m = pe.matmul(psE[:, tt % 2, 0:D], hid[:, e % 2, t, 128 * tt:128 * tt + 128], w2[:, e, t, :],
                                          start=(t == 0), stop=(t == HT - 1))
                        m.then_inc(e_ready, 1)

                def turn_back(b, c, n):
                    pe.wait_ge(e_taken, n * CT + (CT + 1) + START)
                    pe.wait_ge(summed, b * 2 + (c + 1))
                    for f in range(2):
                        for tt in range(CT):
                            m = pe.transpose(psT[0:HC, f, 128 * tt:128 * tt + 128], acc[:, c, tt, HC * f:HC * f + HC], s.ident[:])
                    m.then_inc(turned, 1)

                with pe.Fori(0, NB, 1) as b:
                    hidden(b, 0, 0, b * (2 * EXPERTS))
                    for c in range(2):
                        for e in range(EXPERTS):
                            n = b * (2 * EXPERTS) + (c * EXPERTS + e)
                            if e + 1 < EXPERTS:
                                hidden(b, c, e + 1, n + 1)
                            elif c == 0:
                                hidden(b, 1, 0, n + 1)
                            outputs(e, n)
                        turn_back(b, c, n)

            @block.scalar
            def _(act):
                act.wait_ge(own, 2)
                nc.scalar.activation(pr[:], pr[:], ACT.Exp).then_inc(exp_ready, 1)
                with act.Fori(0, NB, 1) as b:
                    for c in range(2):
                        for e in range(EXPERTS):
                            n = b * (2 * EXPERTS) + (c * EXPERTS + e)
                            act.wait_ge(b1_turned, 2)
                            for t in range(HT):
                                act.wait_ge(h_ready, n * HT + (t + 1))
                                if t == 0:
                                    act.wait_ge(e_ready, n * CT + START)
                                nc.scalar.activation(hid[:, e % 2, t, :], psH[:, t % 3, :], ACT.Gelu,
                                                     bias=b1[:, HT * e + t:HT * e + t + 1]).then_inc(h_done, 1)

            @block.vector
            def _(v):
                chain = Own(v, own)

                def step(ins):
                    chain(ins)
                    chain.wait()

                v.wait_ge(b1_turned, 1)
                v.tensor_copy(b1[:], psE[:, 0, 0:EXPERTS * HT]).then_inc(b1_turned, 1)
                v.wait_ge(logits, 1)
                v.wait_ge(gb_in, 64)
                for g in range(2):
                    v.tensor_scalar(logit_t[:, g, :], psT[:, g, :], gate_b[:, 0:1], None, ALU.add).then_inc(logits_taken, 1)
                v.wait_ge(logits_turned, 1)
                for g in range(2):
                    for t in range(CT):
                        m = v.tensor_copy(pr[:, 16 * g + t:16 * g + 16:CT, :],
                                          psH[:, g, 128 * t:128 * t + 128].rearrange("p (j e) -> p j e", e=32)[:, :, 0:EXPERTS])
                m.then_inc(gates_ready, 1)
                v.wait_ge(gates_ready, 1)
                step(v.reduce_max(tot[:], pr[:], AX.X))
                step(v.tensor_tensor(pr[:], pr[:], tot[:].unsqueeze(2).broadcast_to([128, TT, EXPERTS]), ALU.subtract))
                v.wait_ge(exp_ready, 1)
                step(v.reduce_sum(tot[:], pr[:], AX.X))
                step(v.reciprocal(tot[:], tot[:]))
                step(v.tensor_tensor(pr[:], pr[:], tot[:].unsqueeze(2).broadcast_to([128, TT, EXPERTS]), ALU.mult))
                step(v.memset(rank[:], 0.0))
                for lo in range(EXPERTS):
                    for hi in range(lo + 1, EXPERTS):
                        step(v.tensor_tensor(beats[:], pr[:, :, lo], pr[:, :, hi], ALU.is_ge))
                        step(v.tensor_tensor(rank[:, :, hi], rank[:, :, hi], beats[:], ALU.add))
                        step(v.tensor_scalar(beats[:], beats[:], -1.0, 1.0, ALU.mult, ALU.add))
                        step(v.tensor_tensor(rank[:, :, lo], rank[:, :, lo], beats[:], ALU.add))
                step(v.tensor_scalar(rank[:], rank[:], 1.5, None, ALU.is_le))
                step(v.tensor_tensor(pr[:], pr[:], rank[:], ALU.mult))
                step(v.reduce_sum(tot[:], pr[:], AX.X))
                step(v.tensor_scalar(tot[:], tot[:], 1e-9, None, ALU.add))
                step(v.reciprocal(tot[:], tot[:]))
                step(v.tensor_tensor(gate[:].rearrange("p b c t e -> p (b c t) e"), pr[:],
                                     tot[:].unsqueeze(2).broadcast_to([128, TT, EXPERTS]), ALU.mult))
                v.wait_ge(b2_in, 16)
                with v.Fori(0, NB, 1) as b:
                    for c in range(2):
                        for e in range(EXPERTS):
                            n = b * (2 * EXPERTS) + (c * EXPERTS + e)
                            for tt in range(CT):
                                g = gate[:, b, c, tt, e:e + 1]
                                a = acc[:, c, tt, :]
                                if e == 0:
                                    v.tensor_scalar(a, b2[:, 0, :], g, None, ALU.mult).then_inc(acc_set, 1)
                                    for x in range(1, EXPERTS):
                                        v.wait_ge(acc_set, (b * 2 + c) * (CT * EXPERTS) + (tt * EXPERTS + x))
                                        v.scalar_tensor_tensor(out=a, in0=b2[:, x, :], scalar=gate[:, b, c, tt, x:x + 1],
                                                               in1=a, op0=ALU.mult, op1=ALU.add).then_inc(acc_set, 1)
                                    v.wait_ge(acc_set, (b * 2 + c) * (CT * EXPERTS) + (tt * EXPERTS + EXPERTS))
                                else:
                                    v.wait_ge(e_taken, n * CT + (tt - CT + 2) + START)
                                v.wait_ge(e_ready, n * CT + (CT + tt + 1) + START)
                                v.scalar_tensor_tensor(out=a, in0=psE[:, tt % 2, 0:D], scalar=g, in1=a,
                                                       op0=ALU.mult, op1=ALU.add).then_inc(e_taken, 1)
                        v.wait_ge(turned, b * 2 + (c + 1))
                        v.wait_ge(stored[c], b * 16 + START)
                        v.tensor_tensor(res[:, c, :, :], psT[0:HC, :, :], s.Y[:, b, :, CH * c:CH * c + CH], ALU.add
                                        ).then_inc(summed, 1)


class Views:
    pass


def program(nc, ins, out):
    w = Views()
    (w.x, w.wx, w.wdt, w.dtb, w.alog, w.ds, w.lnw, w.lnb, w.qkvw, w.qkvb, w.projw, w.projb, w.table,
     w.gatew, w.gateb, w.w1, w.b1, w.w2, w.b2) = ins
    w.out = out
    with ExitStack() as ctx:
        def sb(name, shape, dt=F32):
            return ctx.enter_context(nc.sbuf_tensor(name, shape, dt))

        s = Views()
        s.Y = sb("Y", [HC, NB, 2, L])
        s.cols = sb("cols", [HC, NCOL])
        s.ident = sb("ident", [128, 128])
        s.ident_bf = sb("ident_bf", [128, 128], BF16)
        s.average = sb("average", [HC, HC])
        s.sum_sel = sb("sum_sel", [128, 128])
        s.one = sb("one", [128, 1])
        s.eps5 = sb("eps5", [128, 1])
        s.qk_dram = nc.dram_tensor("qk_parts", (NB, 2, QPART, D, L), BF16, kind="Internal").ap()
        s.nm_dram = nc.dram_tensor("max_parts", (QPART * 32, 128), BF16, kind="Internal").ap()
        s.ext = nc.dram_tensor("table_twice", (37, HEADS), F32, kind="Internal").ap()
        with ExitStack() as c2:
            def sb2(name, shape, dt=F32):
                return c2.enter_context(nc.sbuf_tensor(name, shape, dt))
            s.X = sb2("X", [HC, NB + 1, 2, L])
            s.d_sum = sb2("d_sum", [HC, 2])
            s.w_b = sb2("w_b", [HC, K, 2, 128])
            s.w_c = sb2("w_c", [HC, K, 2, 128])
            s.w_dt = sb2("w_dt", [HC, K, 2, D])
            s.a_neg = sb2("a_neg", [128, HC])
            s.spread_sel = sb2("spread_sel", [HC, SUB, 128], BF16)
            s.state_sel = sb2("state_sel", [128, SUB, BLK])
            prepare(nc, w, s)
            scan(nc, w, s)
        with ExitStack() as c2:
            s.Z = c2.enter_context(nc.sbuf_tensor("Z", [HC, NB, 2, L], F32))
            with nc.sbuf_tensor("raw", [HC, NB, 2, L], F32) as raw:
                s.raw = raw
                conv_out(nc, w, s)
        with ExitStack() as c2:
            def sb2(name, shape, dt=F32):
                return c2.enter_context(nc.sbuf_tensor(name, shape, dt))
            s.w_proj = sb2("w_proj", [128, 3, D])
            s.corner_q = sb2("corner_q", [19, HEADS, 19])
            s.corner_k = sb2("corner_k", [19, HEADS, 19])
            s.shift = sb2("shift", [19, 128])
            s.V = sb2("V", [128, NB, 8, HEADS, 32])
            with nc.sbuf_tensor("Zq", [HC, NB, 2, L], F32) as z:
                s.Z = z
                token_norm(nc, s)
                qkv(nc, w, s)
            attention(nc, w, s)
        with nc.sbuf_tensor("Zf", [HC, NB, 2, L], F32) as z:
            s.Z = z
            layer_norm(nc, s, s.Y, s.Z, "lf_")
            experts(nc, w, s)


_INS = ["x", "L0_conv_x_proj_weight", "L0_conv_dt_projs_weight", "L0_conv_dt_projs_bias", "L0_conv_A_logs",
        "L0_conv_Ds", "L0_conv_ln_weight", "L0_conv_ln_bias", "L1_attn_qkv_w", "L1_attn_qkv_b", "L1_attn_proj_w",
        "L1_attn_proj_b", "L1_attn_bias_table", "L1_ffn_gate_w", "L1_ffn_gate_b", "L1_ffn_w1", "L1_ffn_b1",
        "L1_ffn_w2", "L1_ffn_b2"]
_OUT = ((NB, D, HH, WW), "float32")


def kernel(**inputs):
    import numpy as _np
    import concourse.bacc as _bacc
    from concourse import mybir as _mybir
    from concourse.bass_utils import run_bass_kernel_spmd as _run

    nc = _bacc.Bacc("TRN2", target_bir_lowering=False, num_devices=1)
    arrays, args = {}, []
    for name in _INS:
        a = _np.ascontiguousarray(inputs[name])
        arrays[f"in_{name}_dram"] = a
        args.append(nc.dram_tensor(f"in_{name}_dram", a.shape, _mybir.dt.from_np(a.dtype), kind="ExternalInput").ap())
    shape, dtype = _OUT
    out = nc.dram_tensor("out_dram", shape, _mybir.dt.from_np(_np.dtype(dtype)), kind="ExternalOutput").ap()
    program(nc, args, out)
    r = _run(nc, [arrays], core_ids=[0])
    return r.results[0]["out_dram"]
```

```python
from contextlib import ExitStack

import concourse.bass as bass
from concourse import mybir

F32 = mybir.dt.float32
BF16 = mybir.dt.bfloat16
ALU = mybir.AluOpType
ACT = mybir.ActivationFunctionType
AX = mybir.AxisListType

NB = 4
D = 192
HC = 96
HH = WW = 32
L = HH * WW
CH = 512
K = 4
N = 16
R = 6
GN_CH = 6
DD = 8
BLK = 32
NBLK = HC // BLK
SUB = BLK // DD
TILES = HC // DD
UNITS = 2 * K
HEADS = 12
DH = 16
QPART = 3
EXPERTS = 4
HID = 768
HT = HID // 128
START = 1

COL_DTB, COL_DS, COL_LNW, COL_LNB, COL_Q, COL_K, COL_PB = 0, 8, 16, 18, 20, 22, 24
NCOL = 26


class Own:

    def __init__(self, eng, sem):
        self.eng, self.sem, self.n = eng, sem, 0

    def __call__(self, ins):
        ins.then_inc(self.sem, 1)
        self.n += 1
        return ins

    def wait(self):
        self.eng.wait_ge(self.sem, self.n)


def prepare(nc, w, s):
    with ExitStack() as ctx:
        def sb(name, shape, dt=F32):
            return ctx.enter_context(nc.sbuf_tensor(name, shape, dt))

        def sem(name):
            return ctx.enter_context(nc.semaphore(name))

        rows = sb("rows", [NCOL, HC])
        a_rows = sb("a_rows", [HC, 128])
        wx = sb("wx", [R + 2 * N, K, D])
        wdt_rows = sb("wdt_rows", [HC, 2 * K, R])
        wdt = sb("wdt", [R, K, D])
        group = sb("group", [HC, HC])
        stats = sb("stats", [HC, 2 * NB, 2, 6])
        mv = sb("mv", [HC, 2 * NB, 2])
        mean = sb("mean", [HC, 2 * NB])
        spread = sb("spread", [HC, 2 * NB])
        rstd = sb("rstd", [HC, 2 * NB])
        shift = sb("shift_x", [HC, 2 * NB])
        a_exp = sb("a_exp", [128, HC])
        ps = ctx.enter_context(nc.psum_tensor("ps_prep", [128, 8, CH], F32))
        x_in = [sem(f"x_in{b}") for b in range(NB)]
        rows_in, wx_in, wdt_in, a_in = sem("rows_in"), sem("wx_in"), sem("wdt_in"), sem("a_in")
        masks, pe_small, pe_wx, pe_wdt, pe_mean, pe_var = (
            sem("masks"), sem("pe_small"), sem("pe_wx"), sem("pe_wdt"), sem("pe_mean"), sem("pe_var"))
        a_turned = sem("a_turned")
        wdt_turned = sem("wdt_turned")
        shift_ready = sem("shift_ready")
        dve, aexp, std, gp, mean_in, var_in = sem("dve_prep"), sem("aexp"), sem("std"), sem("gp_prep"), sem("mean_in"), sem("var_in")

        with nc.Block() as block:
            @block.sync
            def _(sp):
                for b in range(NB):
                    sp.dma_start(s.X[:, b, :, :], w.x[b].rearrange("(f p) h w -> p f (h w)", p=HC)).then_inc(x_in[b], 16)

            @block.scalar
            def _(act):
                vec = [(COL_DTB, w.dtb.rearrange("k (f p) -> (k f) p", p=HC), 8),
                       (COL_DS, w.ds.rearrange("(k p) -> k p", p=HC), 8),
                       (COL_LNW, w.lnw.rearrange("(f p) -> f p", p=HC), 2),
                       (COL_LNB, w.lnb.rearrange("(f p) -> f p", p=HC), 2),
                       (COL_Q, w.qkvb[0:2 * D].rearrange("(f p) -> f p", p=HC), 4),
                       (COL_PB, w.projb.rearrange("(f p) -> f p", p=HC), 2)]
                for at, src, n in vec:
                    act.dma_start(rows[at:at + n, :], src).then_inc(rows_in, 16)
                act.dma_start(wx[:], w.wx.rearrange("k c d -> c k d")).then_inc(wx_in, 16)
                act.dma_start(a_rows[:], w.alog.rearrange("(g d) n -> g (d n)", d=DD)).then_inc(a_in, 16)
                act.dma_start(wdt_rows[:], w.wdt.rearrange("k (f p) r -> p (k f) r", p=HC)).then_inc(wdt_in, 16)
                act.wait_ge(a_turned, 1)
                nc.scalar.activation(a_exp[:], a_exp[:], ACT.Exp).then_inc(aexp, 1)
                act.wait_ge(pe_var, 1)
                act.wait_ge(gp, 1)
                nc.scalar.activation(spread[:], ps[0:HC, 1, 336:344], ACT.Sqrt, bias=s.eps5[0:HC, :]).then_inc(std, 1)
                act.wait_ge(shift_ready, 1)
                for q in range(NB, 2 * NB):
                    nc.scalar.activation(s.X[:, q // 2, q % 2, :], s.X[:, q // 2, q % 2, :], ACT.Identity,
                                         bias=shift[:, q:q + 1], scale=rstd[:, q:q + 1])
                act.wait_ge(pe_wdt, 2)
                for k in range(K):
                    nc.scalar.copy(s.w_dt[:, k, :, :], ps[0:HC, 2 + k, 0:2 * D].rearrange("p (f d) -> p f d", f=2))

            @block.gpsimd
            def _(pool):
                pool.memset(s.eps5[:], 1e-5).then_inc(gp, 1)
                own = 1

                def step(ins):
                    nonlocal own
                    own += 1
                    ins.then_inc(gp, 1)
                    pool.wait_ge(gp, own)

                step(pool.memset(s.ident[:], 0.0))
                step(pool.affine_select(out=s.ident[:], in_=s.ident[:], compare_op=ALU.not_equal, fill=1.0,
                                        base=0, pattern=[[-1, 128]], channel_multiplier=1))
                pool.memset(s.one[:], 1.0).then_inc(masks, 1)
                step(pool.memset(group[:], 1.0 / GN_CH))
                g3 = group[:].rearrange("p (g e) -> p g e", e=GN_CH)
                step(pool.affine_select(out=g3, in_=g3, compare_op=ALU.is_ge, fill=0.0, base=0,
                                        pattern=[[-GN_CH, HC // GN_CH], [0, GN_CH]], channel_multiplier=1))
                pool.affine_select(out=g3, in_=g3, compare_op=ALU.is_ge, fill=0.0, base=GN_CH - 1,
                                   pattern=[[GN_CH, HC // GN_CH], [0, GN_CH]], channel_multiplier=-1).then_inc(masks, 1)
                pool.memset(s.average[:], 1.0 / D)
                step(pool.memset(s.ident_bf[:], 0.0))
                step(pool.affine_select(out=s.ident_bf[:], in_=s.ident_bf[:], compare_op=ALU.not_equal, fill=1.0,
                                        base=0, pattern=[[-1, 128]], channel_multiplier=1))
                step(pool.memset(s.sum_sel[:], 0.0))
                sel = s.sum_sel[:].rearrange("p (h c) -> p h c", c=32)
                step(pool.affine_select(out=sel, in_=sel, compare_op=ALU.not_equal, fill=1.0, base=-DH,
                                        pattern=[[-32, 4], [0, 32]], channel_multiplier=1))
                step(pool.memset(s.spread_sel[:], 0.0))
                v = s.spread_sel[:].rearrange("p s (d n) -> p s d n", d=DD)
                for part in range(QPART):
                    step(pool.affine_select(out=v, in_=v, compare_op=ALU.not_equal, fill=1.0, base=-BLK * part,
                                            pattern=[[-DD, SUB], [-1, DD], [0, N]], channel_multiplier=1))
                step(pool.memset(s.state_sel[:], 1.0))
                step(pool.affine_select(out=s.state_sel[:], in_=s.state_sel[:], compare_op=ALU.is_ge, fill=0.0, base=0,
                                        pattern=[[N * DD, SUB], [-N, BLK]], channel_multiplier=1))
                pool.affine_select(out=s.state_sel[:], in_=s.state_sel[:], compare_op=ALU.is_ge, fill=0.0, base=N - 1,
                                   pattern=[[-N * DD, SUB], [N, BLK]], channel_multiplier=-1).then_inc(masks, 1)
                pool.memset(s.Y[:, NB - 1, 1, :], 0.0)
                pool.memset(s.X[:, NB, :, :], 0.0)

            @block.tensor
            def _(pe):
                pe.wait_ge(gp, 3)
                pe.wait_ge(rows_in, 6 * 16)
                pe.transpose(ps[0:HC, 0, 0:NCOL], rows[:], s.ident[0:NCOL, 0:NCOL]).then_inc(pe_small, 1)
                pe.wait_ge(a_in, 16)
                pe.transpose(ps[:, 0, 32:32 + HC], a_rows[:], s.ident[0:HC, 0:HC]).then_inc(pe_small, 1)
                pe.wait_ge(wx_in, 16)
                for k in range(K):
                    for f in range(2):
                        q = 2 * k + f
                        m = pe.transpose(ps[0:HC, 1, 38 * q:38 * q + 38], wx[:, k, HC * f:HC * f + HC],
                                         s.ident[0:38, 0:38])
                m.then_inc(pe_wx, 1)
                pe.wait_ge(wdt_in, 16)
                for q in range(2 * K):
                    bank, at = 6 + q // K, 0
                    m = pe.transpose(ps[0:R, bank, at + HC * (q % K):at + HC * (q % K) + HC], wdt_rows[:, q, :],
                                     s.ident[0:HC, 0:HC])
                m.then_inc(pe_wdt, 1)
                pe.wait_ge(wdt_turned, 1)
                for k in range(K):
                    for f in range(2):
                        m = pe.matmul(ps[0:HC, 2 + k, D * f:D * f + D], wx[0:R, k, HC * f:HC * f + HC],
                                      wdt[:, k, :], start=True, stop=True)
                m.then_inc(pe_wdt, 1)
                pe.wait_ge(masks, 2)
                pe.wait_ge(mean_in, 1)
                pe.matmul(ps[0:HC, 1, 320:328], group[:], mean[:], start=True, stop=True).then_inc(pe_mean, 1)
                pe.wait_ge(var_in, 1)
                pe.matmul(ps[0:HC, 1, 336:344], group[:], spread[:], start=True, stop=True).then_inc(pe_var, 1)

            @block.vector
            def _(v):
                own = Own(v, dve)
                for b in range(NB):
                    v.wait_ge(x_in[b], 16)
                    for f in range(2):
                        for c in range(2):
                            own(v.bn_stats(stats[:, 2 * b + f, c, :], s.X[:, b, f, CH * c:CH * c + CH]))
                own.wait()
                for q in range(2 * NB):
                    own(v.bn_aggr(mv[:, q, :], stats[:, q, :, :].rearrange("p c s -> p (c s)")))
                own.wait()
                v.tensor_copy(mean[:], mv[:, :, 0]).then_inc(mean_in, 1)
                v.wait_ge(pe_small, 2)
                v.tensor_copy(a_exp[:], ps[:, 0, 32:32 + HC]).then_inc(a_turned, 1)
                own(v.tensor_copy(s.cols[:], ps[0:HC, 0, 0:NCOL]))
                v.wait_ge(pe_wdt, 1)
                v.tensor_copy(wdt[:, 0:2, :], ps[0:R, 6, 0:4 * HC].rearrange("p (k d) -> p k d", k=2))
                v.tensor_copy(wdt[:, 2:4, :], ps[0:R, 7, 0:4 * HC].rearrange("p (k d) -> p k d", k=2)
                              ).then_inc(wdt_turned, 1)
                v.wait_ge(pe_mean, 1)
                own(v.tensor_tensor(spread[:], mv[:, :, 0], ps[0:HC, 1, 320:328], ALU.subtract))
                own(v.tensor_copy(mean[:], ps[0:HC, 1, 320:328]))
                own.wait()
                own(v.tensor_tensor(spread[:], spread[:], spread[:], ALU.mult))
                own.wait()
                v.tensor_tensor(spread[:], spread[:], mv[:, :, 1], ALU.add).then_inc(var_in, 1)
                v.wait_ge(std, 1)
                own(v.reciprocal(rstd[:], spread[:]))
                own.wait()
                own(v.scalar_tensor_tensor(out=shift[:], in0=mean[:], scalar=-1.0, in1=rstd[:], op0=ALU.mult, op1=ALU.mult))
                own.wait()
                v.sem_inc(shift_ready, 1)
                for q in range(NB):
                    own(v.tensor_scalar(s.X[:, q // 2, q % 2, :], s.X[:, q // 2, q % 2, :], mean[:, q:q + 1],
                                        rstd[:, q:q + 1], ALU.subtract, ALU.mult))
                v.wait_ge(pe_wx, 1)
                for k in range(K):
                    for f in range(2):
                        q = 2 * k + f
                        for i, dst in ((0, s.w_b), (1, s.w_c)):
                            src = ps[0:HC, 1, 38 * q + R + N * i:38 * q + R + N * i + N]
                            own(v.tensor_copy(dst[:, k, f, :].rearrange("p (d n) -> p d n", d=DD),
                                              src.unsqueeze(1).broadcast_to([HC, DD, N])))
                v.wait_ge(aexp, 1)
                own(v.tensor_scalar(s.a_neg[:], a_exp[:], -1.0, None, ALU.mult))
                own.wait()
                own(v.tensor_reduce(s.d_sum[:], s.cols[:, COL_DS:COL_DS + 8].rearrange("p (k f) -> p f k", f=2),
                                    AX.X, ALU.add))
                own.wait()


def scan(nc, w, s):
    with ExitStack() as ctx:
        def sb(name, shape, dt=F32):
            return ctx.enter_context(nc.sbuf_tensor(name, shape, dt))

        def sem(name):
            return ctx.enter_context(nc.semaphore(name))

        xt = sb("xt", [HC, 2, L])
        bc = sb("bc", [128, 2, 2, L])
        z_sb = sb("z_sb", [HC, L])
        sp_e = sb("sp_e", [HC, L])
        dt = sb("dt", [HC, 2, L])
        rest = sb("rest", [HC, 2, L])
        parts = sb("parts", [HC, 2, QPART, L], BF16)
        stack = sb("stack", [HC, 2, 2, NBLK, L], BF16)
        dbu = sb("dbu", [128, 3, CH])
        HR = 6
        hs = sb("hs", [128, HR, L])
        AR = 3
        psA = ctx.enter_context(nc.psum_tensor("psA", [128, AR, CH], F32))
        psU = ctx.enter_context(nc.psum_tensor("psU", [128, 2, CH], F32))
        psY = ctx.enter_context(nc.psum_tensor("psY", [128, 2, CH], F32))
        psP = ctx.enter_context(nc.psum_tensor("psP", [128, CH], F32))

        dt_spread = sem("dt_spread")
        dtu_spread = sem("dtu_spread")
        decay_ready = sem("decay_ready")
        dbu_ready = sem("dbu_ready")
        scan_done = sem("scan_done")
        hc_ready = sem("hc_ready")
        summed = sem("summed")
        y_taken = sem("y_taken")
        z_proj = sem("z_proj")
        bc_proj = sem("bc_proj")
        z_taken = sem("z_taken")
        log_ready = sem("log_ready")
        abs_own, exp_own = sem("abs_own"), sem("exp_own")
        dt_own = sem("dt_own")
        dt_ready = sem("dt_ready")
        bc_ready = sem("bc_ready")
        hi_ready = sem("hi_ready")
        rest_ready = sem("rest_ready")
        mid_ready = sem("mid_ready")
        lo_ready = sem("lo_ready")
        xt_half = sem("xt_half")
        stacked = [sem(f"stacked{p}") for p in range(2)]

        def order(ui):
            p, r, f = ui // 4, ui // 2 % 2, ui % 2
            return p, r, f, p + 2 * r

        def landed(b, ui):
            return (b * (UNITS // 2) + ui // 2 + 1) * (16 * QPART * NBLK)

        Z_PE = {12: (0, 0), 13: (0, 1), 14: (1, 0), 15: (1, 1)}
        BC_PE = {q: (i // 2, i % 2) for i, q in enumerate((0, 1, 2, 3, 6, 7, 8, 9))}

        BC_ACT = (1, 3, 7, 9)
        EARLY = (psA[:, 2, :], psU[:, 0, :], psU[:, 1, :], psP[:, :])

        def source(nb, nu):
            p, r, f, k = order(nu)
            return (lambda h, lo: xt[:, h, lo:lo + CH]) if p else (lambda h, lo: s.X[:, nb, h, lo:lo + CH])

        def units_ahead(b, ui, d):
            return b + (ui + d) // UNITS, (ui + d) % UNITS, b * UNITS + (ui + d)

        with nc.Block() as block:
            @block.tensor
            def _(pe):
                pe.sem_inc(dbu_ready, 2)
                pe.sem_inc(scan_done, 2 + START)
                pe.sem_inc(summed, 1 + START + (SUB - 2))
                for first in (y_taken, hc_ready, dt_spread, dt_ready):
                    pe.sem_inc(first, START)

                def project(out, wt, rhs, h, ready):
                    m = pe.matmul(out, wt, rhs, start=(h == 0), stop=(h == 1))
                    if h == 1:
                        m.then_inc(ready, 1)

                def z_side(q, nb, nu, n1, kk):
                    if q not in Z_PE:
                        return
                    c, h = Z_PE[q]
                    p, r, f, k = order(nu)
                    if h == 0:
                        if c:
                            pe.wait_ge(z_taken, n1 * 2 + 1)
                        elif kk is not None:
                            pe.wait_ge(bc_ready, kk * 4 + 4)
                        elif not isinstance(n1, int):
                            pe.wait_ge(z_taken, n1 * 2)
                        if p:
                            pe.wait_ge(xt_half, nb * 2 + 2)
                    project(psP[0:HC, :], s.w_dt[:, k, h, HC * f:HC * f + HC], source(nb, nu)(h, CH * c), h, z_proj)

                def bc_side(q, nb, nu, n1, kk):
                    if q not in BC_PE:
                        return
                    i, h = BC_PE[q]
                    p, r, f, k = order(nu)
                    if h == 0:
                        if i:
                            pe.wait_ge(bc_ready, kk * 4 + i)
                        else:
                            pe.wait_ge(z_taken, n1 * 2 + 2)
                        if p:
                            pe.wait_ge(xt_half, nb * 2 + 2)
                    project(psP[:, :], (s.w_b, s.w_c)[i // 2][:, k, h, :], source(nb, nu)(h, CH * (i % 2)), h, bc_proj)

                def sum_states(n, trip, c, first=0):
                    if c == 0:
                        if trip == 0:
                            pe.wait_ge(y_taken, n + (1 + START))
                        pe.wait_ge(hc_ready, n * TILES + (TILES + 3 * trip + 3 + START))
                    for j in range(NBLK):
                        slot = (3 * trip + j) % HR
                        m = pe.matmul(psY[BLK * j:BLK * j + BLK, c, :], s.state_sel[:, trip, :],
                                      hs[:, slot, CH * c:CH * c + CH], start=(trip == first), stop=(trip == SUB - 1))
                    if c == 1:
                        m.then_inc(summed, 1)

                def early_z(nu, c):
                    for h in range(2):
                        project(psA[0:HC, c, :], s.w_dt[:, 0, h, HC * nu:HC * nu + HC], source(0, nu)(h, CH * c), h, z_proj)

                for c in range(2):
                    early_z(0, c)
                for i in range(4):
                    for h in range(2):
                        project(EARLY[i], (s.w_b, s.w_c)[i // 2][:, 0, h, :], source(0, 0)(h, CH * (i % 2)), h, bc_proj)
                for c in range(2):
                    pe.wait_ge(z_taken, c + 1)
                    early_z(1, c)
                for c in range(2):
                    sum_states(-1, SUB - 2, c, first=SUB - 2)
                pe.wait_ge(z_taken, 4)
                pe.wait_ge(bc_ready, 4)
                with pe.Fori(0, NB, 1) as b:
                    for ui in range(UNITS):
                        n = b * UNITS + ui
                        p, r, f, k = order(ui)
                        pe.wait_ge(stacked[ui % 2], landed(b, ui))
                        for t in range(TILES):
                            gg, j = t // NBLK, t % NBLK
                            for c in range(2):
                                q = 2 * t + c
                                pos = c if r == 0 else 1 - c
                                g = n * (2 * TILES) + q
                                pe.wait_ge(dbu_ready, g + 1)
                                pe.matmul(psU[:, q % 2, :], s.spread_sel[:, gg, :],
                                          stack[:, ui % 2, 1, j, CH * pos:CH * pos + CH],
                                          start=True, stop=True).then_inc(dtu_spread, 1)
                                pe.wait_ge(scan_done, g + START)
                                pe.matmul(psA[:, q % AR, :], s.spread_sel[:, gg, :],
                                          stack[:, ui % 2, 0, j, CH * pos:CH * pos + CH],
                                          start=True, stop=True).then_inc(dt_spread, 1)
                                if ui % 2:
                                    bc_side(q, *units_ahead(b, ui, 1), b * K + (ui + 1) // 2)
                                z_side(q, *units_ahead(b, ui, 2), b * K + (ui + 1) // 2 if ui % 2 else None)
                                if t % 3 == 2:
                                    if t > 3:
                                        sum_states(n, t // 3 - 1, c)
                                    else:
                                        sum_states(n - 1, SUB - 1, c)
                for c in range(2):
                    sum_states(NB * UNITS - 1, SUB - 1, c)

            @block.scalar
            def _(act):
                def z_side(q, nb, nu, n1, early=False):
                    p, r, f, k = order(nu)
                    if q in (13, 15):
                        c = (q - 13) // 2
                        cs = slice(CH * c, CH * c + CH)
                        bank = psA[0:HC, c, :] if early else psP[0:HC, :]
                        bias = s.cols[:, COL_DTB + 2 * k + f:COL_DTB + 2 * k + f + 1]
                        act.wait_ge(z_proj, n1 * 2 + c + 1)
                        act.wait_ge(dt_own, n1 * 2)
                        nc.scalar.activation(z_sb[:, cs], bank, ACT.Identity, bias=bias).then_inc(z_taken, 1)
                    if q in (14, 16):
                        c = (q - 14) // 2
                        cs = slice(CH * c, CH * c + CH)
                        act.wait_ge(z_taken, n1 * 2 + c + 1)
                        nc.scalar.activation(sp_e[:, cs], z_sb[:, cs], ACT.Abs).then_inc(abs_own, 1)
                    if q in (17, 20):
                        c = (q - 17) // 3
                        act.wait_ge(abs_own, n1 * 2 + c + 1)
                        e = sp_e[:, CH * c:CH * c + CH]
                        nc.scalar.activation(e, e, ACT.Exp, scale=-1.0).then_inc(exp_own, 1)
                        act.wait_ge(exp_own, n1 * 2 + c + 1)
                        nc.scalar.activation(e, e, ACT.Ln, bias=s.one[0:HC, :]).then_inc(log_ready, 1)

                def bc_side(q, nu, kk, early=False):
                    if q in BC_ACT:
                        i = BC_ACT.index(q)
                        act.wait_ge(bc_proj, kk * 4 + i + 1)
                        if i == 0 and not isinstance(kk, int):
                            act.wait_ge(hc_ready, (kk - 1) * (2 * TILES) + (TILES + START))
                        nc.scalar.copy(bc[:, nu // 2 % 2, i // 2, CH * (i % 2):CH * (i % 2) + CH],
                                       EARLY[i] if early else psP[:, :]).then_inc(bc_ready, 1)

                def split_side(q, n1, b, ui):
                    if q == 0:
                        act.wait_ge(dt_ready, n1 * 2 + 2 + START)
                        if ui is not None:
                            act.wait_ge(stacked[ui % 2], landed(b, ui))
                        for tq in range(2):
                            nc.scalar.copy(parts[:, tq, 0, :], dt[:, tq, :]).then_inc(hi_ready, 1)
                    if q in (6, 10):
                        tq = (q - 6) // 4
                        act.wait_ge(rest_ready, n1 * 2 + tq + 1)
                        nc.scalar.copy(parts[:, tq, 1, :], rest[:, tq, :]).then_inc(mid_ready, 1)

                nc.scalar.preload_act_table_set("natural_log_exp_and_others")
                for q in (13, 14, 15, 16, 17, 20):
                    z_side(q, 0, 0, 0, early=True)
                split_side(0, 0, 0, None)
                bc_side(1, 0, 0, early=True)
                split_side(6, 0, 0, None)
                bc_side(3, 0, 0, early=True)
                split_side(10, 0, 0, None)
                bc_side(7, 0, 0, early=True)
                bc_side(9, 0, 0, early=True)
                for q in (13, 14, 15, 16, 17, 20):
                    z_side(q, 0, 1, 1, early=True)
                with act.Fori(0, NB, 1) as b:
                    for ui in range(UNITS):
                        n = b * UNITS + ui
                        p, r, f, k = order(ui)
                        for t in range(TILES):
                            gg, j = t // NBLK, t % NBLK
                            col = k * (D // DD) + TILES * f + SUB * j + gg
                            for c in range(2):
                                q = 2 * t + c
                                g = n * (2 * TILES) + q
                                act.wait_ge(dt_spread, g + 1 + START)
                                nc.scalar.activation(psA[:, q % AR, :], psA[:, q % AR, :], ACT.Exp,
                                                     scale=s.a_neg[:, col:col + 1]).then_inc(decay_ready, 1)
                                if ui % 2:
                                    bc_side(q, (ui + 1) % UNITS, b * K + (ui + 1) // 2)
                                split_side(q, n + 1, b, ui)
                                z_side(q, *units_ahead(b, ui, 2))
                                if ui == 1 and q in (21, 22):
                                    h = q - 21
                                    act.wait_ge(dt_ready, b * (2 * UNITS) + START)
                                    nc.scalar.copy(xt[:, h, :].rearrange("p (w h) -> p w h", w=WW),
                                                   s.X[:, b, h, :].rearrange("p (h w) -> p w h", h=HH)
                                                   ).then_inc(xt_half, 1)

            @block.gpsimd
            def _(pool):
                def split_side(t, n1):
                    for tq in range(2):
                        if t == 2 * tq:
                            pool.wait_ge(hi_ready, n1 * 2 + tq + 1)
                            pool.wait_ge(mid_ready, n1 * 2)
                            pool.wait_ge(lo_ready, n1 * 3)
                            pool.tensor_tensor(rest[:, tq, :], dt[:, tq, :], parts[:, tq, 0, :],
                                               ALU.subtract).then_inc(rest_ready, 1)
                        if t == 5 + 2 * tq:
                            cs = slice(0, (2 - tq) * CH)
                            pool.wait_ge(mid_ready, n1 * 2 + tq + 1)
                            pool.tensor_tensor(parts[:, tq, 2, cs], rest[:, tq, cs], parts[:, tq, 1, cs],
                                               ALU.subtract).then_inc(lo_ready, 1)

                pool.memset(hs[:], 0.0).then_inc(hc_ready, TILES)
                for t in (0, 2, 5, 7):
                    split_side(t, 0)
                with pool.Fori(0, NB, 1) as b:
                    for ui in range(UNITS):
                        n = b * UNITS + ui
                        kslot = ui // 2 % 2
                        pool.wait_ge(bc_ready, (b * K + ui // 2 + 1) * 4)
                        for t in range(TILES):
                            m = n * TILES + t
                            pool.wait_ge(scan_done, 2 * m + 2 + 2 + START)
                            h = hs[:, t % HR, :]
                            pool.tensor_tensor(h, h, bc[:, kslot, 1, :], ALU.mult).then_inc(hc_ready, 1)
                            split_side(t, n + 1)

            @block.vector
            def _(v):
                own = [0]

                def z_side(q, nb, nu, n1):
                    p, r, f, k = order(nu)
                    if q in (19, 22):
                        c = (q - 19) // 3
                        cs = slice(CH * c, CH * c + CH)
                        v.wait_ge(log_ready, n1 * 2 + c + 1)
                        v.wait_ge(rest_ready, n1 * 2)
                        v.scalar_tensor_tensor(out=dt[:, 0, cs], in0=z_sb[:, cs], scalar=0.0, in1=sp_e[:, cs],
                                               op0=ALU.max, op1=ALU.add).then_inc(dt_own, 1)
                        v.wait_ge(dt_own, n1 * 2 + c + 1)
                        v.tensor_tensor(dt[:, 1, cs], dt[:, 0, cs], source(nb, nu)(f, CH * c),
                                        ALU.mult).then_inc(dt_ready, 1)

                def product(n, ui, q, b):
                    p, r, f, k = order(ui)
                    g = n * (2 * TILES) + q
                    pos = q % 2 if r == 0 else 1 - q % 2
                    if q == 0 and ui % 2 == 0:
                        v.wait_ge(bc_ready, (b * K + ui // 2 + 1) * 4)
                    v.wait_ge(dtu_spread, g + 1)
                    v.wait_ge(scan_done, g + START)
                    v.tensor_tensor(dbu[:, q % 3, :], psU[:, q % 2, :],
                                    bc[:, ui // 2 % 2, 0, CH * pos:CH * pos + CH], ALU.mult).then_inc(dbu_ready, 1)

                def take(n, b, ui):
                    p, r, f, k = order(ui)
                    v.wait_ge(summed, n * SUB + (2 * SUB + 1 + START))
                    acc = psY[0:HC, :, :].rearrange("p c l -> p (c l)")
                    y = s.Y[:, b, f, :]
                    if p == 0 and r == 0:
                        v.scalar_tensor_tensor(out=y, in0=s.X[:, b, f, :], scalar=s.d_sum[:, f:f + 1], in1=acc,
                                               op0=ALU.mult, op1=ALU.add).then_inc(y_taken, 1)
                    elif p == 0:
                        v.tensor_tensor(y, y, acc, ALU.add).then_inc(y_taken, 1)
                    else:
                        yt = y.rearrange("p (h w) -> p w h", h=HH)
                        v.tensor_tensor(yt, yt, acc.rearrange("p (w h) -> p w h", w=WW), ALU.add).then_inc(y_taken, 1)

                def split_side(q, n1):
                    if q == 13:
                        v.wait_ge(mid_ready, n1 * 2 + 2)
                        v.tensor_tensor(parts[:, 1, 2, CH:L], rest[:, 1, CH:L], parts[:, 1, 1, CH:L],
                                        ALU.subtract).then_inc(lo_ready, 1)

                for n1 in range(2):
                    for q in (19, 22):
                        z_side(q, 0, n1, n1)
                    if n1 == 0:
                        split_side(13, 0)
                with v.Fori(0, NB, 1) as b:
                    for ui in range(UNITS):
                        n = b * UNITS + ui
                        p, r, f, k = order(ui)
                        product(n, ui, 0, b)
                        for q in range(2 * TILES):
                            t = q // 2
                            g = n * (2 * TILES) + q
                            if q + 1 < 2 * TILES:
                                product(n, ui, q + 1, b)
                            pos = q % 2 if r == 0 else 1 - q % 2
                            if q % 6 == 0:
                                v.wait_ge(summed, n * SUB + (SUB + q // 6 + START))
                            v.wait_ge(decay_ready, g + 1)
                            v.wait_ge(dbu_ready, g + 1 + 2)
                            if q % 2:
                                v.wait_ge(scan_done, g + 2 + START)
                            h = hs[:, t % HR, CH * pos:CH * pos + CH]
                            da, du = psA[:, q % AR, :], dbu[:, q % 3, :]
                            if r:
                                h, da, du = h[:, ::-1], da[:, ::-1], du[:, ::-1]
                            if q % 2 == 0:
                                init = 0.0
                            else:
                                at = CH - 1 if r == 0 else CH
                                init = hs[:, t % HR, at:at + 1]
                            v.tensor_tensor_scan(h, da, du, init, ALU.mult, ALU.add).then_inc(scan_done, 1)
                            if q == 7:
                                take(n - 1, b if ui else (b + (NB - 1)) % NB, (ui - 1) % UNITS)
                            z_side(q, *units_ahead(b, ui, 2))
                            split_side(q, n + 1)
                take(NB * UNITS - 1, NB - 1, UNITS - 1)

            @block.sync
            def _(sp):
                def stack_up(n1, slot):
                    for part, ready in enumerate((hi_ready, mid_ready, lo_ready)):
                        sp.wait_ge(ready, n1 * 3 + 3 if part == 2 else n1 * 2 + 2)
                        for j in range(NBLK):
                            sp.dma_start(stack[BLK * part:BLK * part + BLK, slot, :, j, :],
                                         parts[BLK * j:BLK * j + BLK, :, part, :]).then_inc(stacked[slot], 16)

                stack_up(0, 0)
                with sp.Fori(0, NB, 1) as b:
                    for ui in range(UNITS):
                        n = b * UNITS + ui
                        sp.wait_ge(dt_spread, n * (2 * TILES) + START)
                        stack_up(n + 1, (ui + 1) % 2)
                sp.wait_ge(stacked[0], landed(NB, 0))


def layer_norm(nc, s, src, dst, tag, after=None):
    with ExitStack() as ctx:
        def sb(name, shape, dt=F32):
            return ctx.enter_context(nc.sbuf_tensor(tag + name, shape, dt))

        def sem(name):
            return ctx.enter_context(nc.semaphore(tag + name))

        both = sb("both", [HC, 2, CH])
        sq = sb("sq", [HC, 2, 2, CH])
        dev = sb("dev", [HC, 3, CH])
        ps_mean = ctx.enter_context(nc.psum_tensor(tag + "ps_mean", [HC, 2, CH], F32))
        ps_var = ctx.enter_context(nc.psum_tensor(tag + "ps_var", [HC, 2, CH], F32))
        mean_ready, var_ready = sem("mean_ready"), sem("var_ready")
        centred, normed = sem("centred"), sem("normed")
        squared, log_ready, dev_ready = sem("squared"), sem("log_ready"), sem("dev_ready")
        both_ready, sq_ready = sem("both_ready"), sem("sq_ready")
        STEPS = 2 * NB

        def part(t, i, f):
            return t[:, i // 2, f, CH * (i % 2):CH * (i % 2) + CH]

        more = after(ctx, sb, sem, normed) if after else {}
        with nc.Block() as block:
            @block.tensor
            def _(pe):
                for i in range(STEPS + 1):
                    if i < STEPS:
                        if i >= 2:
                            pe.wait_ge(centred, i - 1)
                        pe.wait_ge(both_ready, i + 1)
                        pe.matmul(ps_mean[:, i % 2, :], s.average[:], both[:, i % 2, :], start=True, stop=True
                                  ).then_inc(mean_ready, 1)
                    if i:
                        pe.wait_ge(sq_ready, i)
                        if i >= 3:
                            pe.wait_ge(log_ready, i - 2)
                        pe.matmul(ps_var[:, (i - 1) % 2, :], s.average[:], sq[:, (i - 1) % 2, 0, :], start=True, stop=True
                                  ).then_inc(var_ready, 1)

            @block.vector
            def _(v):
                if "load" in more:
                    more["load"](v)
                for i in range(STEPS + 2):
                    if i < STEPS:
                        v.wait_ge(mean_ready, i + 1)
                        for f in range(2):
                            m = v.tensor_tensor(part(dst, i, f), part(src, i, f), ps_mean[:, i % 2, :], ALU.subtract)
                        m.then_inc(centred, 1)
                    if i >= 2:
                        v.wait_ge(dev_ready, i - 1)
                        v.wait_ge(centred, i - 1)
                        d = dev[:, (i - 2) % 3, :]
                        for f in range(2):
                            m = v.tensor_tensor(part(dst, i - 2, f), part(dst, i - 2, f), d, ALU.mult)
                        m.then_inc(normed, 1)
                if "vector" in more:
                    more["vector"](v)

            @block.scalar
            def _(act):
                nc.scalar.preload_act_table_set("natural_log_exp_and_others")
                for i in range(STEPS + 1):
                    if i < STEPS:
                        act.wait_ge(centred, i + 1)
                        if i >= 2:
                            act.wait_ge(var_ready, i - 1)
                        for f in range(2):
                            m = nc.scalar.activation(sq[:, i % 2, f, :], part(dst, i, f), ACT.Square)
                        m.then_inc(squared, 1)
                    if i:
                        act.wait_ge(var_ready, i)
                        if i >= 4:
                            act.wait_ge(normed, i - 3)
                        d = dev[:, (i - 1) % 3, :]
                        nc.scalar.activation(d, ps_var[:, (i - 1) % 2, :], ACT.Ln, bias=s.eps5[0:HC, :]).then_inc(log_ready, 1)
                        act.wait_ge(log_ready, i)
                        nc.scalar.activation(d, d, ACT.Exp, scale=-0.5).then_inc(dev_ready, 1)
                if "scalar" in more:
                    more["scalar"](act)

            @block.gpsimd
            def _(pool):
                if "clear" in more:
                    more["clear"](pool)
                for i in range(STEPS + 1):
                    if i < STEPS:
                        if i >= 2:
                            pool.wait_ge(mean_ready, i - 1)
                        pool.tensor_tensor(both[:, i % 2, :], part(src, i, 0), part(src, i, 1), ALU.add).then_inc(both_ready, 1)
                    if i:
                        pool.wait_ge(squared, i)
                        q = sq[:, (i - 1) % 2, :, :]
                        pool.tensor_tensor(q[:, 0, :], q[:, 0, :], q[:, 1, :], ALU.add).then_inc(sq_ready, 1)
                if "gpsimd" in more:
                    more["gpsimd"](pool)

            if "sync" in more:
                @block.sync
                def _(sp):
                    more["sync"](sp)


def conv_out(nc, w, s):
    def after(ctx, sb, sem, normed):
        x_in = [sem(f"x_again{b}") for b in range(NB)]
        gelu_done = sem("gelu_done")
        cleared = sem("cleared")

        def gpsimd(pool):
            pool.memset(s.V[:], 0.0).then_inc(cleared, 1)
            pool.wait_ge(cleared, 1)
            pool.memset(s.V[:, :, :, :, DH:DH + 1].rearrange("p b t h o -> p (b t) (h o)"), 1.0)

        def scalar(act):
            act.wait_ge(normed, 2 * NB)
            for b in range(NB):
                for f in range(2):
                    nc.scalar.activation(s.Z[:, b, f, :], s.Z[:, b, f, :], ACT.Gelu,
                                         bias=s.cols[:, COL_LNB + f:COL_LNB + f + 1],
                                         scale=s.cols[:, COL_LNW + f:COL_LNW + f + 1]).then_inc(gelu_done, 1)

        def vector(v):
            for b in range(NB):
                v.wait_ge(x_in[b], 16)
                for f in range(2):
                    v.wait_ge(gelu_done, 2 * b + f + 1)
                    v.tensor_tensor(s.Y[:, b, f, :], s.raw[:, b, f, :], s.Z[:, b, f, :], ALU.add)

        def sync(sp):
            for b in range(NB):
                sp.dma_start(s.raw[:, b, :, :], w.x[b].rearrange("(f p) h w -> p f (h w)", p=HC)).then_inc(x_in[b], 16)

        return {"scalar": scalar, "vector": vector, "sync": sync, "gpsimd": gpsimd}

    layer_norm(nc, s, s.Y, s.Z, "lc_", after)


def qkv(nc, w, s):
    with ExitStack() as ctx:
        def sb(name, shape, dt=F32):
            return ctx.enter_context(nc.sbuf_tensor(name, shape, dt))

        def sem(name):
            return ctx.enter_context(nc.semaphore(name))

        w_rows = sb("w_rows", [HC, 6, D])
        w_qkv = sb("w_qkv", [HC, 2, 3 * D])
        vb = sb("vb", [128, D])
        qb = sb("qb", [HC, 4])
        p_rows = sb("p_rows", [HC, 2, D])
        p_pad = sb("p_pad", [HC, 2, 3, 4, 32])
        SLOTS = 3
        val = sb("val", [HC, SLOTS, L])
        rest = sb("qrest", [HC, SLOTS, L])
        parts = sb("qparts", [HC, SLOTS, QPART, L], BF16)
        hankel = sb("hankel", [19, 19, HEADS])
        last_row = sb("last_row", [19, HEADS])
        RING = 4
        ps_w = ctx.enter_context(nc.psum_tensor("ps_w", [128, RING, CH], F32))
        VRING = 2
        ps_v = ctx.enter_context(nc.psum_tensor("ps_v", [128, VRING, CH], F32))
        ps_mean = ctx.enter_context(nc.psum_tensor("ps_mean", [HC, CH], F32))
        ps_var = ctx.enter_context(nc.psum_tensor("ps_var", [HC, CH], F32))
        both = sb("both", [HC, 2, CH])
        sq = sb("sq", [HC, 2, 2, CH])
        dev = sb("dev", [HC, 2, CH])
        w_in, vb_in, p_in, tab_ext, tab_in, last_in = (
            sem("w_in"), sem("vb_in"), sem("p_in"), sem("tab_ext"), sem("tab_in"), sem("last_in"))
        pool_ready, w_turned, w_taken, q_proj, q_taken, v_proj, v_taken = (
            sem("pool_ready"), sem("w_turned"), sem("w_taken"), sem("q_proj"), sem("q_taken"), sem("v_proj"), sem("v_taken"))
        own_v, hi_ready, rest_ready, mid_ready, lo_ready, padded, corner, corner_turned = (
            sem("own_v"), sem("qhi"), sem("qrestr"), sem("qmid"), sem("qlo"), sem("padded"), sem("corner"), sem("corner_turned"))
        both_ready, sq_ready = sem("both_ready"), sem("sq_ready")
        mean_ready, var_ready = sem("mean_ready"), sem("var_ready")
        centred, normed = sem("centred"), sem("normed")
        squared, log_ready, dev_ready = sem("squared"), sem("log_ready"), sem("dev_ready")
        stored = [sem(f"stored{i}") for i in range(SLOTS)]
        NQ = 4 * NB

        def chunk(t, c):
            return t[:, c // 2, :, CH * (c % 2):CH * (c % 2) + CH]

        def norm_step(i, first, second):
            b, x = i // 4, i % 4
            if b + 1 < NB:
                (second if x % 2 else first)(2 * (b + 1) + x // 2)

        with nc.Block() as block:
            @block.sync
            def _(sp):
                sp.dma_start(w_rows[:], w.qkvw.rearrange("(m p) d -> p m d", p=HC)).then_inc(w_in, 16)
                sp.dma_start(vb[:], w.qkvb[2 * D:3 * D].rearrange("(o d) -> o d", o=1).broadcast_to([128, D])).then_inc(vb_in, 16)
                sp.dma_start(p_rows[:], w.projw.rearrange("(m p) d -> p m d", p=HC)).then_inc(p_in, 16)
                sp.dma_start(s.ext[0:19, :], w.table).then_inc(tab_ext, 16)
                sp.dma_start(s.ext[19:37, :], w.table[0:18, :]).then_inc(tab_ext, 16)
                sp.dma_start(last_row[:], w.table[18:19, :].broadcast_to([19, HEADS])).then_inc(last_in, 16)
                sp.wait_ge(tab_ext, 32)
                win = bass.AP(s.ext[:, :].tensor, 0, [[HEADS, 19], [1, 19 * HEADS]])
                sp.dma_start(hankel[:].rearrange("p e h -> p (e h)"), win).then_inc(tab_in, 16)
                for i in range(NQ):
                    b, qk, f = i // 4, i // 2 % 2, i % 2
                    sp.wait_ge(lo_ready, i + 1)
                    sp.wait_ge(mid_ready, i + 1)
                    sp.dma_start(s.qk_dram[b, qk, :, HC * f:HC * f + HC, :].rearrange("a p l -> p a l"),
                                 parts[:, i % SLOTS, :, :]).then_inc(stored[i % SLOTS], 16)
                for i in range(SLOTS):
                    sp.wait_ge(stored[i], 16 * len(range(i, NQ, SLOTS)))

            @block.gpsimd
            def _(pool):
                def add_halves(c):
                    if c >= 2:
                        pool.wait_ge(mean_ready, c - 1)
                    y = chunk(s.Y, c)
                    pool.tensor_tensor(both[:, c % 2, :], y[:, 0, :], y[:, 1, :], ALU.add).then_inc(both_ready, 1)

                def add_squares(c):
                    pool.wait_ge(squared, c + 1)
                    q = sq[:, c % 2, :, :]
                    pool.tensor_tensor(q[:, 0, :], q[:, 0, :], q[:, 1, :], ALU.add).then_inc(sq_ready, 1)

                for stage in (add_halves, add_squares):
                    for c in range(2):
                        stage(c)
                pool.memset(p_pad[:], 0.0).then_inc(pool_ready, 1)
                pool.memset(s.shift[:], 0.0).then_inc(pool_ready, 1)
                pool.wait_ge(pool_ready, 2)
                pool.affine_select(out=s.shift[:], in_=s.shift[:], compare_op=ALU.not_equal, fill=1.0, base=128 - 19,
                                   pattern=[[-1, 128]], channel_multiplier=1).then_inc(pool_ready, 1)
                for c in range(2, 2 * NB):
                    add_halves(c)
                    add_squares(c)
                pool.wait_ge(corner, 2)
                pool.affine_select(out=s.corner_q[:], in_=s.corner_q[:], compare_op=ALU.is_ge, fill=0.0, base=0,
                                   pattern=[[0, HEADS], [1, 19]], channel_multiplier=-1).then_inc(corner, 1)

            @block.tensor
            def _(pe):
                def mean(c):
                    pe.wait_ge(both_ready, c + 1)
                    if c:
                        pe.wait_ge(centred, c)
                    pe.matmul(ps_mean[:, :], s.average[:], both[:, c % 2, :], start=True, stop=True).then_inc(mean_ready, 1)

                def variance(c):
                    pe.wait_ge(sq_ready, c + 1)
                    if c:
                        pe.wait_ge(log_ready, c)
                    pe.matmul(ps_var[:, :], s.average[:], sq[:, c % 2, 0, :], start=True, stop=True).then_inc(var_ready, 1)

                for c in range(2):
                    mean(c)
                pe.wait_ge(w_in, 16)
                for m in range(6):
                    for f in range(2):
                        t = pe.transpose(ps_w[0:HC, 2 * f + m // 3, HC * (m % 3):HC * (m % 3) + HC],
                                         w_rows[:, m, HC * f:HC * f + HC], s.ident[0:HC, 0:HC])
                t.then_inc(w_turned, 1)
                for c in range(2):
                    variance(c)
                pe.wait_ge(w_taken, 1)
                nv = 0
                for b in range(NB):
                    pe.wait_ge(normed, 2 * (b + 1))
                    for j in range(8):
                        if j % 2 == 0:
                            norm_step(4 * b + j // 2, mean, variance)
                        i = 8 * b + j
                        qk, f, c = j // 4, j // 2 % 2, j % 2
                        if i >= RING:
                            pe.wait_ge(q_taken, i - RING + 1)
                        for h in range(2):
                            t = pe.matmul(ps_w[0:HC, i % RING, :], w_qkv[:, h, D * qk + HC * f:D * qk + HC * f + HC],
                                          s.Z[:, b, h, CH * c:CH * c + CH], start=(h == 0), stop=(h == 1))
                        t.then_inc(q_proj, 1)
                        if nv >= VRING:
                            pe.wait_ge(v_taken, nv - VRING + 1)
                        for h in range(2):
                            t = pe.matmul(ps_v[:, nv % VRING, 0:D], s.Z[:, b, h, 128 * j:128 * j + 128],
                                          w_qkv[:, h, 2 * D:3 * D], start=(h == 0), stop=(h == 1))
                        t.then_inc(v_proj, 1)
                        nv += 1
                pe.wait_ge(q_taken, 8 * NB)
                pe.wait_ge(padded, 1)
                for g in range(3):
                    for f in range(2):
                        t = pe.transpose(ps_w[:, g, HC * f:HC * f + HC],
                                         p_pad[:, f, g, :, :].rearrange("p j c -> p (j c)"), s.ident[0:HC, 0:HC])
                pe.wait_ge(corner, 3)
                for h in range(HEADS):
                    t = pe.transpose(ps_w[0:19, 3, 19 * h:19 * h + 19], s.corner_q[:, h, :], s.ident[0:19, 0:19])
                t.then_inc(corner_turned, 1)

            @block.scalar
            def _(act):
                def square(c):
                    act.wait_ge(centred, c + 1)
                    if c >= 2:
                        act.wait_ge(var_ready, c - 1)
                    nc.scalar.activation(sq[:, c % 2, :, :], chunk(s.Z, c), ACT.Square).then_inc(squared, 1)

                def invert(c):
                    act.wait_ge(var_ready, c + 1)
                    if c >= 2:
                        act.wait_ge(normed, c - 1)
                    d = dev[:, c % 2, :]
                    nc.scalar.activation(d, ps_var[:, :], ACT.Ln, bias=s.eps5[0:HC, :]).then_inc(log_ready, 1)
                    act.wait_ge(log_ready, c + 1)
                    nc.scalar.activation(d, d, ACT.Exp, scale=-0.5).then_inc(dev_ready, 1)

                nc.scalar.preload_act_table_set("natural_log_exp_and_others")
                for stage in (square, invert):
                    for c in range(2):
                        stage(c)
                for i in range(NQ):
                    b, qk, f = i // 4, i // 2 % 2, i % 2
                    norm_step(i, square, invert)
                    act.wait_ge(own_v, 1)
                    if i >= SLOTS:
                        act.wait_ge(rest_ready, i - SLOTS + 1)
                    for c in range(2):
                        act.wait_ge(q_proj, 2 * i + c + 1)
                        nc.scalar.activation(val[:, i % SLOTS, CH * c:CH * c + CH], ps_w[0:HC, (2 * i + c) % RING, :], ACT.Identity,
                                             bias=qb[:, 2 * qk + f:2 * qk + f + 1], scale=(DH ** -0.5 if qk == 0 else 1.0)
                                             ).then_inc(q_taken, 1)
                    act.wait_ge(q_taken, 2 * i + 2)
                    if i >= SLOTS:
                        act.wait_ge(stored[i % SLOTS], 16 * (i // SLOTS))
                    nc.scalar.copy(parts[:, i % SLOTS, 0, :], val[:, i % SLOTS, :]).then_inc(hi_ready, 1)
                    if i:
                        act.wait_ge(rest_ready, i)
                        nc.scalar.copy(parts[:, (i - 1) % SLOTS, 1, :], rest[:, (i - 1) % SLOTS, :]).then_inc(mid_ready, 1)
                act.wait_ge(rest_ready, NQ)
                nc.scalar.copy(parts[:, (NQ - 1) % SLOTS, 1, :], rest[:, (NQ - 1) % SLOTS, :]).then_inc(mid_ready, 1)

            @block.vector
            def _(v):
                def centre(c):
                    v.wait_ge(mean_ready, c + 1)
                    v.tensor_tensor(chunk(s.Z, c), chunk(s.Y, c), ps_mean[:, :].unsqueeze(1).broadcast_to([HC, 2, CH]),
                                    ALU.subtract).then_inc(centred, 1)

                def scale(c):
                    v.wait_ge(dev_ready, c + 1)
                    v.wait_ge(centred, c + 1)
                    z = chunk(s.Z, c)
                    v.tensor_tensor(z, z, dev[:, c % 2, :].unsqueeze(1).broadcast_to([HC, 2, CH]), ALU.mult
                                    ).then_inc(normed, 1)

                for c in range(2):
                    centre(c)
                v.tensor_scalar(qb[:, 0:2], s.cols[:, COL_Q:COL_Q + 2], DH ** -0.5, None, ALU.mult)
                v.tensor_copy(qb[:, 2:4], s.cols[:, COL_K:COL_K + 2]).then_inc(own_v, 1)
                v.wait_ge(w_turned, 1)
                for f in range(2):
                    for g in range(2):
                        t = v.tensor_copy(w_qkv[:, f, 3 * HC * g:3 * HC * g + 3 * HC], ps_w[0:HC, 2 * f + g, 0:3 * HC])
                t.then_inc(w_taken, 1)
                for c in range(2):
                    scale(c)
                v.wait_ge(vb_in, 16)
                nv = 0
                for i in range(NQ + 1):
                    if i < NQ:
                        norm_step(i, centre, scale)
                        for _ in range(2):
                            v.wait_ge(v_proj, nv + 1)
                            v.tensor_tensor(s.V[:, nv // 8, nv % 8, :, 0:DH],
                                            ps_v[:, nv % VRING, 0:D].rearrange("p (h d) -> p h d", d=DH),
                                            vb[:].rearrange("p (h d) -> p h d", d=DH), ALU.add).then_inc(v_taken, 1)
                            nv += 1
                        v.wait_ge(hi_ready, i + 1)
                        if i >= SLOTS:
                            v.wait_ge(mid_ready, i - SLOTS + 1)
                        v.tensor_tensor(rest[:, i % SLOTS, :], val[:, i % SLOTS, :], parts[:, i % SLOTS, 0, :],
                                        ALU.subtract).then_inc(rest_ready, 1)
                    if i:
                        v.wait_ge(mid_ready, i)
                        v.tensor_tensor(parts[:, (i - 1) % SLOTS, 2, :], rest[:, (i - 1) % SLOTS, :],
                                        parts[:, (i - 1) % SLOTS, 1, :],
                                        ALU.subtract).then_inc(lo_ready, 1)
                v.wait_ge(p_in, 16)
                v.wait_ge(pool_ready, 1)
                for f in range(2):
                    v.tensor_copy(p_pad[:, f, :, :, 0:DH].rearrange("p g j c -> p (g j) c"),
                                  p_rows[:, f, :].rearrange("p (g c) -> p g c", c=DH))
                    t = v.tensor_copy(p_pad[:, f, 0, 0, DH:DH + 1], s.cols[:, COL_PB + f:COL_PB + f + 1])
                t.then_inc(padded, 1)
                v.wait_ge(tab_in, 16)
                v.wait_ge(last_in, 16)
                v.tensor_copy(s.corner_q[:], hankel[:].rearrange("p e h -> p h e")[:, :, ::-1]).then_inc(corner, 1)
                v.wait_ge(corner, 1)
                v.tensor_tensor(s.corner_q[:], s.corner_q[:], last_row[:].unsqueeze(2).broadcast_to([19, HEADS, 19]),
                                ALU.subtract).then_inc(corner, 1)
                v.wait_ge(corner_turned, 1)
                v.tensor_copy(s.corner_k[:].rearrange("p h j -> p (h j)"), ps_w[0:19, 3, 0:19 * HEADS])
                v.tensor_copy(s.w_proj[:], ps_w[:, 0:3, 0:D])


def attention(nc, w, s):
    with ExitStack() as ctx:
        def sb(name, shape, dt=F32):
            return ctx.enter_context(nc.sbuf_tensor(name, shape, dt))

        def sem(name):
            return ctx.enter_context(nc.semaphore(name))

        Q_PARTS, K_PARTS = [0, 0, 1, 1, 0, 2], [0, 1, 0, 1, 2, 0]
        KQ = DH * len(Q_PARTS)
        KM = KQ + QPART
        NHG = 3
        GH = 4
        KT = L // 128
        HALF = 2 * NHG * KT
        MAXES = GH * KT * 2

        qs = sb("qs", [KM, NHG, GH, L], BF16)
        ks = sb("ks", [KM, NHG, GH, L], BF16)
        mx = sb("mx", [128, NHG, MAXES])
        zero = sb("zero", [128, 32])
        top = sb("top", [128, 32])
        nm = sb("nm", [128, 2, 32])
        nmp = sb("nmp", [128, QPART, 32], BF16)
        nmt = sb("nmt", [QPART * 32, 128], BF16)
        P = sb("P", [128, 2, GH, CH])
        v_now = sb("v_now", [128, KT, HEADS, 32])
        o_raw = sb("o_raw", [128, 2, CH])
        rec = sb("rec", [128, CH])
        o_n = sb("o_n", [128, NHG, L])
        R = 3
        ps1 = ctx.enter_context(nc.psum_tensor("ps1", [128, R, CH], F32))
        ps2 = ctx.enter_context(nc.psum_tensor("ps2", [128, R, CH], F32))
        assert NHG * MAXES % R == 0 and HALF * GH % R == 0
        psO = ctx.enter_context(nc.psum_tensor("psO", [128, CH], F32))
        psM = ctx.enter_context(nc.psum_tensor("psM", [128, CH], F32))

        stack_in = [sem(f"stack_in{i}") for i in range(NHG)]
        rows_set = sem("rows_set")
        s1_ready = sem("s1_ready")
        max_done = sem("max_done")
        s2_ready = sem("s2_ready")
        exp_done = sem("exp_done")
        pv_done = sem("pv_done")
        o_taken = sem("o_taken")
        misc_ready = sem("misc_ready")
        misc_taken = sem("misc_taken")
        own = sem("own_at")
        top_ready = sem("top_ready")
        nmp_ready = sem("nmp_ready")
        nm_store, nm_in = sem("nm_store"), sem("nm_in")
        rec_ready = sem("rec_ready")
        on_ready = sem("on_ready")
        v_set = sem("v_set")
        OWN = 4

        MISC = 3 * NHG + 4
        PROJ = (3 * NHG - 1, 3 * NHG, 3 * NHG + 2, 3 * NHG + 3)
        LAST_SUMS = 3 * NHG + 1

        def step_ahead(b, hg, d):
            return b + (hg + d) // NHG, (hg + d) % NHG, b * NHG + hg + d

        LATER = [(0, hg, qc) for hg in range(NHG) for qc in range(2) if hg or qc] + [(1, 0, 0)]

        READ_AT, LOG_AT, INVERT_AT = (0, 2), (3, 1), (4, 1)
        NORM_AT = 4

        def ahead(qc, kt, before):
            if before:
                return [[MAXES // 2 * (1 - qc) + GH * kt + x] for x in range(GH)]
            return [[2 * (GH * kt + x), 2 * (GH * kt + x) + 1] for x in range(GH)]

        def in_psM(b, hg, qc):
            return b * MISC + (1 + 3 * hg + 1) if qc else b * MISC + (1 + 3 * hg - 1)

        with nc.Block() as block:
            @block.gpsimd
            def _(pool):
                pool.memset(ks[KQ:KM, :, :, :].rearrange("p g h l -> p (g h l)"), 1.0).then_inc(rows_set, 1)
                pool.wait_ge(rows_set, 1)
                pool.memset(zero[:], 0.0).then_inc(rows_set, 1)

                def split_max(i):
                    link = [0]

                    def done(ins):
                        link[0] += 1
                        ins.then_inc(own, 1)
                        pool.wait_ge(own, i * OWN + link[0])

                    pool.wait_ge(top_ready, i + 1)
                    if not isinstance(i, int):
                        pool.wait_ge(nm_in, i * 16)
                    done(pool.tensor_tensor(nm[:, 0, :], zero[:], top[:], ALU.subtract))
                    done(pool.tensor_tensor(nmp[:, 0, :], nm[:, 0, :], zero[:], ALU.add))
                    done(pool.tensor_tensor(nm[:, 1, :], nm[:, 0, :], nmp[:, 0, :], ALU.subtract))
                    done(pool.tensor_tensor(nmp[:, 1, :], nm[:, 1, :], zero[:], ALU.add))
                    pool.tensor_tensor(nmp[:, 2, :], nm[:, 1, :], nmp[:, 1, :], ALU.subtract).then_inc(nmp_ready, 1)

                def place(b, hg):
                    h = slice(GH * hg, GH * hg + GH)
                    pool.tensor_copy(v_now[:, :, h, :].rearrange("p t h d -> p t (h d)"),
                                     s.V[:, b, :, h, :].rearrange("p t h d -> p t (h d)")).then_inc(v_set, 1)

                pool.wait_ge(rows_set, 2)
                for hg in range(NHG):
                    place(0, hg)
                split_max(0)
                with pool.Fori(0, NB, 1) as b:
                    for hg in range(NHG):
                        split_max(b * NHG + (hg + 1))
                        pool.wait_ge(pv_done, (b * NHG + (hg + 1)) * (2 * KT) + 1 + START)
                        place((b + 1) % NB, hg)

            @block.sync
            def _(sp):
                def load(b, hg):
                    for j in range(len(Q_PARTS)):
                        for stack, qk, part in ((qs, 0, Q_PARTS[j]), (ks, 1, K_PARTS[j])):
                            sp.dma_start(stack[DH * j:DH * j + DH, hg, :, :],
                                         s.qk_dram[b, qk, part, DH * GH * hg:DH * GH * (hg + 1), :]
                                         .rearrange("(h c) l -> c h l", c=DH)).then_inc(stack_in[hg], 16)

                def maxima(i, hg):
                    sp.dma_start(s.nm_dram[:, :], nmt[:]).then_inc(nm_store, 16)
                    sp.wait_ge(nm_store, (i + 1) * 16)
                    sp.dma_start(qs[KQ:KM, hg, :, :].rearrange("p h l -> p (h l)"),
                                 s.nm_dram[:, :].rearrange("(a r) c -> a (r c)", a=QPART)).then_inc(nm_in, 16)
                    sp.wait_ge(nm_in, (i + 1) * 16)

                for hg in range(NHG):
                    load(0, hg)
                sp.wait_ge(misc_taken, 1)
                maxima(0, 0)
                with sp.Fori(0, NB, 1) as b:
                    for hg in range(NHG):
                        sp.wait_ge(misc_taken, b * MISC + (3 * hg + 2))
                        maxima(b * NHG + (hg + 1), (hg + 1) % NHG)
                        sp.wait_ge(s2_ready, (b * HALF + (hg + 1) * 2 * KT) * GH)
                        load((b + 1) % NB, hg)
                for hg in range(NHG):
                    sp.wait_ge(stack_in[hg], (NB + 1) * 2 * len(Q_PARTS) * 16)

            @block.tensor
            def _(pe):
                pe.sem_inc(max_done, R - 1)
                pe.sem_inc(exp_done, R)
                pe.sem_inc(pv_done, 1 + START)
                pe.sem_inc(on_ready, 1 + START)
                pe.sem_inc(o_taken, START)

                def first_scores(u, i, hg):
                    head, qt, c = u // (2 * KT), u // 2 % KT, u % 2
                    pe.wait_ge(max_done, i * MAXES + u)
                    corner = qt == 0 and c == 1
                    bank = (hg * MAXES + u) % R
                    m = pe.matmul(ps1[:, bank, :], qs[0:KQ, hg, head, 128 * qt:128 * qt + 128],
                                  ks[0:KQ, hg, head, CH * c:CH * c + CH], start=True, stop=not corner)
                    if corner:
                        m = pe.matmul(ps1[:, bank, CH - 19:CH], s.ident[0:19, :], s.corner_q[:, GH * hg + head, :],
                                      start=False, stop=True)
                    m.then_inc(s1_ready, 1)

                def second_scores(sl, hg, qc, kt, head):
                    pe.wait_ge(exp_done, sl * GH + (head + 1))
                    bank = (((2 * hg + qc) * KT + kt) * GH + head) % R
                    corner = qc == 0 and kt == KT - 1
                    m = pe.matmul(ps2[:, bank, :], ks[0:KM, hg, head, 128 * kt:128 * kt + 128],
                                  qs[0:KM, hg, head, CH * qc:CH * qc + CH], start=True, stop=not corner)
                    if corner:
                        m = pe.matmul(ps2[:, bank, 0:19], s.shift[:], s.corner_k[:, GH * hg + head, :],
                                      start=False, stop=True)
                    m.then_inc(s2_ready, 1)

                def values(part, sl, hg, kt, half):
                    if part == 0:
                        pe.wait_ge(exp_done, sl * GH + (GH + R))
                        if kt == 0:
                            pe.wait_ge(o_taken, half + START)
                    cols = slice(CH // 2 * part, CH // 2 * (part + 1))
                    for head in range(GH):
                        m = pe.matmul(psO[32 * head:32 * head + 32, cols], v_now[:, kt, GH * hg + head, :],
                                      P[:, kt % 2, head, cols], start=(kt == 0 and part == 0),
                                      stop=(kt == KT - 1 and part == 1))
                    if part == 1:
                        m.then_inc(pv_done, 1)

                def turn_maxima(use):
                    pe.wait_ge(misc_taken, use)
                    pe.transpose(psM[0:QPART * 32, 0:64].bitcast(BF16), nmp[:].rearrange("p a r -> p (a r)"),
                                 s.ident_bf[:]).then_inc(misc_ready, 1)

                def spread_sums(use, half, hb):
                    pe.wait_ge(o_taken, half + 1 + START)
                    pe.wait_ge(misc_taken, use)
                    pe.matmul(psM[:, :], s.sum_sel[:], o_raw[:, hb, :], start=True, stop=True).then_inc(misc_ready, 1)

                def project(b, x):
                    c, f = x // 2, x % 2
                    pe.wait_ge(misc_taken, b * MISC + (1 + PROJ[x]))
                    pe.wait_ge(on_ready, b * (2 * NHG) + (2 * NHG + c) + START)
                    for g in range(NHG):
                        m = pe.matmul(psM[0:HC, :], s.w_proj[:, g, HC * f:HC * f + HC], o_n[:, g, CH * c:CH * c + CH],
                                      start=(g == 0), stop=(g == NHG - 1))
                    m.then_inc(misc_ready, 1)

                pe.wait_ge(stack_in[0], 2 * len(Q_PARTS) * 16)
                for u in range(MAXES):
                    first_scores(u, 0, 0)
                pe.wait_ge(nmp_ready, 1)
                turn_maxima(0)
                pe.wait_ge(stack_in[1], 2 * len(Q_PARTS) * 16)
                pe.wait_ge(rows_set, 1)
                def half_of(b, hg, qc, before):
                    half = b * (2 * NHG) + (2 * hg + qc)
                    nb, nhg, ni = step_ahead(b, hg, 1 + qc)
                    if qc == 0:
                        pe.wait_ge(nm_in, (b * NHG + (hg + 1)) * 16)
                        pe.wait_ge(v_set, b * NHG + (hg + 1))
                    else:
                        pe.wait_ge(stack_in[nhg], (nb + 1) * (2 * len(Q_PARTS) * 16))
                    for kt in range(KT):
                        sl = half * KT + kt
                        if kt:
                            late = (sl - 1, hg, kt - 1, half)
                        else:
                            late = (sl - 1, before[1], KT - 1, half - 1) if before else None
                        for x in range(GH):
                            for u in ahead(qc, kt, before)[x]:
                                first_scores(u, ni, nhg)
                            second_scores(sl, hg, qc, kt, x)
                            if late and x in (1, 2):
                                values(x - 1, *late)
                        if kt == 2 and before:
                            if hg or qc:
                                spread_sums(in_psM(b, hg, qc), half - 1, 1 - qc)
                            else:
                                spread_sums(before[0] * MISC + (1 + LAST_SUMS), half - 1, 1)
                        if kt == 1 and qc == 1:
                            pe.wait_ge(nmp_ready, b * NHG + (hg + 2))
                            turn_maxima(b * MISC + (1 + 3 * hg))
                        if kt >= 6 and hg == NHG - 1 and qc == 1:
                            project(b, kt - 6)
                        if kt >= 6 and hg == 0 and qc == 0 and before:
                            project(before[0], kt - 4)

                def halves(b, later):
                    for d, hg, qc in later:
                        half_of(b + d if d else b, hg, qc, (b, NHG - 1) if d else (b, hg - (1 - qc)))

                half_of(0, 0, 0, None)
                with pe.Fori(0, NB - 1, 1) as b:
                    halves(b, LATER)
                halves(NB - 1, LATER[:-1])
                half = NB * 2 * NHG - 1
                for part in range(2):
                    values(part, half * KT + KT - 1, NHG - 1, KT - 1, half)
                spread_sums((NB - 1) * MISC + (1 + LAST_SUMS), half, 1)
                project(NB - 1, 2)
                project(NB - 1, 3)

            @block.scalar
            def _(act):
                def read_sums(half, qc):
                    act.wait_ge(pv_done, half * KT + (KT + 1) + START)
                    act.wait_ge(on_ready, half + START)
                    nc.scalar.copy(o_raw[:, qc, :], psO[:, :]).then_inc(o_taken, 1)

                def log_sums(use, half):
                    act.wait_ge(misc_ready, use + 1)
                    act.wait_ge(on_ready, half + 1 + START)
                    nc.scalar.activation(rec[:], psM[:, :], ACT.Ln).then_inc(misc_taken, 1)

                def invert_sums(use):
                    act.wait_ge(misc_taken, use + 1)
                    nc.scalar.activation(rec[:], rec[:], ACT.Exp, scale=-1.0).then_inc(rec_ready, 1)

                nc.scalar.preload_act_table_set("natural_log_exp_and_others")
                def half_of(b, hg, qc, before):
                    half = b * (2 * NHG) + (2 * hg + qc)
                    use = None
                    if before:
                        use = in_psM(b, hg, qc) if hg or qc else before[0] * MISC + (1 + LAST_SUMS)
                    for kt in range(KT):
                        sl = half * KT + kt
                        act.wait_ge(pv_done, sl + START)
                        for head in range(GH):
                            act.wait_ge(s2_ready, sl * GH + (head + 1))
                            bank = (((2 * hg + qc) * KT + kt) * GH + head) % R
                            nc.scalar.activation(P[:, kt % 2, head, :], ps2[:, bank, :], ACT.Exp).then_inc(exp_done, 1)
                            if before and (kt, head) == READ_AT:
                                read_sums(half - 1, 1 - qc)
                            if before and (kt, head) == LOG_AT:
                                log_sums(use, half - 1)
                            if before and (kt, head) == INVERT_AT:
                                invert_sums(use)

                def halves(b, later):
                    for d, hg, qc in later:
                        half_of(b + d if d else b, hg, qc, (b,))

                half_of(0, 0, 0, None)
                with act.Fori(0, NB - 1, 1) as b:
                    halves(b, LATER)
                halves(NB - 1, LATER[:-1])
                half = NB * 2 * NHG - 1
                read_sums(half, 1)
                log_sums((NB - 1) * MISC + (1 + LAST_SUMS), half)
                invert_sums((NB - 1) * MISC + (1 + LAST_SUMS))

            @block.vector
            def _(v):
                def tile_max(i, u, slot):
                    v.wait_ge(s1_ready, i * MAXES + (u + 1))
                    v.reduce_max(mx[:, slot, u:u + 1], ps1[:, (slot * MAXES + u) % R, :], AX.X).then_inc(max_done, 1)

                def join_chunks(i, slot):
                    v.wait_ge(max_done, i * MAXES + (MAXES + R - 1))
                    v.reduce_max(top[:], mx[:, slot, :].rearrange("p (t c) -> p t c", c=2), AX.X).then_inc(top_ready, 1)

                def take_maxima(use, i):
                    v.wait_ge(misc_ready, use + 1)
                    v.wait_ge(nm_store, i * 16)
                    v.tensor_copy(nmt[:], psM[0:QPART * 32, 0:64].bitcast(BF16)).then_inc(misc_taken, 1)

                def normalise(half, hg, qc):
                    v.wait_ge(rec_ready, half + 1)
                    v.tensor_tensor(o_n[:, hg, CH * qc:CH * qc + CH], o_raw[:, qc, :], rec[:], ALU.mult
                                    ).then_inc(on_ready, 1)

                def add_projection(b, x):
                    c, f = x // 2, x % 2
                    v.wait_ge(misc_ready, b * MISC + (2 + PROJ[x]))
                    y = s.Y[:, b, f, CH * c:CH * c + CH]
                    v.tensor_tensor(y, y, psM[0:HC, :], ALU.add).then_inc(misc_taken, 1)

                for u in range(MAXES):
                    tile_max(0, u, 0)
                join_chunks(0, 0)
                take_maxima(0, 0)
                def half_of(b, hg, qc, before):
                    half = b * (2 * NHG) + (2 * hg + qc)
                    nb, nhg, ni = step_ahead(b, hg, 1 + qc)
                    for kt in range(KT):
                        for us in ahead(qc, kt, before):
                            for u in us:
                                tile_max(ni, u, nhg)
                        if kt == 1 and qc == 1:
                            take_maxima(b * MISC + (1 + 3 * hg), b * NHG + (hg + 1))
                        if kt == NORM_AT and before:
                            normalise(half - 1, before[1], 1 - qc)
                        if kt >= 6 and hg == NHG - 1 and qc == 1:
                            add_projection(b, kt - 6)
                        if kt >= 6 and hg == 0 and qc == 0 and before:
                            add_projection(before[0], kt - 4)
                    if qc == 0:
                        join_chunks(ni, nhg)

                def halves(b, later):
                    for d, hg, qc in later:
                        half_of(b + d if d else b, hg, qc, (b, NHG - 1) if d else (b, hg - (1 - qc)))

                half_of(0, 0, 0, None)
                with v.Fori(0, NB - 1, 1) as b:
                    halves(b, LATER)
                halves(NB - 1, LATER[:-1])
                normalise(NB * 2 * NHG - 1, NHG - 1, 1)
                add_projection(NB - 1, 2)
                add_projection(NB - 1, 3)


def expert_norm(nc, w, s):
    def after(ctx, sb, sem, normed):
        cleared = sem("cleared")
        weights_in = [sem(f"weights_in{i}") for i in range(2)]

        def clear(pool):
            pool.memset(s.gate_w[:], 0.0).then_inc(cleared, 1)
            pool.memset(s.gate_b[:], 0.0).then_inc(cleared, 1)

        def sync(sp):
            for e in range(EXPERTS):
                sp.dma_start(s.w1[:, e, :, :], w.w1[e].rearrange("(f p) h -> p f h", p=HC)).then_inc(weights_in[0], 16)
                sp.dma_start(s.w2[:, e, :, :], w.w2[e].rearrange("(t p) d -> p t d", p=128)).then_inc(weights_in[0], 16)
            sp.dma_start(s.b1_rows[:], w.b1.rearrange("e (t p) -> (e t) p", p=128)).then_inc(weights_in[1], 16)
            sp.dma_start(s.b2[:], w.b2.rearrange("(o e) d -> o e d", o=1).broadcast_to([128, EXPERTS, D])
                         ).then_inc(weights_in[1], 16)
            sp.wait_ge(cleared, 2)
            sp.dma_start(s.gate_w[:, :, 0:EXPERTS], w.gatew.rearrange("(f p) e -> p f e", p=HC)).then_inc(weights_in[1], 16)
            for j in range(4):
                sp.dma_start(s.gate_b[32 * j:32 * j + EXPERTS, :], w.gateb.rearrange("(e o) -> e o", o=1)
                             ).then_inc(weights_in[1], 16)
            sp.wait_ge(weights_in[0], 2 * EXPERTS * 16)
            sp.wait_ge(weights_in[1], 7 * 16)

        return {"clear": clear, "sync": sync}

    layer_norm(nc, s, s.Y, s.Z, "lf_", after)


def experts(nc, w, s):
    with ExitStack() as ctx:
        def sb(name, shape, dt=F32):
            return ctx.enter_context(nc.sbuf_tensor(name, shape, dt))

        def sem(name):
            return ctx.enter_context(nc.semaphore(name))

        TT = NB * L // 128
        CT = CH // 128
        w1, w2, b1_rows, b2, gate_w, gate_b = s.w1, s.w2, s.b1_rows, s.b2, s.gate_w, s.gate_b
        b1 = sb("b1", [128, EXPERTS * HT])
        logit_t = sb("logit_t", [128, 2, CH])
        pr = sb("pr", [128, TT, EXPERTS])
        tot = sb("tot", [128, TT])
        beats = sb("beats", [128, TT])
        rank = sb("rank", [128, TT, EXPERTS])
        gate = sb("gate", [128, NB, 2, CT, EXPERTS])
        hid = sb("hid", [128, 2, HT, CH])
        acc = sb("acc", [128, 2, CT, D])
        res = sb("res", [HC, 2, 2, CH])
        psH = ctx.enter_context(nc.psum_tensor("psH", [128, 3, CH], F32))
        psE = ctx.enter_context(nc.psum_tensor("psE", [128, 2, CH], F32))
        psT = ctx.enter_context(nc.psum_tensor("psT", [128, 2, CH], F32))
        b1_turned, logits, logits_taken, logits_turned, own, gates_ready = (
            sem("b1_turned"), sem("logits"), sem("logits_taken"), sem("logits_turned"), sem("own_ex"),
            sem("gates_ready"))
        exp_ready = sem("exp_ready")
        h_ready = sem("h_ready")
        h_done = sem("h_done")
        e_ready = sem("e_ready")
        e_taken = sem("e_taken")
        acc_set = sem("acc_set")
        turned = sem("turned")
        summed = sem("res_ready")
        stored = [sem(f"res_out{c}") for c in range(2)]

        with nc.Block() as block:
            @block.sync
            def _(sp):
                with sp.Fori(0, NB, 1) as b:
                    for c in range(2):
                        sp.wait_ge(summed, b * 2 + (c + 2))
                        sp.dma_start(w.out[b].rearrange("(f p) h w -> p f (h w)", p=HC)[:, :, CH * c:CH * c + CH],
                                     res[:, c, :, :]).then_inc(stored[c], 16)
                for c in range(2):
                    sp.wait_ge(stored[c], 16 * NB + START)

            @block.tensor
            def _(pe):
                pe.sem_inc(h_done, 2 + START)
                pe.sem_inc(e_ready, CT + START)
                for c in range(2):
                    pe.sem_inc(stored[c], START)
                pe.sem_inc(e_taken, 1 + START)
                pe.sem_inc(summed, 1)
                pe.transpose(psE[:, 0, 0:EXPERTS * HT], b1_rows[:], s.ident[0:EXPERTS * HT, 0:EXPERTS * HT]).then_inc(b1_turned, 1)
                for g in range(2):
                    for f in range(2):
                        for j in range(4):
                            i = 4 * g + j
                            m = pe.matmul(psT[32 * j:32 * j + 32, g, :], gate_w[:, f, :],
                                          s.Z[:, i // 2, f, CH * (i % 2):CH * (i % 2) + CH], start=(f == 0), stop=(f == 1))
                m.then_inc(logits, 1)
                pe.wait_ge(logits_taken, 2)
                for g in range(2):
                    for t in range(CT):
                        m = pe.transpose(psH[:, g, 128 * t:128 * t + 128], logit_t[:, g, 128 * t:128 * t + 128], s.ident[:])
                m.then_inc(logits_turned, 1)
                pe.wait_ge(gates_ready, 1)

                def hidden(b, c, e, n):
                    for t in range(HT):
                        pe.wait_ge(h_done, n * HT + t + START)
                        for f in range(2):
                            m = pe.matmul(psH[:, t % 3, :], w1[:, e, f, 128 * t:128 * t + 128],
                                          s.Z[:, b, f, CH * c:CH * c + CH], start=(f == 0), stop=(f == 1))
                        m.then_inc(h_ready, 1)

                def outputs(e, n):
                    pe.wait_ge(h_done, n * HT + (HT + 2) + START)
                    for tt in range(CT):
                        pe.wait_ge(e_taken, n * CT + tt + START)
                        for t in range(HT):
                            m = pe.matmul(psE[:, tt % 2, 0:D], hid[:, e % 2, t, 128 * tt:128 * tt + 128], w2[:, e, t, :],
                                          start=(t == 0), stop=(t == HT - 1))
                        m.then_inc(e_ready, 1)

                def turn_back(b, c, n):
                    pe.wait_ge(e_taken, n * CT + (CT + 1) + START)
                    pe.wait_ge(summed, b * 2 + (c + 1))
                    for f in range(2):
                        for tt in range(CT):
                            m = pe.transpose(psT[0:HC, f, 128 * tt:128 * tt + 128], acc[:, c, tt, HC * f:HC * f + HC], s.ident[:])
                    m.then_inc(turned, 1)

                with pe.Fori(0, NB, 1) as b:
                    hidden(b, 0, 0, b * (2 * EXPERTS))
                    for c in range(2):
                        for e in range(EXPERTS):
                            n = b * (2 * EXPERTS) + (c * EXPERTS + e)
                            if e + 1 < EXPERTS:
                                hidden(b, c, e + 1, n + 1)
                            elif c == 0:
                                hidden(b, 1, 0, n + 1)
                            outputs(e, n)
                        turn_back(b, c, n)

            @block.scalar
            def _(act):
                act.wait_ge(own, 2)
                nc.scalar.activation(pr[:], pr[:], ACT.Exp).then_inc(exp_ready, 1)
                with act.Fori(0, NB, 1) as b:
                    for c in range(2):
                        for e in range(EXPERTS):
                            n = b * (2 * EXPERTS) + (c * EXPERTS + e)
                            act.wait_ge(b1_turned, 2)
                            for t in range(HT):
                                act.wait_ge(h_ready, n * HT + (t + 1))
                                if t == 0:
                                    act.wait_ge(e_ready, n * CT + START)
                                nc.scalar.activation(hid[:, e % 2, t, :], psH[:, t % 3, :], ACT.Gelu,
                                                     bias=b1[:, HT * e + t:HT * e + t + 1]).then_inc(h_done, 1)

            @block.vector
            def _(v):
                chain = Own(v, own)

                def step(ins):
                    chain(ins)
                    chain.wait()

                v.wait_ge(b1_turned, 1)
                v.tensor_copy(b1[:], psE[:, 0, 0:EXPERTS * HT]).then_inc(b1_turned, 1)
                v.wait_ge(logits, 1)
                for g in range(2):
                    v.tensor_scalar(logit_t[:, g, :], psT[:, g, :], gate_b[:, 0:1], None, ALU.add).then_inc(logits_taken, 1)
                v.wait_ge(logits_turned, 1)
                for g in range(2):
                    for t in range(CT):
                        m = v.tensor_copy(pr[:, 16 * g + t:16 * g + 16:CT, :],
                                          psH[:, g, 128 * t:128 * t + 128].rearrange("p (j e) -> p j e", e=32)[:, :, 0:EXPERTS])
                m.then_inc(gates_ready, 1)
                v.wait_ge(gates_ready, 1)
                step(v.reduce_max(tot[:], pr[:], AX.X))
                step(v.tensor_tensor(pr[:], pr[:], tot[:].unsqueeze(2).broadcast_to([128, TT, EXPERTS]), ALU.subtract))
                v.wait_ge(exp_ready, 1)
                step(v.reduce_sum(tot[:], pr[:], AX.X))
                step(v.reciprocal(tot[:], tot[:]))
                step(v.tensor_tensor(pr[:], pr[:], tot[:].unsqueeze(2).broadcast_to([128, TT, EXPERTS]), ALU.mult))
                step(v.memset(rank[:], 0.0))
                for lo in range(EXPERTS):
                    for hi in range(lo + 1, EXPERTS):
                        step(v.tensor_tensor(beats[:], pr[:, :, lo], pr[:, :, hi], ALU.is_ge))
                        step(v.tensor_tensor(rank[:, :, hi], rank[:, :, hi], beats[:], ALU.add))
                        step(v.tensor_scalar(beats[:], beats[:], -1.0, 1.0, ALU.mult, ALU.add))
                        step(v.tensor_tensor(rank[:, :, lo], rank[:, :, lo], beats[:], ALU.add))
                step(v.tensor_scalar(rank[:], rank[:], 1.5, None, ALU.is_le))
                step(v.tensor_tensor(pr[:], pr[:], rank[:], ALU.mult))
                step(v.reduce_sum(tot[:], pr[:], AX.X))
                step(v.tensor_scalar(tot[:], tot[:], 1e-9, None, ALU.add))
                step(v.reciprocal(tot[:], tot[:]))
                step(v.tensor_tensor(gate[:].rearrange("p b c t e -> p (b c t) e"), pr[:],
                                     tot[:].unsqueeze(2).broadcast_to([128, TT, EXPERTS]), ALU.mult))
                with v.Fori(0, NB, 1) as b:
                    for c in range(2):
                        for e in range(EXPERTS):
                            n = b * (2 * EXPERTS) + (c * EXPERTS + e)
                            for tt in range(CT):
                                g = gate[:, b, c, tt, e:e + 1]
                                a = acc[:, c, tt, :]
                                if e == 0:
                                    v.tensor_scalar(a, b2[:, 0, :], g, None, ALU.mult).then_inc(acc_set, 1)
                                    for x in range(1, EXPERTS):
                                        v.wait_ge(acc_set, (b * 2 + c) * (CT * EXPERTS) + (tt * EXPERTS + x))
                                        v.scalar_tensor_tensor(out=a, in0=b2[:, x, :], scalar=gate[:, b, c, tt, x:x + 1],
                                                               in1=a, op0=ALU.mult, op1=ALU.add).then_inc(acc_set, 1)
                                    v.wait_ge(acc_set, (b * 2 + c) * (CT * EXPERTS) + (tt * EXPERTS + EXPERTS))
                                else:
                                    v.wait_ge(e_taken, n * CT + (tt - CT + 2) + START)
                                v.wait_ge(e_ready, n * CT + (CT + tt + 1) + START)
                                v.scalar_tensor_tensor(out=a, in0=psE[:, tt % 2, 0:D], scalar=g, in1=a,
                                                       op0=ALU.mult, op1=ALU.add).then_inc(e_taken, 1)
                        v.wait_ge(turned, b * 2 + (c + 1))
                        v.wait_ge(stored[c], b * 16 + START)
                        v.tensor_tensor(res[:, c, :, :], psT[0:HC, :, :], s.Y[:, b, :, CH * c:CH * c + CH], ALU.add
                                        ).then_inc(summed, 1)


class Views:
    pass


def program(nc, ins, out):
    w = Views()
    (w.x, w.wx, w.wdt, w.dtb, w.alog, w.ds, w.lnw, w.lnb, w.qkvw, w.qkvb, w.projw, w.projb, w.table,
     w.gatew, w.gateb, w.w1, w.b1, w.w2, w.b2) = ins
    w.out = out
    with ExitStack() as ctx:
        def sb(name, shape, dt=F32):
            return ctx.enter_context(nc.sbuf_tensor(name, shape, dt))

        s = Views()
        s.Y = sb("Y", [HC, NB, 2, L])
        s.cols = sb("cols", [HC, NCOL])
        s.ident = sb("ident", [128, 128])
        s.ident_bf = sb("ident_bf", [128, 128], BF16)
        s.average = sb("average", [HC, HC])
        s.sum_sel = sb("sum_sel", [128, 128])
        s.one = sb("one", [128, 1])
        s.eps5 = sb("eps5", [128, 1])
        s.qk_dram = nc.dram_tensor("qk_parts", (NB, 2, QPART, D, L), BF16, kind="Internal").ap()
        s.nm_dram = nc.dram_tensor("max_parts", (QPART * 32, 128), BF16, kind="Internal").ap()
        s.ext = nc.dram_tensor("table_twice", (37, HEADS), F32, kind="Internal").ap()
        with ExitStack() as c2:
            def sb2(name, shape, dt=F32):
                return c2.enter_context(nc.sbuf_tensor(name, shape, dt))
            s.X = sb2("X", [HC, NB + 1, 2, L])
            s.d_sum = sb2("d_sum", [HC, 2])
            s.w_b = sb2("w_b", [HC, K, 2, 128])
            s.w_c = sb2("w_c", [HC, K, 2, 128])
            s.w_dt = sb2("w_dt", [HC, K, 2, D])
            s.a_neg = sb2("a_neg", [128, HC])
            s.spread_sel = sb2("spread_sel", [HC, SUB, 128], BF16)
            s.state_sel = sb2("state_sel", [128, SUB, BLK])
            prepare(nc, w, s)
            scan(nc, w, s)
        with ExitStack() as c2:
            def sb2(name, shape, dt=F32):
                return c2.enter_context(nc.sbuf_tensor(name, shape, dt))
            s.w_proj = sb2("w_proj", [128, 3, D])
            s.corner_q = sb2("corner_q", [19, HEADS, 19])
            s.corner_k = sb2("corner_k", [19, HEADS, 19])
            s.shift = sb2("shift", [19, 128])
            s.V = sb2("V", [128, NB, 8, HEADS, 32])
            with nc.sbuf_tensor("Z", [HC, NB, 2, L], F32) as z, nc.sbuf_tensor("raw", [HC, NB, 2, L], F32) as raw:
                s.Z, s.raw = z, raw
                conv_out(nc, w, s)
            with nc.sbuf_tensor("Zq", [HC, NB, 2, L], F32) as z:
                s.Z = z
                qkv(nc, w, s)
            attention(nc, w, s)
        with ExitStack() as c2:
            def sb2(name, shape, dt=F32):
                return c2.enter_context(nc.sbuf_tensor(name, shape, dt))
            s.Z = sb2("Zf", [HC, NB, 2, L])
            s.w1 = sb2("w1", [HC, EXPERTS, 2, HID])
            s.w2 = sb2("w2", [128, EXPERTS, HT, D])
            s.b1_rows = sb2("b1_rows", [EXPERTS * HT, 128])
            s.b2 = sb2("b2", [128, EXPERTS, D])
            s.gate_w = sb2("gate_w", [HC, 2, 32])
            s.gate_b = sb2("gate_b", [128, 1])
            expert_norm(nc, w, s)
            experts(nc, w, s)


_INS = ["x", "L0_conv_x_proj_weight", "L0_conv_dt_projs_weight", "L0_conv_dt_projs_bias", "L0_conv_A_logs",
        "L0_conv_Ds", "L0_conv_ln_weight", "L0_conv_ln_bias", "L1_attn_qkv_w", "L1_attn_qkv_b", "L1_attn_proj_w",
        "L1_attn_proj_b", "L1_attn_bias_table", "L1_ffn_gate_w", "L1_ffn_gate_b", "L1_ffn_w1", "L1_ffn_b1",
        "L1_ffn_w2", "L1_ffn_b2"]
_OUT = ((NB, D, HH, WW), "float32")


def kernel(**inputs):
    import numpy as _np
    import concourse.bacc as _bacc
    from concourse import mybir as _mybir
    from concourse.bass_utils import run_bass_kernel_spmd as _run

    nc = _bacc.Bacc("TRN2", target_bir_lowering=False, num_devices=1)
    arrays, args = {}, []
    for name in _INS:
        a = _np.ascontiguousarray(inputs[name])
        arrays[f"in_{name}_dram"] = a
        args.append(nc.dram_tensor(f"in_{name}_dram", a.shape, _mybir.dt.from_np(a.dtype), kind="ExternalInput").ap())
    shape, dtype = _OUT
    out = nc.dram_tensor("out_dram", shape, _mybir.dt.from_np(_np.dtype(dtype)), kind="ExternalOutput").ap()
    program(nc, args, out)
    r = _run(nc, [arrays], core_ids=[0])
    return r.results[0]["out_dram"]
```
